# Optimizing a Trainium2 kernel written in Bass

```python
import numpy as np
import jax
import jax.numpy as jnp

def _softmax(x, axis=-1):
    return jax.nn.softmax(x, axis=axis)

def _gelu(x):
    return jax.nn.gelu(x, approximate=True)

def _silu(x):
    return jax.nn.silu(x)

def _sigmoid(x):
    return jax.nn.sigmoid(x)

def _layernorm(x, axis=-1, eps=1e-05):
    m = jnp.mean(x, axis=axis, keepdims=True)
    v = jnp.var(x, axis=axis, keepdims=True)
    return (x - m) / jnp.sqrt(v + eps)

def _scatter_add(tgt, idx, src, axis=0):
    return tgt.at[idx].add(src)

def _segment_sum(src, seg, n):
    return jax.ops.segment_sum(src, seg, n)
kernel_name = 'mk_seq_postln_d1_jaxref_r4_20d2d7'

def setup_inputs(seed: int=0):
    np.random.seed(seed)
    _w = jnp.asarray

    def _L0_attn_setup():
        import jax, jax.numpy as jnp
        import numpy as np
        B, T, D_MODEL = (4, 1024, 512)
        D_LATENT = 128
        D_COMP = 64
        THETA = 10000.0
        LN_EPS = 1e-05

        def _rope_tables(seq_len: int, dim: int):
            inv_freq = 1.0 / THETA ** (jnp.arange(0, dim, 2, dtype=jnp.float32) / dim)
            freqs = jnp.arange(seq_len, dtype=jnp.float32)[:, None] * inv_freq[None, :]
            cos = jnp.concatenate([jnp.cos(freqs), jnp.cos(freqs)], axis=-1)
            sin = jnp.concatenate([jnp.sin(freqs), jnp.sin(freqs)], axis=-1)
            return (cos, sin)

        def _rotate_half(x):
            x1, x2 = jnp.split(x, 2, axis=-1)
            return jnp.concatenate([-x2, x1], axis=-1)
        key = jax.random.key(seed)
        ks = jax.random.split(key, 8)
        s = 0.02
        return {'x': jax.random.normal(ks[0], (B, T, D_MODEL), dtype=jnp.float32), 'W_to_kv': jax.random.normal(ks[1], (D_LATENT, D_MODEL), dtype=jnp.float32) * s, 'W_compress': jax.random.normal(ks[2], (D_COMP, D_LATENT), dtype=jnp.float32) * s, 'ln_gamma': jnp.ones((D_COMP,), dtype=jnp.float32), 'ln_beta': jnp.zeros((D_COMP,), dtype=jnp.float32), 'W_q_comp': jax.random.normal(ks[3], (D_COMP, D_COMP), dtype=jnp.float32) * s, 'W_kv_comp': jax.random.normal(ks[4], (2 * D_COMP, D_COMP), dtype=jnp.float32) * s, 'W_comp2lat': jax.random.normal(ks[5], (D_LATENT, D_COMP), dtype=jnp.float32) * s, 'W_out_res': jnp.zeros((D_MODEL, D_LATENT), dtype=jnp.float32), 'b_out_res': jnp.zeros((D_MODEL,), dtype=jnp.float32)}
    _L0_attn_in = _L0_attn_setup()

    def _L0_ffn_setup():
        import jax, jax.numpy as jnp
        import numpy as np
        B, S, D = (2, 512, 512)
        F = 256
        E = 64
        K = 8
        C = 256
        NORM_TOPK = False

        def _moe(x, gate_w, w_gate, w_up, w_down):
            b, s, d = x.shape
            T = b * s
            x2 = x.reshape(T, d)
            logits = x2 @ gate_w.T
            probs = jax.nn.softmax(logits.astype(jnp.float32), axis=-1)
            top_w, top_i = jax.lax.top_k(probs, K)
            if NORM_TOPK:
                top_w = top_w / jnp.sum(top_w, axis=-1, keepdims=True)
            top_w = top_w.astype(x.dtype)
            flat_e = top_i.reshape(-1)
            flat_w = top_w.reshape(-1)
            tok = jnp.arange(T * K) // K
            onehot = jax.nn.one_hot(flat_e, E, dtype=jnp.int32)
            pos = jnp.sum(jnp.cumsum(onehot, axis=0) * onehot, axis=-1) - 1
            valid = pos < C
            loc = flat_e * C + jnp.minimum(pos, C - 1)
            flat_w = jnp.where(valid, flat_w, 0.0)
            safe_loc = jnp.where(valid, loc, E * C)
            xg = jnp.zeros((E * C + 1, d), dtype=x.dtype).at[safe_loc].set(x2[tok])[:E * C]
            xg = xg.reshape(E, C, d)
            h = jax.nn.silu(jnp.einsum('ecd,edf->ecf', xg, w_gate)) * jnp.einsum('ecd,edf->ecf', xg, w_up)
            y = jnp.einsum('ecf,efd->ecd', h, w_down).reshape(E * C, d)
            y_tok = y[loc] * flat_w[:, None]
            out = jnp.zeros((T, d), dtype=x.dtype).at[tok].add(y_tok)
            return out.reshape(b, s, d)
        key = jax.random.key(seed)
        ks = jax.random.split(key, 5)
        scale = 0.02
        return {'hidden_states': jax.random.normal(ks[0], (B, S, D), dtype=jnp.float32), 'gate_w': jax.random.normal(ks[1], (E, D), dtype=jnp.float32) * scale, 'w_gate': jax.random.normal(ks[2], (E, D, F), dtype=jnp.float32) * scale, 'w_up': jax.random.normal(ks[3], (E, D, F), dtype=jnp.float32) * scale, 'w_down': jax.random.normal(ks[4], (E, F, D), dtype=jnp.float32) * scale}
    _L0_ffn_in = _L0_ffn_setup()
    _d = {'L0_attn_x': _L0_attn_in['x'], 'L0_attn_W_to_kv': _L0_attn_in['W_to_kv'], 'L0_attn_W_compress': _L0_attn_in['W_compress'], 'L0_attn_ln_gamma': _L0_attn_in['ln_gamma'], 'L0_attn_ln_beta': _L0_attn_in['ln_beta'], 'L0_attn_W_q_comp': _L0_attn_in['W_q_comp'], 'L0_attn_W_kv_comp': _L0_attn_in['W_kv_comp'], 'L0_attn_W_comp2lat': _L0_attn_in['W_comp2lat'], 'L0_attn_W_out_res': _L0_attn_in['W_out_res'], 'L0_attn_b_out_res': _L0_attn_in['b_out_res'], 'L0_ffn_gate_w': _L0_ffn_in['gate_w'], 'L0_ffn_w_gate': _L0_ffn_in['w_gate'], 'L0_ffn_w_up': _L0_ffn_in['w_up'], 'L0_ffn_w_down': _L0_ffn_in['w_down']}
    _x0 = _d['L0_attn_x']
    _d['L0_attn_x'] = jax.random.normal(jax.random.fold_in(jax.random.key(seed), 1), (16, 512, 512), dtype=_x0.dtype)
    del _x0
    return _d

def reference(L0_attn_x, L0_attn_W_to_kv, L0_attn_W_compress, L0_attn_ln_gamma, L0_attn_ln_beta, L0_attn_W_q_comp, L0_attn_W_kv_comp, L0_attn_W_comp2lat, L0_attn_W_out_res, L0_attn_b_out_res, L0_ffn_gate_w, L0_ffn_w_gate, L0_ffn_w_up, L0_ffn_w_down):

    def _L0_attn_ref(x, W_to_kv, W_compress, ln_gamma, ln_beta, W_q_comp, W_kv_comp, W_comp2lat, W_out_res, b_out_res):
        import jax, jax.numpy as jnp
        import numpy as np
        B, T, D_MODEL = (4, 1024, 512)
        D_LATENT = 128
        D_COMP = 64
        THETA = 10000.0
        LN_EPS = 1e-05

        def _rope_tables(seq_len: int, dim: int):
            inv_freq = 1.0 / THETA ** (jnp.arange(0, dim, 2, dtype=jnp.float32) / dim)
            freqs = jnp.arange(seq_len, dtype=jnp.float32)[:, None] * inv_freq[None, :]
            cos = jnp.concatenate([jnp.cos(freqs), jnp.cos(freqs)], axis=-1)
            sin = jnp.concatenate([jnp.sin(freqs), jnp.sin(freqs)], axis=-1)
            return (cos, sin)

        def _rotate_half(x):
            x1, x2 = jnp.split(x, 2, axis=-1)
            return jnp.concatenate([-x2, x1], axis=-1)
        Bx, Tx, _ = x.shape
        dc = W_compress.shape[0]
        kv_latent = x @ W_to_kv.T
        c = kv_latent @ W_compress.T
        mu = jnp.mean(c, axis=-1, keepdims=True)
        var = jnp.mean((c - mu) ** 2, axis=-1, keepdims=True)
        ch = (c - mu) * jax.lax.rsqrt(var + LN_EPS) * ln_gamma + ln_beta
        q = ch @ W_q_comp.T
        kv = ch @ W_kv_comp.T
        k, v = jnp.split(kv, 2, axis=-1)
        cos, sin = _rope_tables(Tx, dc)
        q = q * cos + _rotate_half(q) * sin
        k = k * cos + _rotate_half(k) * sin
        scale = 1.0 / jnp.sqrt(jnp.float32(dc))
        scores = jnp.einsum('btd,bsd->bts', q, k) * scale
        causal = jnp.tril(jnp.ones((Tx, Tx), dtype=bool))
        scores = jnp.where(causal[None], scores, jnp.float32(-1e+30))
        attn = jax.nn.softmax(scores, axis=-1)
        o = jnp.einsum('bts,bsd->btd', attn, v)
        z = o @ W_comp2lat.T
        out = z @ W_to_kv + z @ W_out_res.T + b_out_res
        return out

    def _L0_ffn_ref(hidden_states, gate_w, w_gate, w_up, w_down):
        import jax, jax.numpy as jnp
        import numpy as np
        B, S, D = (2, 512, 512)
        F = 256
        E = 64
        K = 8
        C = 256
        NORM_TOPK = False

        def _moe(x, gate_w, w_gate, w_up, w_down):
            b, s, d = x.shape
            T = b * s
            x2 = x.reshape(T, d)
            logits = x2 @ gate_w.T
            probs = jax.nn.softmax(logits.astype(jnp.float32), axis=-1)
            top_w, top_i = jax.lax.top_k(probs, K)
            if NORM_TOPK:
                top_w = top_w / jnp.sum(top_w, axis=-1, keepdims=True)
            top_w = top_w.astype(x.dtype)
            flat_e = top_i.reshape(-1)
            flat_w = top_w.reshape(-1)
            tok = jnp.arange(T * K) // K
            onehot = jax.nn.one_hot(flat_e, E, dtype=jnp.int32)
            pos = jnp.sum(jnp.cumsum(onehot, axis=0) * onehot, axis=-1) - 1
            valid = pos < C
            loc = flat_e * C + jnp.minimum(pos, C - 1)
            flat_w = jnp.where(valid, flat_w, 0.0)
            safe_loc = jnp.where(valid, loc, E * C)
            xg = jnp.zeros((E * C + 1, d), dtype=x.dtype).at[safe_loc].set(x2[tok])[:E * C]
            xg = xg.reshape(E, C, d)
            h = jax.nn.silu(jnp.einsum('ecd,edf->ecf', xg, w_gate)) * jnp.einsum('ecd,edf->ecf', xg, w_up)
            y = jnp.einsum('ecf,efd->ecd', h, w_down).reshape(E * C, d)
            y_tok = y[loc] * flat_w[:, None]
            out = jnp.zeros((T, d), dtype=x.dtype).at[tok].add(y_tok)
            return out.reshape(b, s, d)
        return _moe(hidden_states, gate_w, w_gate, w_up, w_down)
    x = L0_attn_x
    x = _layernorm(x + _L0_attn_ref(x, L0_attn_W_to_kv, L0_attn_W_compress, L0_attn_ln_gamma, L0_attn_ln_beta, L0_attn_W_q_comp, L0_attn_W_kv_comp, L0_attn_W_comp2lat, L0_attn_W_out_res, L0_attn_b_out_res), axis=-1)
    x = _layernorm(x + _L0_ffn_ref(x, L0_ffn_gate_w, L0_ffn_w_gate, L0_ffn_w_up, L0_ffn_w_down), axis=-1)
    return x

_drawn_inputs = setup_inputs


def setup_inputs(seed=0):
    import zlib

    import numpy as np

    out = dict(_drawn_inputs(seed))
    spreads = {'L0_attn_ln_gamma': (1.0, 0.6),
     'L0_attn_ln_beta': (0.0, 0.8),
     'L0_attn_W_out_res': (0.0, 0.8),
     'L0_attn_b_out_res': (0.0, 0.1)}
    factors = {'L0_attn_W_to_kv': 8.0,
     'L0_attn_W_compress': 8.0,
     'L0_attn_W_q_comp': 8.0,
     'L0_attn_W_kv_comp': 8.0,
     'L0_attn_W_comp2lat': 8.0,
     'L0_ffn_gate_w': 8.0,
     'L0_ffn_w_gate': 8.0,
     'L0_ffn_w_up': 8.0,
     'L0_ffn_w_down': 8.0}
    for name, (base, spread) in spreads.items():
        noise = np.random.default_rng([zlib.crc32(name.encode()), seed]).standard_normal(out[name].shape)
        drawn = base * np.exp(spread * noise) if base else spread * noise
        out[name] = jnp.asarray(drawn.astype(out[name].dtype))
    for name, factor in factors.items():
        out[name] = (out[name] * factor).astype(out[name].dtype)
    return out
```

```python
from contextlib import ExitStack

import concourse.bass as bass
from concourse import mybir

F32 = mybir.dt.float32
BF16 = mybir.dt.bfloat16
F16 = mybir.dt.float16
I32 = mybir.dt.int32
U32 = mybir.dt.uint32
ALU = mybir.AluOpType
ACT = mybir.ActivationFunctionType
AX = mybir.AxisListType

P = 128
SEQS, SEQ, D = 16, 512, 512
TOKENS = SEQS * SEQ
LAT, DC = 128, 64
E, TOPK, CAP, FF = 64, 8, 256, 256
KD = D // P
KF = FF // P
JT = SEQ // P
PAIRS = SEQS // 2
TILES = 2 * JT
HALVES = CAP // P
BLOCKS = E * HALVES
ROW = D + E
DUMMY = CAP
EPS = 1e-5
LOG_TINY = -104.0
TAKEN = -1e30

LAG_PROBS = 1
LAG_NORM = 2
LAG_OT = 3
LAG_OUT = 4
LAG_X1 = 5
LAG_X1T = 6
LAG_LOGITS = 7


def attention_router_moe(nc, xT, x, w_kv, w_compT, gamma, beta, w_proj, w_c2l, w_resT, bias, gateT,
                         w_experts, rope, const, out):
    table = nc.dram_tensor("token_table", [TOKENS + DUMMY, ROW], F32, kind="Internal").ap()
    total = nc.dram_tensor("running_sum", [TOKENS + DUMMY, D], F32, kind="Internal").ap()
    ctx = ExitStack()
    sems = {}
    places = []

    def sb(name, shape, dt=F32):
        return ctx.enter_context(nc.sbuf_tensor(name, shape, dt))

    def S(name):
        return sems[name]

    def wait(eng, name, per, q, k):
        value = q * per + k
        if isinstance(value, int) and value <= 0:
            return
        eng.wait_ge(S(name), value)

    def wait_apart(eng, *waits):
        for name, per, q, k in waits:
            wait(eng, name, per, q, k)
        if not all(isinstance(q, int) for _, _, q, _ in waits):
            n = len(places)
            places.append(waits[0][0])
            if eng.engine == nc.vector.engine:
                nc.vector.memset(scrap_v[:, n:n + 1], 0.0)
            else:
                nc.gpsimd.tensor_tensor(scrap_p[:, n:n + 1], eps_pow[:, 0:1], eps_pow[:, 0:1], ALU.add
                                        ).then_inc(S("scrap_written"), 1)

    def tile_at(p, m, lag):
        d = m - lag
        return p + d // TILES, d % TILES

    def live(q):
        return not isinstance(q, int) or 0 <= q < PAIRS

    with ctx:
        rope_sb = sb("rope_sb", [P, 4, SEQ])
        ident = sb("ident", [P, P])
        ident_h = sb("ident_h", [P, P], BF16)
        causal_h = sb("causal_h", [P, P], BF16)
        before_h = sb("before_h", [P, P], BF16)
        ones_h = sb("ones_h", [P, P], BF16)
        ramp_h = sb("ramp_h", [P, P], F16)
        const_f = sb("const_f", [P, 5, P])
        local_id = sb("local_id", [P, TILES])
        slot_base = sb("slot_base", [P, TILES, E])
        empty_row = sb("empty_row", [P, P])
        eps_pow = sb("eps_pow", [P, TILES])
        eps_add = sb("eps_add", [P, TILES])
        scrap_v = sb("scrap_v", [P, 64])
        scrap_p = sb("scrap_p", [P, 64])
        bias_sb = sb("bias_sb", [P, D])
        gamma_sb = sb("gamma_sb", [P, 1])
        beta_sb = sb("beta_sb", [P, 1])
        gate_sb = sb("gate_sb", [P, KD, E])
        proj = sb("proj", [P, 5, P])
        w_kv_sb = sb("w_kv_sb", [LAT, D])
        w_comp_sb = sb("w_comp_sb", [LAT, DC])
        w_c2l_sb = sb("w_c2l_sb", [LAT, 2 * DC])
        w_sum = sb("w_sum", [LAT, D])
        w_in = sb("w_in", [P, KD, DC])
        w_out = sb("w_out", [P, D])
        xT_sb = sb("xT_sb", [P, KD, TILES * P])
        x_sb = sb("x_sb", [P, TILES, D])
        x1_sb = sb("x1_sb", [P, TILES, D])
        c_sum = sb("c_sum", [P, TILES])
        c_negmean = sb("c_negmean", [P, TILES])
        c_cen = sb("c_cen", [P, TILES, DC])
        c_sq = sb("c_sq", [P, TILES, DC])
        c_ssq = sb("c_ssq", [P, TILES])
        c_var = sb("c_var", [P, TILES])
        c_rstd = sb("c_rstd", [P, TILES])
        c_norm = sb("c_norm", [P, TILES, DC])
        chT = sb("chT", [P, SEQ])
        turned = sb("turned", [P, 4, SEQ])
        qT = sb("qT", [P, SEQ])
        kT = sb("kT", [P, SEQ])
        v_sb = sb("v_sb", [P, JT, P])
        neg_max = sb("neg_max", [P, TILES])
        exp_sum = sb("exp_sum", [P, TILES])
        exp_inv = sb("exp_inv", [P, TILES])
        probs = sb("probs", [P, 2, SEQ])
        probsT = sb("probsT", [P, 2, SEQ])
        o_sb = sb("o_sb", [P, 2, P])
        oT = sb("oT", [P, 2, P])
        y_sb = sb("y_sb", [P, 2, D])
        y_stats = sb("y_stats", [P, 2, 6])
        y_mv = sb("y_mv", [P, TILES, 2])
        y_var = sb("y_var", [P, 2])
        y_rstd = sb("y_rstd", [P, TILES])
        x1T = sb("x1T", [P, 2, D])
        logits = sb("logits", [P, TILES, E])
        l_max = sb("l_max", [P, TILES])
        l_cen = sb("l_cen", [P, TILES, E])
        l_exp = sb("l_exp", [P, TILES, E])
        l_sum = sb("l_sum", [P, TILES])
        l_inv = sb("l_inv", [P, TILES])
        r_probs = sb("r_probs", [P, TILES, E])
        top8 = sb("top8", [P, TILES, TOPK])
        l_left = sb("l_left", [P, TILES, E])
        chosen = sb("chosen", [P, TILES, E], BF16)
        earlier = sb("earlier", [P, E], BF16)
        c_choice = sb("c_choice", [P, E])
        fits = sb("fits", [P, TILES, E])
        slot = sb("slot", [P, TILES, E])
        slot8 = sb("slot8", [P, TILES, TOPK])
        slot_i = sb("slot_i", [P, TILES, TOPK], I32)
        block_i = sb("block_i", [P, TILES, TOPK], I32)
        place_i = sb("place_i", [P, TILES, TOPK], I32)
        block_f = sb("block_f", [P, TILES, TOPK])
        place_f = sb("place_f", [P, TILES, TOPK])
        hot_place = sb("hot_place", [P, 2, 2 * TOPK, P], F16)
        hot_block = sb("hot_block", [P, 2, 2 * TOPK, P], F16)
        pair_base = sb("pair_base", [P, 1])
        id_part = sb("id_part", [P, BLOCKS])
        ids = sb("ids", [P, BLOCKS])
        ids_t = sb("ids_t", [P, BLOCKS])
        rows_u = sb("rows_u", [P, BLOCKS], U32)
        W_GU, W_DN = KD * 2 * FF, KF * D
        w_gu = sb("w_gu", [P, 2, W_GU])
        w_dn = sb("w_dn", [P, 2, W_DN])
        rows_get = sb("rows_get", [P, 2 * HALVES], U32)
        rows_put = sb("rows_put", [P, 2 * HALVES], U32)
        xg = sb("xg", [P, 2 * HALVES, ROW])
        xgT = xT_sb[:, :, :].rearrange("p k n -> p (k n)")[:, 0:2 * KD * CAP].rearrange(
            "p (r k c) -> p r k c", r=2, k=KD)
        gate_act = x_sb[:, 0, :]
        h_sb = x_sb[:, 1:3, :]
        ye = x_sb[:, 3:3 + 2 * HALVES, :]
        w_slot = sb("w_slot", [P, 2 * HALVES])
        zeros = l_left[:, :, :].rearrange("p t e -> p (t e)")
        f_stats = sb("f_stats", [P, 4, 6])
        f_mv = sb("f_mv", [P, 4, 2])
        f_var = sb("f_var", [P, 4])
        f_rstd = sb("f_rstd", [P, 4])
        bank = [ctx.enter_context(nc.psum_tensor(f"bank{i}", [P, 512], F32)) for i in range(8)]
        FINAL = 4
        ROUNDS3 = TOKENS // (FINAL * P)

        for name in (
            "bias_loaded", "c_cen_done", "c_mean_done", "c_norm_done", "c_rstd_done", "c_sq_done",
            "c_ssq_done", "c_sum_done", "c_var_done", "chT_done", "chT_ps", "choice_sum", "chosen_done",
            "compressed", "const_done", "const_loaded", "dummy_stored", "earlier_done", "exp_done",
            "f_mv_done", "f_rstd_done", "f_stats_done", "f_var_done", "final_done", "gate_done",
            "gate_loaded", "h_done", "hot_done", "hot_used", "id_part_done", "ids_done", "inv_done",
            "l_cen_done", "l_exp_done", "l_inv_done", "l_left_done", "l_max_done", "l_ready", "l_sum_done",
            "logits_done", "logits_ps", "max_done", "mv_done", "oT_done", "oT_ps", "o_done", "o_ps",
            "out_ps", "pos_ps", "started", "probsT_done", "probsT_ps", "probs_done", "probs_stored",
            "proj_ps", "proj_zero", "qk_ready", "res_done", "route_loaded", "rows_ready", "rows_step",
            "rstd_done", "scores_done", "scrap_written", "slot8_done", "slot_done", "slot_i_done", "slot_sum", "split_done",
            "split_f_done", "stats_done", "top8_done", "turned_done", "up_ps", "v_done", "v_ps",
            "w_fold2_loaded", "w_fold_loaded", "w_in_done", "w_in_ps", "w_out_done", "w_out_ps",
            "w_slot_done", "w_sum_done", "x1T_done", "x1T_ps", "x1_done", "xT_loaded", "xb_done",
            "xgT_done0", "xgT_done1", "xgT_ps", "y_done", "y_read0", "y_read1", "y_var_done", "zeros_ready",
            "gu_loaded0", "gu_loaded1", "dn_loaded0", "dn_loaded1", "sum_loaded0", "sum_loaded1",
            "out_stored0", "out_stored1", "gathered0", "gathered1", "added0", "added1",
        ):
            sems[name] = ctx.enter_context(nc.semaphore(name))
        for m in range(TILES):
            for name in ("x_loaded%d" % m, "x1_stored%d" % m):
                sems[name] = ctx.enter_context(nc.semaphore(name))
        block = ctx.enter_context(nc.Block())

        def slot_of(m):
            return (m % 2) * JT + m // 2

        def rounds(eng, body):
            for p in (-1, 0, 1, 2):
                body(p)
            with eng.Fori(3, PAIRS - 1) as p:
                body(p)
            for p in (PAIRS - 1, PAIRS, PAIRS + 1):
                body(p)

        x_t = x.rearrange("(q s p) d -> q s p d", s=TILES, p=P)
        xT_t = xT.rearrange("q p n -> q p n")
        row_t = table[0:TOKENS, :].rearrange("(q s p) d -> q s p d", s=TILES, p=P)
        rowp_t = table[0:TOKENS, D:ROW].rearrange("(q s p) d -> q p s d", s=TILES, p=P)
        sum_t = total[0:TOKENS, :].rearrange("(q s p) d -> q s p d", s=TILES, p=P)
        sum3 = total[0:TOKENS, :].rearrange("(r s p) d -> r p s d", s=FINAL, p=P)
        out3 = out.rearrange("(r s p) d -> r p s d", s=FINAL, p=P)

        @block.sync
        def _(sp):
            def load_x(q, m):
                sp.dma_start(x_sb[:, m, :], x_t[bass.ds(q, 1), slot_of(m), :, :].rearrange("a p d -> p (a d)")
                             ).then_inc(S("x_loaded%d" % m), 16)

            def load_xT(q):
                sp.dma_start(xT_sb[:, :, :].rearrange("p k n -> p (k n)"),
                             xT_t[bass.ds(q, 1), :, :].rearrange("a p n -> p (a n)")
                             ).then_inc(S("xT_loaded"), 16)

            def load_gu(g, r):
                sp.dma_start(w_gu[:, r, :], w_experts[bass.ds(g * 2 + r, 1), :, 0:W_GU].rearrange("a p n -> p (a n)")
                             ).then_inc(S("gu_loaded%d" % r), 16)

            def load_dn(g, r):
                sp.dma_start(w_dn[:, r, :], w_experts[bass.ds(g * 2 + r, 1), :, W_GU:W_GU + W_DN].rearrange("a p n -> p (a n)")
                             ).then_inc(S("dn_loaded%d" % r), 16)

            sp.dma_start(w_kv_sb[:, :], w_kv).then_inc(S("w_fold_loaded"), 16)
            sp.dma_start(w_comp_sb[:, :], w_compT).then_inc(S("w_fold_loaded"), 16)
            load_xT(0)
            sp.dma_start(w_sum[:, :], w_resT).then_inc(S("w_fold2_loaded"), 16)
            sp.dma_start(w_c2l_sb[:, :], w_c2l).then_inc(S("w_fold2_loaded"), 16)
            sp.dma_start(ident[:, :], const[0, :, :]).then_inc(S("const_loaded"), 16)
            sp.dma_start(const_f[:, :, :], const[0:5, :, :].rearrange("c p n -> p c n")).then_inc(S("const_loaded"), 16)
            sp.dma_start(rope_sb[:, :, :], rope.rearrange("c p n -> p c n")).then_inc(S("const_loaded"), 16)
            sp.wait_ge(S("proj_zero"), 1)
            for b in range(2):
                part = slice(DC * b, DC * b + DC)
                sp.dma_start(proj[part, :, part], w_proj.rearrange("c p n -> p c n")).then_inc(S("const_loaded"), 16)
                sp.dma_start(gamma_sb[part, :], gamma).then_inc(S("const_loaded"), 16)
                sp.dma_start(beta_sb[part, :], beta).then_inc(S("const_loaded"), 16)
            sp.dma_start(bias_sb[:, :], bias[0:1, :].to_broadcast([P, D])).then_inc(S("bias_loaded"), 16)
            for m in range(TILES):
                load_x(0, m)
            sp.dma_start(gate_sb[:, :, :], gateT.rearrange("(k p) e -> p k e", p=P)).then_inc(S("gate_loaded"), 16)
            sp.dma_start(empty_row[:, :], const[5, :, :]).then_inc(S("route_loaded"), 16)
            sp.dma_start(slot_base[:, :, :].rearrange("p t e -> p (t e)"),
                         const[6:10, :, :].rearrange("c p n -> p c n")).then_inc(S("route_loaded"), 16)
            sp.dma_start(local_id[:, :], const[10, :, 0:TILES]).then_inc(S("route_loaded"), 16)
            sp.wait_ge(S("zeros_ready"), 1)
            for h in range(DUMMY // P):
                rows = slice(TOKENS + h * P, TOKENS + (h + 1) * P)
                sp.dma_start(table[rows, 0:D], zeros[:, :]).then_inc(S("dummy_stored"), 16)
                sp.dma_start(table[rows, D:ROW], zeros[:, 0:E]).then_inc(S("dummy_stored"), 16)
                sp.dma_start(total[rows, :], zeros[:, :]).then_inc(S("dummy_stored"), 16)

            def body(p):
                for m in range(TILES):
                    if m == 2 and live(p + 2) and (not isinstance(p, int) or p + 2 >= 1):
                        if not isinstance(p, int) or p + 2 < PAIRS:
                            wait(sp, "compressed", 2, p + 1, 2)
                            load_xT(p + 2)
                    q, t = tile_at(p, m, LAG_X1)
                    if live(q):
                        wait(sp, "x1_done", TILES, q, t + 1)
                        sp.dma_start(row_t[bass.ds(q, 1), slot_of(t), :, 0:D].rearrange("a p d -> p (a d)"),
                                     x1_sb[:, t, :]).then_inc(S("x1_stored%d" % t), 16)
                        sp.dma_start(sum_t[bass.ds(q, 1), slot_of(t), :, :].rearrange("a p d -> p (a d)"),
                                     x1_sb[:, t, :]).then_inc(S("x1_stored%d" % t), 16)
                    if live(q) and (not isinstance(q, int) or q + 1 < PAIRS):
                        wait(sp, "res_done", TILES, q, t + 1)
                        load_x(q + 1, t)
                    if m == 7 and live(p - 1):
                        wait(sp, "probs_done", 1, p - 1, 1)
                        sp.dma_start(rowp_t[bass.ds(p - 1, 1), :, :, :].rearrange("a p s e -> p (a s) e"),
                                     r_probs[:, :, :]).then_inc(S("probs_stored"), 16)

            for p in (-1, 0, 1):
                body(p)
            with sp.Fori(2, PAIRS - 2) as p:
                body(p)
            body(PAIRS - 2)
            for r in range(2):
                load_gu(0, r)
                load_dn(0, r)
            for p in (PAIRS - 1, PAIRS, PAIRS + 1):
                body(p)

            for r in range(2):
                wait(sp, "up_ps", 4, 0, 2 * r + 2)
                load_gu(1, r)
            with sp.Fori(1, E // 2 - 1) as g:
                for r in range(2):
                    wait(sp, "y_done", 4, g - 1, 2 * r + 2)
                    load_dn(g, r)
                    wait(sp, "up_ps", 4, g, 2 * r + 2)
                    load_gu(g + 1, r)
            for r in range(2):
                wait(sp, "y_done", 4, E // 2 - 2, 2 * r + 2)
                load_dn(E // 2 - 1, r)

            for r in range(2):
                wait(sp, "added%d" % r, 32, E // 2, 0)

            def load_sum(n, r):
                sp.dma_start(x_sb[:, FINAL * r:FINAL * (r + 1), :],
                             sum3[bass.ds(n, 1), :, :, :].rearrange("a p s d -> p (a s) d")
                             ).then_inc(S("sum_loaded%d" % r), 16)

            def store_out(g, r):
                wait(sp, "final_done", 2, g, r + 1)
                sp.dma_start(out3[bass.ds(g * 2 + r, 1), :, :, :].rearrange("a p s d -> p (a s) d"),
                             x1_sb[:, FINAL * r:FINAL * (r + 1), :]).then_inc(S("out_stored%d" % r), 16)

            for r in range(2):
                load_sum(r, r)
            with sp.Fori(0, ROUNDS3 // 2 - 1) as g:
                for r in range(2):
                    store_out(g, r)
                    load_sum(g * 2 + (r + 2), r)
            for r in range(2):
                store_out(ROUNDS3 // 2 - 1, r)
            for r in range(2):
                sp.wait_ge(S("out_stored%d" % r), 16 * (ROUNDS3 // 2))

        @block.tensor
        def _(pe):
            pe.wait_ge(S("w_fold_loaded"), 32)
            for k in range(KD):
                last = nc.tensor.matmul(bank[0][:, k * DC:(k + 1) * DC], w_kv_sb[:, k * P:(k + 1) * P],
                                        w_comp_sb[:, :], start=True, stop=True)
            last.then_inc(S("w_in_ps"), 1)
            pe.wait_ge(S("w_sum_done"), 1)
            nc.tensor.matmul(bank[1][:, :], w_c2l_sb[:, :], w_sum[:, :], start=True, stop=True
                             ).then_inc(S("w_out_ps"), 1)
            pe.wait_ge(S("w_in_done"), 1)
            pe.wait_ge(S("w_out_done"), 1)
            pe.wait_ge(S("const_loaded"), 16 * 9)
            pe.wait_ge(S("const_done"), 5)

            def body(p):
                for m in range(TILES):
                    j, b = m // 2, m % 2
                    if live(p):
                        if m == 0:
                            wait(pe, "qk_ready", 2, p, 2)
                        wait(pe, "exp_done", TILES, p, m - 1)
                        s_ps = bank[2 + m % 2]
                        n = P * (j + 1)
                        part = slice(DC * b, DC * b + DC)
                        nc.tensor.matmul(s_ps[:, 0:n], qT[part, P * j:P * (j + 1)], kT[part, 0:n],
                                         start=True, stop=False)
                        nc.tensor.matmul(s_ps[:, P * j:n], ident_h[:, :], causal_h[:, :],
                                         start=False, stop=True).then_inc(S("scores_done"), 1)
                    q, t = tile_at(p, m, LAG_OUT)
                    if live(q):
                        wait(pe, "oT_done", JT, q, t // 2 + 1)
                        wait(pe, "x1T_done", TILES, q, t - 2)
                        wait(pe, "res_done", TILES, q, t)
                        part = slice(DC * (t % 2), DC * (t % 2) + DC)
                        nc.tensor.matmul(bank[6][:, :], oT[part, (t // 2) % 2, :], w_out[part, :],
                                         start=True, stop=True).then_inc(S("out_ps"), 1)
                    q, t = tile_at(p, m, LAG_LOGITS)
                    if live(q):
                        if isinstance(q, int) and q == 0 and t == 0:
                            pe.wait_ge(S("gate_loaded"), 16)
                        wait(pe, "x1T_done", TILES, q, t + 1)
                        q2, t2 = tile_at(p, m, LAG_NORM)
                        if live(q2):
                            wait(pe, "o_done", TILES, q2, t2 + 1)
                        at = 384 + E * (t % 2)
                        for k in range(KD):
                            last = nc.tensor.matmul(bank[5][:, at:at + E], x1T[:, t % 2, P * k:P * (k + 1)],
                                                    gate_sb[:, k, :], start=(k == 0), stop=(k == KD - 1))
                        last.then_inc(S("logits_ps"), 1)
                    q, t = tile_at(p, m, LAG_PROBS)
                    if live(q):
                        wait(pe, "exp_done", TILES, q, t + 1)
                        wait(pe, "probsT_done", TILES, q, t)
                        for i in range(t // 2 + 1):
                            last = nc.tensor.transpose(bank[4][:, P * i:P * (i + 1)],
                                                       probs[:, t % 2, P * i:P * (i + 1)], ident[:, :])
                        last.then_inc(S("probsT_ps"), 1)
                    if m % 2 == 1:
                        q, t = tile_at(p, m, LAG_OT)
                        if live(q):
                            wait(pe, "o_done", TILES, q, t + 2)
                            q7, t7 = tile_at(p, m, LAG_LOGITS)
                            if live(q7):
                                wait(pe, "logits_done", TILES, q7, t7 + 1)
                            nc.tensor.transpose(bank[5][:, 256:384], o_sb[:, (t // 2) % 2, :], ident[:, :]
                                                ).then_inc(S("oT_ps"), 1)
                    q3 = p - 2
                    if m == 0 and live(q3):
                        wait(pe, "chosen_done", 1, q3, 1)
                        wait(pe, "earlier_done", 1, q3, 1)
                        wait(pe, "ids_done", 1, q3, 0)
                        pos = bank[7][:, :].rearrange("p (t e) -> p t e", e=E)
                        nc.tensor.matmul(pos, before_h[:, :], chosen[:, :, :], start=True, stop=False)
                        for s in range(TILES - 1):
                            n = TILES - 1 - s
                            nc.tensor.matmul(pos[:, s + 1:TILES, :], ones_h[:, :],
                                             chosen[:, s:s + 1, :].to_broadcast([P, n, E]),
                                             start=False, stop=False)
                        nc.tensor.matmul(pos, ones_h[:, :], earlier[:, None, :].to_broadcast([P, TILES, E]),
                                         start=False, stop=True).then_inc(S("pos_ps"), 1)
                    if 3 <= m <= 6 and live(q3):
                        c = m - 3
                        wait(pe, "hot_done", 4, q3, c + 1)
                        for i in range(2 * TOPK):
                            last = nc.tensor.matmul(bank[7][:, 0:BLOCKS], hot_place[:, c % 2, i, :],
                                                    hot_block[:, c % 2, i, :],
                                                    start=(c == 0 and i == 0), stop=(c == 3 and i == 2 * TOPK - 1))
                        last.then_inc(S("hot_used"), 1)
                    q1 = p + 1
                    if live(q1):
                        if m in (0, 1):
                            if m == 0:
                                wait(pe, "xT_loaded", 16, q1, 16)
                                wait(pe, "turned_done", 4, q1, 0)
                            for n in range(4 * m, 4 * m + 4):
                                at = P * slot_of(n)
                                for k in range(KD):
                                    last = nc.tensor.matmul(bank[0][:, DC * n:DC * (n + 1)],
                                                            xT_sb[:, k, at:at + P], w_in[:, k, :],
                                                            start=(k == 0), stop=(k == KD - 1))
                            last.then_inc(S("compressed"), 1)
                        if m == 4:
                            wait(pe, "c_norm_done", 1, q1, 1)
                            wait(pe, "v_done", 1, q1, 0)
                            for j in range(JT):
                                last = nc.tensor.transpose(bank[1][:, P * j:P * (j + 1)],
                                                           c_norm[:, 2 * j:2 * j + 2, :].rearrange("p t c -> p (t c)"),
                                                           ident[:, :])
                            last.then_inc(S("chT_ps"), 1)
                        if m == 5:
                            wait(pe, "chT_done", 1, q1, 1)
                            wait(pe, "c_cen_done", 1, q1, 1)
                            nc.tensor.matmul(bank[1][:, :], proj[:, 0, :], chT[:, :], start=True, stop=True
                                             ).then_inc(S("proj_ps"), 1)
                            nc.tensor.matmul(bank[0][:, :], proj[:, 1, :], chT[:, :], start=True, stop=True
                                             ).then_inc(S("proj_ps"), 1)
                        if m == 6:
                            wait(pe, "turned_done", 4, q1, 1)
                            nc.tensor.matmul(bank[1][:, :], proj[:, 2, :], chT[:, :], start=True, stop=True
                                             ).then_inc(S("proj_ps"), 1)
                            wait(pe, "turned_done", 4, q1, 2)
                            nc.tensor.matmul(bank[0][:, :], proj[:, 3, :], chT[:, :], start=True, stop=True
                                             ).then_inc(S("proj_ps"), 1)
                        if m == 7:
                            wait(pe, "turned_done", 4, q1, 3)
                            for j in range(JT):
                                last = nc.tensor.matmul(bank[1][:, P * j:P * (j + 1)], chT[:, P * j:P * (j + 1)],
                                                        proj[:, 4, :], start=True, stop=True)
                            last.then_inc(S("v_ps"), 1)
                    q, t = tile_at(p, m, LAG_X1T)
                    if live(q):
                        wait(pe, "x1_done", TILES, q, t + 1)
                        wait(pe, "x1T_done", TILES, q, t)
                        q4, t4 = tile_at(p, m, LAG_OUT)
                        if live(q4):
                            wait(pe, "res_done", TILES, q4, t4 + 1)
                        for k in range(KD):
                            last = nc.tensor.transpose(bank[6][:, P * k:P * (k + 1)],
                                                       x1_sb[:, t, P * k:P * (k + 1)], ident[:, :])
                        last.then_inc(S("x1T_ps"), 1)
                    q, t = tile_at(p, m, LAG_PROBS)
                    if live(q):
                        if t == 0:
                            wait(pe, "v_done", 1, q, 1)
                        wait(pe, "probsT_done", TILES, q, t + 1)
                        for name, per, lag in (("o_done", 1, LAG_NORM), ("logits_done", 1, LAG_LOGITS),
                                               ("oT_done", 2, LAG_OT + (m + 1) % 2)):
                            q5, t5 = tile_at(p, m, lag)
                            if live(q5):
                                wait(pe, name, TILES // per, q5, t5 // per + 1)
                        j, b = t // 2, t % 2
                        at = P * (j % 2) + DC * b
                        for i in range(j + 1):
                            last = nc.tensor.matmul(bank[5][:, at:at + DC], probsT[:, t % 2, P * i:P * (i + 1)],
                                                    v_sb[:, i, DC * b:DC * (b + 1)], start=(i == 0), stop=(i == j))
                        last.then_inc(S("o_ps"), 1)

            rounds(pe, body)

            def tokens_in(g, r):
                wait(pe, "gathered%d" % r, 32, g, 32)
                for i in range(2):
                    wait(pe, "xgT_done%d" % i, 2, g, r)
                    for kk in range(2):
                        for h in range(HALVES):
                            k = 2 * i + kk
                            at = CAP * kk + P * h
                            last = nc.tensor.transpose(bank[i][:, at:at + P],
                                                       xg[:, HALVES * r + h, P * k:P * (k + 1)], ident[:, :])
                    last.then_inc(S("xgT_ps"), 1)

            def up(g, r):
                wait(pe, "gu_loaded%d" % r, 16, g, 16)
                wait(pe, "xgT_done0", 2, g, r + 1)
                wait(pe, "xgT_done1", 2, g, r + 1)
                wait(pe, "h_done", 2, g, r)
                for u in range(2):
                    for f in range(KF):
                        for k in range(KD):
                            at = 2 * FF * k + FF * u + P * f
                            last = nc.tensor.matmul(bank[2 + u][:, CAP * f:CAP * (f + 1)],
                                                    w_gu[:, r, at:at + P], xgT[:, r, k, :],
                                                    start=(k == 0), stop=(k == KD - 1))
                    last.then_inc(S("up_ps"), 1)

            def down(g, r):
                wait(pe, "dn_loaded%d" % r, 16, g, 16)
                wait(pe, "h_done", 2, g, r + 1)
                for h in range(HALVES):
                    wait(pe, "y_read%d" % h, 2, g, r)
                    for f in range(KF):
                        last = nc.tensor.matmul(bank[4 + h][:, :], h_sb[:, r, CAP * f + P * h:CAP * f + P * (h + 1)],
                                                w_dn[:, r, D * f:D * (f + 1)], start=(f == 0), stop=(f == KF - 1))
                    last.then_inc(S("y_done"), 1)

            for r in range(2):
                tokens_in(0, r)
                up(0, r)
            def both(g):
                for r in range(2):
                    tokens_in(g, r)
                    down(g - 1, r)
                    up(g, r)

            both(1)
            with pe.Fori(2, E // 2) as g:
                both(g)
            for r in range(2):
                down(E // 2 - 1, r)

        @block.vector
        def _(dve):
            nc.vector.memset(proj[:, :, :], 0.0).then_inc(S("proj_zero"), 1)
            nc.vector.memset(zeros[:, :], 0.0).then_inc(S("zeros_ready"), 1)
            nc.vector.memset(earlier[:, :], 0.0).then_inc(S("earlier_done"), 1)
            nc.vector.memset(ids[:, :], 0.0)
            nc.vector.memset(pair_base[:, :], 0.0)
            nc.vector.memset(eps_add[:, :], EPS)
            nc.vector.memset(eps_pow[:, :], -0.5).then_inc(S("started"), 1)
            dve.wait_ge(S("w_in_ps"), 1)
            nc.vector.tensor_copy(w_in[:, :, :].rearrange("p k c -> p (k c)"), bank[0][:, 0:KD * DC]
                                  ).then_inc(S("w_in_done"), 1)
            dve.wait_ge(S("w_fold2_loaded"), 32)
            nc.vector.tensor_add(w_sum[:, :], w_sum[:, :], w_kv_sb[:, :]).then_inc(S("w_sum_done"), 1)
            dve.wait_ge(S("w_out_ps"), 1)
            nc.vector.tensor_copy(w_out[:, :], bank[1][:, :]).then_inc(S("w_out_done"), 1)
            dve.wait_ge(S("const_loaded"), 16 * 9)
            for i, half in enumerate((ident_h, causal_h, before_h, ones_h, ramp_h)):
                nc.vector.tensor_copy(half[:, :], const_f[:, i, :]).then_inc(S("const_done"), 1)

            def body(p):
                for m in range(TILES):
                    if live(p):
                        wait(dve, "scores_done", TILES, p, m + 1)
                        wait(dve, "exp_done", TILES, p, m - 7)
                        nc.vector.tensor_reduce(neg_max[:, m:m + 1], bank[2 + m % 2][:, 0:P * (m // 2 + 1)],
                                                AX.X, ALU.max, negate=True).then_inc(S("max_done"), 1)
                    q, t = tile_at(p, m, LAG_NORM)
                    if live(q):
                        wait(dve, "exp_done", TILES, q, t + 1)
                        nc.vector.reciprocal(exp_inv[:, t:t + 1], exp_sum[:, t:t + 1]).then_inc(S("inv_done"), 1)
                        wait(dve, "inv_done", TILES, q, t + 1)
                        wait(dve, "o_ps", TILES, q, t + 1)
                        wait(dve, "oT_ps", JT, q, t // 2 - 1)
                        at = P * ((t // 2) % 2) + DC * (t % 2)
                        nc.vector.tensor_scalar(o_sb[:, (t // 2) % 2, DC * (t % 2):DC * (t % 2 + 1)],
                                                bank[5][:, at:at + DC], exp_inv[:, t:t + 1], None, ALU.mult
                                                ).then_inc(S("o_done"), 1)
                    q, t = tile_at(p, m, LAG_X1)
                    if live(q):
                        wait(dve, "rstd_done", TILES, q, t + 1)
                        wait(dve, "x1_stored%d" % t, 32, q, 0)
                        wait(dve, "x1T_ps", TILES, q, t - 7)
                        nc.vector.tensor_scalar(x1_sb[:, t, :], y_sb[:, t % 2, :], y_mv[:, t, 0:1],
                                                y_rstd[:, t:t + 1], ALU.subtract, ALU.mult).then_inc(S("x1_done"), 1)
                    q, t = tile_at(p, m, LAG_OUT)
                    if live(q):
                        wait(dve, "out_ps", TILES, q, t + 1)
                        wait(dve, "xb_done", TILES, q, t + 1)
                        nc.vector.tensor_add(y_sb[:, t % 2, :], bank[6][:, :], x_sb[:, t, :]).then_inc(S("res_done"), 1)
                        wait(dve, "res_done", TILES, q, t + 1)
                        nc.vector.bn_stats(y_stats[:, t % 2, :], y_sb[:, t % 2, :]).then_inc(S("stats_done"), 1)
                        wait_apart(dve, ("stats_done", TILES, q, t + 1))
                        nc.vector.bn_aggr(y_mv[:, t, :], y_stats[:, t % 2, :]).then_inc(S("mv_done"), 1)
                    q1 = p + 1
                    if live(q1):
                        if m == 2:
                            wait(dve, "compressed", 2, q1, 2)
                            c_ps = bank[0][:, :].rearrange("p (t c) -> p t c", c=DC)
                            nc.vector.reduce_sum(c_sum[:, :], c_ps, AX.X).then_inc(S("c_sum_done"), 1)
                            wait(dve, "c_sum_done", 1, q1, 1)
                            nc.vector.tensor_scalar(c_negmean[:, :], c_sum[:, :], -1.0 / DC, None, ALU.mult
                                                    ).then_inc(S("c_mean_done"), 1)
                            wait(dve, "c_mean_done", 1, q1, 1)
                            nc.vector.tensor_add(c_cen[:, :, :], c_ps, c_negmean[:, :, None].to_broadcast([P, TILES, DC])
                                                 ).then_inc(S("c_cen_done"), 1)
                        if m == 3:
                            wait(dve, "c_sq_done", 1, q1, 1)
                            nc.vector.reduce_sum(c_ssq[:, :], c_sq[:, :, :], AX.X).then_inc(S("c_ssq_done"), 1)
                            wait(dve, "c_ssq_done", 1, q1, 1)
                            wait(dve, "c_rstd_done", 1, q1, 0)
                            nc.vector.tensor_scalar(c_var[:, :], c_ssq[:, :], 1.0 / DC, EPS, ALU.mult, ALU.add
                                                    ).then_inc(S("c_var_done"), 1)
                        if m == 4:
                            wait(dve, "c_rstd_done", 1, q1, 1)
                            wait(dve, "chT_ps", 1, q1, 0)
                            nc.vector.tensor_mul(c_norm[:, :, :], c_cen[:, :, :],
                                                 c_rstd[:, :, None].to_broadcast([P, TILES, DC])
                                                 ).then_inc(S("c_norm_done"), 1)
                        if m in (5, 6):
                            for i in (2 * (m - 5), 2 * (m - 5) + 1):
                                wait(dve, "proj_ps", 4, q1, i + 1)
                                nc.vector.tensor_mul(turned[:, i, :], bank[1 - i % 2][:, :], rope_sb[:, i, :]
                                                     ).then_inc(S("turned_done"), 1)
                    q3 = p - 2
                    if live(q3):
                        if m == 0:
                            wait(dve, "pos_ps", 1, q3, 1)
                            pos = bank[7][:, :].rearrange("p (t e) -> p t e", e=E)
                            flat = "p t e -> p (t e)"
                            nc.vector.scalar_tensor_tensor(fits[:, :, :].rearrange(flat), bank[7][:, :], float(CAP),
                                                           chosen[:, :, :].rearrange(flat), ALU.is_lt, ALU.mult)
                            nc.vector.tensor_add(slot[:, :, :], pos, slot_base[:, :, :]).then_inc(S("slot_sum"), 1)
                            nc.vector.reduce_sum(c_choice[:, :], chosen[:, :, :].rearrange("p t e -> p e t"), AX.X
                                                 ).then_inc(S("choice_sum"), 1)
                            wait(dve, "slot_sum", 1, q3, 1)
                            nc.vector.tensor_mul(slot[:, :, :], slot[:, :, :], fits[:, :, :]).then_inc(S("slot_done"), 1)
                            wait(dve, "choice_sum", 1, q3, 1)
                            nc.vector.tensor_add(earlier[:, :], earlier[:, :], c_choice[:, :]).then_inc(S("earlier_done"), 1)
                        if m == 1:
                            wait_apart(dve, ("slot_done", 1, q3, 1))
                            for s in range(TILES):
                                last = nc.vector.max(slot8[:, s, :], slot[:, s, :])
                            last.then_inc(S("slot8_done"), 1)
                            wait(dve, "slot8_done", 1, q3, 1)
                            nc.vector.tensor_scalar(slot_i[:, :, :], slot8[:, :, :], -1.0, None, ALU.add
                                                    ).then_inc(S("slot_i_done"), 1)
                            wait(dve, "slot_i_done", 1, q3, 1)
                            nc.vector.tensor_scalar(block_i[:, :, :], slot_i[:, :, :], 7, None, ALU.arith_shift_right)
                            nc.vector.tensor_scalar(place_i[:, :, :], slot_i[:, :, :], P - 1, None, ALU.bitwise_and
                                                    ).then_inc(S("split_done"), 1)
                            wait(dve, "split_done", 1, q3, 1)
                            nc.vector.tensor_copy(block_f[:, :, :], block_i[:, :, :])
                            nc.vector.tensor_copy(place_f[:, :, :], place_i[:, :, :]).then_inc(S("split_f_done"), 1)
                        if 2 <= m <= 5:
                            c = m - 2
                            if c == 0:
                                wait(dve, "split_f_done", 1, q3, 1)
                            if c >= 2:
                                wait(dve, "hot_used", 4, q3, c - 1)
                            for i in range(2 * TOPK):
                                s, k = 2 * c + i // TOPK, i % TOPK
                                nc.vector.tensor_scalar(hot_place[:, c % 2, i, :], ramp_h[:, :],
                                                        place_f[:, s, k:k + 1], None, ALU.is_equal)
                                last = nc.vector.tensor_scalar(hot_block[:, c % 2, i, :], ramp_h[:, :],
                                                               block_f[:, s, k:k + 1], local_id[:, s:s + 1],
                                                               ALU.is_equal, ALU.mult)
                            last.then_inc(S("hot_done"), 1)
                        if m == 7:
                            wait(dve, "hot_used", 4, q3, 4)
                            nc.vector.scalar_tensor_tensor(id_part[:, :], bank[7][:, 0:BLOCKS], 0.0,
                                                           pair_base[:, 0:1].to_broadcast([P, BLOCKS]),
                                                           ALU.is_gt, ALU.mult)
                            nc.vector.tensor_add(ids_t[:, :], ids[:, :], bank[7][:, 0:BLOCKS]).then_inc(S("id_part_done"), 1)
                            wait(dve, "id_part_done", 1, q3, 1)
                            nc.vector.tensor_scalar_add(pair_base[:, :], pair_base[:, :], float(TILES * P))
                            nc.vector.tensor_add(ids[:, :], ids_t[:, :], id_part[:, :]).then_inc(S("ids_done"), 1)
                    q3 = p - 1
                    if live(q3):
                        if m == 6:
                            wait(dve, "logits_done", TILES, q3, TILES)
                            nc.vector.reduce_max(l_max[:, :], logits[:, :, :], AX.X).then_inc(S("l_max_done"), 1)
                            wait(dve, "l_max_done", 1, q3, 1)
                            wait(dve, "l_exp_done", 1, q3, 0)
                            nc.vector.tensor_sub(l_cen[:, :, :], logits[:, :, :],
                                                 l_max[:, :, None].to_broadcast([P, TILES, E])).then_inc(S("l_cen_done"), 1)
                            wait(dve, "l_cen_done", 1, q3, 1)
                            nc.vector.tensor_scalar_max(l_cen[:, :, :], l_cen[:, :, :], LOG_TINY).then_inc(S("l_ready"), 1)
                        if m == 7:
                            wait(dve, "l_exp_done", 1, q3, 1)
                            nc.vector.reduce_sum(l_sum[:, :], l_exp[:, :, :], AX.X).then_inc(S("l_sum_done"), 1)
                            wait(dve, "l_sum_done", 1, q3, 1)
                            nc.vector.reciprocal(l_inv[:, :], l_sum[:, :]).then_inc(S("l_inv_done"), 1)
                            for s in range(TILES):
                                last = nc.vector.max(top8[:, s, :], l_cen[:, s, :])
                            last.then_inc(S("top8_done"), 1)
                            wait(dve, "l_inv_done", 1, q3, 1)
                            wait(dve, "probs_stored", 16, q3, 0)
                            nc.vector.tensor_mul(r_probs[:, :, :], l_exp[:, :, :],
                                                 l_inv[:, :, None].to_broadcast([P, TILES, E])).then_inc(S("probs_done"), 1)
                            wait_apart(dve, ("top8_done", 1, q3, 1))
                            if isinstance(q3, int) and q3 == 0:
                                dve.wait_ge(S("dummy_stored"), 16 * 3 * (DUMMY // P))
                            for s in range(TILES):
                                last = nc.vector.match_replace(l_left[:, s, :], top8[:, s, :], l_cen[:, s, :], TAKEN)
                            last.then_inc(S("l_left_done"), 1)
                            wait(dve, "l_left_done", 1, q3, 1)
                            wait(dve, "pos_ps", 1, q3, 0)
                            nc.vector.tensor_scalar(chosen[:, :, :], l_left[:, :, :], 0.5 * TAKEN, None, ALU.is_lt
                                                    ).then_inc(S("chosen_done"), 1)
                            wait(dve, "chosen_done", 1, q3, 1)
                    if m == 7 and live(q1):
                        wait(dve, "scores_done", TILES, p, TILES)
                        wait(dve, "turned_done", 4, q1, 4)
                        nc.vector.tensor_add(qT[:, :], turned[:, 0, :], turned[:, 1, :]).then_inc(S("qk_ready"), 1)
                        nc.vector.tensor_add(kT[:, :], turned[:, 2, :], turned[:, 3, :]).then_inc(S("qk_ready"), 1)

            dve.wait_ge(S("route_loaded"), 48)
            rounds(dve, body)

            dve.wait_ge(S("ids_done"), PAIRS)
            nc.vector.tensor_scalar(id_part[:, :], ids[:, :], 0.0, None, ALU.is_equal).then_inc(S("rows_step"), 1)
            dve.wait_ge(S("rows_step"), 1)
            nc.vector.tensor_mul(id_part[:, :], id_part[:, :], empty_row[:, :]).then_inc(S("rows_step"), 1)
            dve.wait_ge(S("rows_step"), 2)
            nc.vector.tensor_add(ids_t[:, :], ids[:, :], id_part[:, :]).then_inc(S("rows_step"), 1)
            dve.wait_ge(S("rows_step"), 3)
            nc.vector.tensor_scalar(rows_u[:, :], ids_t[:, :], -1.0, None, ALU.add).then_inc(S("rows_step"), 1)
            dve.wait_ge(S("rows_step"), 4)

            def list_of(g, r):
                return rows_u[:, bass.ds(g * (2 * HALVES) + HALVES * r, HALVES)]

            def list_get(g, r):
                wait(dve, "gathered%d" % r, 32, g, 0)
                nc.vector.tensor_copy(rows_get[:, HALVES * r:HALVES * (r + 1)], list_of(g, r)
                                      ).then_inc(S("rows_ready"), 1)

            def evac(g, r):
                wait(dve, "xgT_ps", 4, g, 2 * r + 2)
                wait(dve, "up_ps", 4, g, 2 * r - 2)
                nc.vector.tensor_copy(xgT[:, r, 2:4, :].rearrange("p k c -> p (k c)"), bank[1][:, :]
                                      ).then_inc(S("xgT_done1"), 1)

            def weigh(g, r):
                wait(dve, "gathered%d" % r, 32, g, 32)
                wait(dve, "y_read0", 2, g, r - 1)
                wait(dve, "y_read1", 2, g, r - 1)
                nc.vector.tensor_copy(w_slot[:, HALVES * r:HALVES * (r + 1)],
                                      xg[:, HALVES * r:HALVES * (r + 1), bass.ds(g * 2 + (D + r), 1)
                                         ].rearrange("p h a -> p (h a)")).then_inc(S("w_slot_done"), 1)

            def product(g, r):
                wait(dve, "gate_done", 2, g, r + 1)
                wait(dve, "up_ps", 4, g, 2 * r + 2)
                wait(dve, "y_done", 4, g, 2 * r - 2)
                nc.vector.tensor_mul(h_sb[:, r, :], gate_act, bank[3][:, :]).then_inc(S("h_done"), 1)

            def scale(g, r):
                wait(dve, "added%d" % r, 32, g, 0)
                nc.vector.tensor_copy(rows_put[:, HALVES * r:HALVES * (r + 1)], list_of(g, r))
                wait(dve, "y_done", 4, g, 2 * r + 2)
                wait(dve, "w_slot_done", 2, g, r + 1)
                nc.vector.tensor_scalar(ye[:, HALVES * r + 1, :], bank[5][:, :],
                                        w_slot[:, HALVES * r + 1:HALVES * r + 2], None, ALU.mult
                                        ).then_inc(S("y_read1"), 1)

            for r in range(2):
                list_get(0, r)
            for r in range(2):
                evac(0, r)
                weigh(0, r)
                product(0, r)
            def both(g):
                for r in range(2):
                    list_get(g, r)
                    evac(g, r)
                    scale(g - 1, r)
                    weigh(g, r)
                    product(g, r)

            both(1)
            with dve.Fori(2, E // 2) as g:
                both(g)
            for r in range(2):
                scale(E // 2 - 1, r)

            def final(g):
                for r in range(2):
                    buf = x_sb[:, FINAL * r:FINAL * (r + 1), :]
                    wait(dve, "sum_loaded%d" % r, 16, g, 16)
                    wait(dve, "out_stored%d" % r, 16, g, 0)
                    for s in range(FINAL):
                        last = nc.vector.bn_stats(f_stats[:, s, :], buf[:, s, :])
                    last.then_inc(S("f_stats_done"), 1)
                    wait_apart(dve, ("f_stats_done", 2, g, r + 1))
                    for s in range(FINAL):
                        last = nc.vector.bn_aggr(f_mv[:, s, :], f_stats[:, s, :])
                    last.then_inc(S("f_mv_done"), 1)
                    wait(dve, "f_rstd_done", 2, g, r + 1)
                    for s in range(FINAL):
                        last = nc.vector.tensor_scalar(x1_sb[:, FINAL * r + s, :], buf[:, s, :], f_mv[:, s, 0:1],
                                                f_rstd[:, s:s + 1], ALU.subtract, ALU.mult)
                    last.then_inc(S("final_done"), 1)

            final(0)
            with dve.Fori(1, ROUNDS3 // 2) as g:
                final(g)

        @block.scalar
        def _(act):
            def body(p):
                for m in range(TILES):
                    if live(p):
                        wait(act, "max_done", TILES, p, m + 1)
                        wait(act, "probsT_ps", TILES, p, m - 1)
                        wait(act, "inv_done", TILES, p, m - 7)
                        n = P * (m // 2 + 1)
                        nc.scalar.activation(probs[:, m % 2, 0:n], bank[2 + m % 2][:, 0:n], ACT.Exp,
                                             bias=neg_max[:, m:m + 1], accum_out=exp_sum[:, m:m + 1]
                                             ).then_inc(S("exp_done"), 1)
                    q, t = tile_at(p, m, LAG_LOGITS)
                    if live(q):
                        wait(act, "logits_ps", TILES, q, t + 1)
                        wait(act, "l_cen_done", 1, q, 0)
                        at = 384 + E * (t % 2)
                        nc.scalar.copy(logits[:, slot_of(t), :], bank[5][:, at:at + E]).then_inc(S("logits_done"), 1)
                    q, t = tile_at(p, m, LAG_PROBS)
                    if live(q):
                        wait(act, "probsT_ps", TILES, q, t + 1)
                        wait(act, "o_ps", TILES, q, t - 1)
                        n = P * (t // 2 + 1)
                        nc.scalar.copy(probsT[:, t % 2, 0:n], bank[4][:, 0:n]).then_inc(S("probsT_done"), 1)
                    if m % 2 == 1:
                        q, t = tile_at(p, m, LAG_OT)
                        if live(q):
                            wait(act, "oT_ps", JT, q, t // 2 + 1)
                            wait(act, "out_ps", TILES, q, t - 2)
                            nc.scalar.copy(oT[:, (t // 2) % 2, :], bank[5][:, 256:384]).then_inc(S("oT_done"), 1)
                    if m == 0 and live(p):
                        wait(act, "v_ps", 1, p, 1)
                        wait(act, "o_ps", TILES, p, 0)
                        nc.scalar.copy(v_sb[:, :, :].rearrange("p j c -> p (j c)"), bank[1][:, :]
                                       ).then_inc(S("v_done"), 1)
                    q, t = tile_at(p, m, LAG_X1T)
                    if live(q):
                        wait(act, "x1T_ps", TILES, q, t + 1)
                        wait(act, "logits_ps", TILES, q, t - 1)
                        nc.scalar.copy(x1T[:, t % 2, :], bank[6][:, :]).then_inc(S("x1T_done"), 1)
                    if m == 4 and live(p + 1):
                        wait(act, "chT_ps", 1, p + 1, 1)
                        wait(act, "v_ps", 1, p + 1, 0)
                        nc.scalar.activation(chT[:, :], bank[1][:, :], ACT.Identity, bias=beta_sb[:, :],
                                             scale=gamma_sb[:, :]).then_inc(S("chT_done"), 1)
                    if m == 6 and live(p - 1):
                        wait(act, "l_ready", 1, p - 1, 1)
                        wait(act, "probs_done", 1, p - 1, 0)
                        nc.scalar.activation(l_exp[:, :, :], l_cen[:, :, :], ACT.Exp).then_inc(S("l_exp_done"), 1)

            act.wait_ge(S("const_loaded"), 16 * 9)
            rounds(act, body)

            def evac(g, r):
                wait(act, "xgT_ps", 4, g, 2 * r + 1)
                wait(act, "up_ps", 4, g, 2 * r - 2)
                nc.scalar.copy(xgT[:, r, 0:2, :].rearrange("p k c -> p (k c)"), bank[0][:, :]
                               ).then_inc(S("xgT_done0"), 1)

            def gate(g, r):
                wait(act, "up_ps", 4, g, 2 * r + 1)
                wait(act, "h_done", 2, g, r)
                nc.scalar.activation(gate_act, bank[2][:, :], ACT.Silu).then_inc(S("gate_done"), 1)

            def scale(g, r):
                wait(act, "y_done", 4, g, 2 * r + 1)
                wait(act, "w_slot_done", 2, g, r + 1)
                wait(act, "added%d" % r, 32, g, 0)
                nc.scalar.activation(ye[:, HALVES * r, :], bank[4][:, :], ACT.Copy,
                                     scale=w_slot[:, HALVES * r:HALVES * r + 1]).then_inc(S("y_read0"), 1)

            for r in range(2):
                evac(0, r)
                gate(0, r)
            def both(g):
                for r in range(2):
                    evac(g, r)
                    scale(g - 1, r)
                    gate(g, r)

            both(1)
            with act.Fori(2, E // 2) as g:
                both(g)
            for r in range(2):
                scale(E // 2 - 1, r)

        @block.gpsimd
        def _(pool):
            pool.wait_ge(S("bias_loaded"), 16)
            pool.wait_ge(S("started"), 1)
            nc.gpsimd.memset(scrap_p[:, :], 0.0).then_inc(S("scrap_written"), 1)

            def body(p):
                for m in range(TILES):
                    if live(p):
                        wait(pool, "x_loaded%d" % m, 16, p, 16)
                        nc.gpsimd.tensor_tensor(x_sb[:, m, :], x_sb[:, m, :], bias_sb[:, :], ALU.add
                                                ).then_inc(S("xb_done"), 1)
                    q, t = tile_at(p, m, LAG_OUT)
                    if live(q):
                        wait(pool, "mv_done", TILES, q, t + 1)
                        nc.gpsimd.tensor_tensor(y_var[:, t % 2:t % 2 + 1], y_mv[:, t, 1:2], eps_add[:, 0:1], ALU.add
                                                ).then_inc(S("y_var_done"), 1)
                        wait(pool, "y_var_done", TILES, q, t + 1)
                        wait(pool, "x1_done", TILES, q, t - 7)
                        nc.gpsimd.tensor_tensor(y_rstd[:, t:t + 1], y_var[:, t % 2:t % 2 + 1], eps_pow[:, 0:1], ALU.pow
                                                ).then_inc(S("rstd_done"), 1)
                    q1 = p + 1
                    if live(q1):
                        if m == 2:
                            wait(pool, "c_cen_done", 1, q1, 1)
                            wait(pool, "c_ssq_done", 1, q1, 0)
                            nc.gpsimd.tensor_tensor(c_sq[:, :, :], c_cen[:, :, :], c_cen[:, :, :], ALU.mult
                                                    ).then_inc(S("c_sq_done"), 1)
                        if m == 3:
                            wait(pool, "c_var_done", 1, q1, 1)
                            wait(pool, "c_norm_done", 1, q1, 0)
                            nc.gpsimd.tensor_tensor(c_rstd[:, :], c_var[:, :], eps_pow[:, :], ALU.pow
                                                    ).then_inc(S("c_rstd_done"), 1)

            rounds(pool, body)

            def gather(g, r):
                if not isinstance(g, int):
                    wait(pool, "scrap_written", 4, g - 2, 1)
                wait_apart(pool, ("rows_ready", 2, g, r + 1), ("xgT_ps", 4, g, 2 * r - 2),
                           ("w_slot_done", 2, g, r - 1))
                for h in range(HALVES):
                    nc.gpsimd.indirect_dma_start(
                        xg[:, HALVES * r + h, :], None, table[:, :],
                        bass.IndirectOffsetOnAxis(rows_get[:, HALVES * r + h:HALVES * r + h + 1], 0),
                        bounds_check=TOKENS + DUMMY - 1).then_inc(S("gathered%d" % r), 16)

            def scatter(g, r):
                wait_apart(pool, ("added%d" % (1 - r), 32, g, 32 * r), ("y_read0", 2, g, r + 1),
                           ("y_read1", 2, g, r + 1))
                for h in range(HALVES):
                    nc.gpsimd.indirect_dma_start(
                        total[:, :],
                        bass.IndirectOffsetOnAxis(rows_put[:, HALVES * r + h:HALVES * r + h + 1], 0),
                        ye[:, HALVES * r + h, :], None,
                        bounds_check=TOKENS + DUMMY - 1, compute_op=ALU.add).then_inc(S("added%d" % r), 16)

            pool.wait_ge(S("dummy_stored"), 16 * 3 * (DUMMY // P))
            pool.wait_ge(S("probs_stored"), 16 * PAIRS)
            for m in range(TILES):
                pool.wait_ge(S("x1_stored%d" % m), 32 * PAIRS)
            for r in range(2):
                gather(0, r)
            def both(g):
                for r in range(2):
                    gather(g, r)
                    scatter(g - 1, r)

            both(1)
            with pool.Fori(2, E // 2) as g:
                both(g)
            for r in range(2):
                scatter(E // 2 - 1, r)

            with pool.Fori(0, ROUNDS3 // 2) as g:
                for r in range(2):
                    wait(pool, "f_mv_done", 2, g, r + 1)
                    nc.gpsimd.tensor_tensor(f_var[:, :], f_mv[:, :, 1], eps_add[:, 0:FINAL], ALU.add).then_inc(S("f_var_done"), 1)
                    pool.wait_ge(S("f_var_done"), g * 2 + (r + 1))
                    nc.gpsimd.tensor_tensor(f_rstd[:, :], f_var[:, :], eps_pow[:, 0:FINAL], ALU.pow
                                            ).then_inc(S("f_rstd_done"), 1)


def constants():
    import numpy as np
    f = np.float32
    inv = (f(1.0) / f(10000.0) ** (np.arange(0, DC, 2, dtype=f) / f(DC))).astype(f)
    angle = np.arange(SEQ, dtype=f)[:, None] * inv[None, :]
    cos, sin = np.cos(angle).astype(f).T, np.sin(angle).astype(f).T
    cos, sin = np.concatenate([cos, cos]), np.concatenate([-sin, sin])
    scale = f(DC ** -0.5)
    rope = np.stack([np.concatenate([a, a]) for a in (cos * scale, sin * scale, cos, sin)]).astype(f)
    i = np.arange(P)
    const = np.zeros((11, P, P), f)
    const[0] = np.eye(P)
    const[1] = np.where(i[None, :] <= i[:, None], 0.0, TAKEN)
    const[2] = i[:, None] < i[None, :]
    const[3] = 1.0
    const[4] = i[None, :]
    const[5] = TOKENS + 1 + P * (i[None, :] % HALVES) + i[:, None]
    const[6:10] = np.tile(np.arange(E) * CAP + 1, TILES).reshape(4, 1, P)
    const[10, :, 0:TILES] = P * np.arange(TILES)[None, :] + i[:, None] + 1
    return rope, const


def kernel(**inputs):
    import numpy as np
    import concourse.bacc as bacc
    from concourse.bass_utils import run_bass_kernel_spmd

    a = {k.replace("L0_attn_", "").replace("L0_ffn_", ""): np.asarray(v) for k, v in inputs.items()}
    rope, const = constants()
    x = a["x"].reshape(TOKENS, D)
    half = np.r_[DC // 2:DC, 0:DC // 2]
    q, k, v = a["W_q_comp"], a["W_kv_comp"][:DC], a["W_kv_comp"][DC:]
    gu = np.concatenate([a["w_gate"].reshape(E, KD, P, FF), a["w_up"].reshape(E, KD, P, FF)], axis=3)
    gu = gu.transpose(0, 2, 1, 3).reshape(E, P, KD * 2 * FF)
    dn = a["w_down"].reshape(E, KF, P, D).transpose(0, 2, 1, 3).reshape(E, P, KF * D)
    arrays = {
        "xT": x.reshape(PAIRS, TILES * P, KD, P).transpose(0, 3, 2, 1).reshape(PAIRS, P, KD * TILES * P),
        "x": x,
        "w_kv": a["W_to_kv"],
        "w_compT": a["W_compress"].T,
        "gamma": a["ln_gamma"][:, None],
        "beta": a["ln_beta"][:, None],
        "w_proj": np.stack([q.T, q[half].T, k.T, k[half].T, v.T]),
        "w_c2l": np.concatenate([a["W_comp2lat"]] * 2, axis=1),
        "w_resT": a["W_out_res"].T,
        "bias": a["b_out_res"][None, :],
        "gateT": a["gate_w"].T,
        "w_experts": np.concatenate([gu, dn], axis=2),
        "rope": rope,
        "const": const,
    }
    arrays = {n: np.ascontiguousarray(v) for n, v in arrays.items()}
    nc = bacc.Bacc("TRN2", target_bir_lowering=False, num_devices=1)
    args = [nc.dram_tensor(n, v.shape, mybir.dt.from_np(v.dtype), kind="ExternalInput").ap() for n, v in arrays.items()]
    args.append(nc.dram_tensor("out", (TOKENS, D), F32, kind="ExternalOutput").ap())
    attention_router_moe(nc, *args)
    r = run_bass_kernel_spmd(nc, [arrays], core_ids=[0])
    return r.results[0]["out"].reshape(SEQS, SEQ, D)
```

```python
from contextlib import ExitStack

import concourse.bass as bass
from concourse import mybir

F32 = mybir.dt.float32
BF16 = mybir.dt.bfloat16
F16 = mybir.dt.float16
I32 = mybir.dt.int32
U32 = mybir.dt.uint32
ALU = mybir.AluOpType
ACT = mybir.ActivationFunctionType
AX = mybir.AxisListType

P = 128
SEQS, SEQ, D = 16, 512, 512
TOKENS = SEQS * SEQ
LAT, DC = 128, 64
E, TOPK, CAP, FF = 64, 8, 256, 256
KD = D // P
KF = FF // P
JT = SEQ // P
PAIRS = SEQS // 2
TILES = 2 * JT
HALVES = CAP // P
BLOCKS = E * HALVES
ROW = D + E
DUMMY = CAP
EPS = 1e-5
LOG_TINY = -104.0
TAKEN = -1e30

LAG_PROBS = 1
LAG_OUT = 2
LAG_X1 = 4


def attention_router_moe(nc, xT, x, w_kv, w_compT, gamma, beta, w_proj, w_c2l, w_resT, bias, bias_col, gateT,
                         w_experts, rope, const, out):
    table = nc.dram_tensor("token_table", [TOKENS + DUMMY, ROW], F32, kind="Internal").ap()
    total = nc.dram_tensor("running_sum", [TOKENS + DUMMY, D], F32, kind="Internal").ap()
    ctx = ExitStack()
    sems = {}
    places = []

    def sb(name, shape, dt=F32):
        return ctx.enter_context(nc.sbuf_tensor(name, shape, dt))

    def S(name):
        return sems[name]

    def wait(eng, name, per, q, k):
        value = q * per + k
        if isinstance(value, int) and value <= 0:
            return
        eng.wait_ge(S(name), value)

    def wait_apart(eng, *waits):
        for name, per, q, k in waits:
            wait(eng, name, per, q, k)
        if not all(isinstance(q, int) for _, _, q, _ in waits):
            n = len(places)
            places.append(waits[0][0])
            if eng.engine == nc.vector.engine:
                nc.vector.memset(scrap_v[:, n:n + 1], 0.0)
            else:
                nc.gpsimd.tensor_tensor(scrap_p[:, n:n + 1], eps_pow[:, 0:1], eps_pow[:, 0:1], ALU.add
                                        ).then_inc(S("scrap_written"), 1)

    def tile_at(p, m, lag):
        d = m - lag
        return p + d // TILES, d % TILES

    def live(q):
        return not isinstance(q, int) or 0 <= q < PAIRS

    with ctx:
        rope_sb = sb("rope_sb", [P, 4, SEQ])
        ident = sb("ident", [P, P])
        ident_h = sb("ident_h", [P, P], BF16)
        causal_h = sb("causal_h", [P, P], BF16)
        before_h = sb("before_h", [P, P], BF16)
        ones_h = sb("ones_h", [P, P], BF16)
        ramp_h = sb("ramp_h", [P, P, 2], F16)
        const_f = sb("const_f", [P, 5, P])
        local_id = sb("local_id", [P, TILES])
        slot_base = sb("slot_base", [P, TILES, E])
        empty_row = sb("empty_row", [P, P])
        eps_pow = sb("eps_pow", [P, TILES])
        eps_add = sb("eps_add", [P, TILES])
        scrap_v = sb("scrap_v", [P, 64])
        scrap_p = sb("scrap_p", [P, 64])
        bias_sb = sb("bias_sb", [P, D])
        gamma_sb = sb("gamma_sb", [P, 1])
        beta_sb = sb("beta_sb", [P, 1])
        proj = sb("proj", [P, 5, P])
        w_kv_sb = sb("w_kv_sb", [LAT, D])
        w_comp_sb = sb("w_comp_sb", [LAT, DC])
        w_c2l_sb = sb("w_c2l_sb", [LAT, 2 * DC])
        w_sum = sb("w_sum", [LAT, D])
        w_x = sb("w_x", [P, KD, DC + E])
        w_in, gate_sb = w_x[:, :, 0:DC], w_x[:, :, DC:DC + E]
        w_out = sb("w_out", [P, D])
        w_outT = sb("w_outT", [P, KD, P])
        w_out_gate = sb("w_out_gate", [P, E])
        w_in_mean = sb("w_in_mean", [P, KD])
        bias_cols = sb("bias_cols", [P, KD])
        bias_rep = sb("bias_rep", [P, KD, P])
        bias_gate = sb("bias_gate", [P, E])
        minus_one = sb("minus_one", [P, 1])
        xT_sb = sb("xT_sb", [P, KD, TILES * P])
        x_sb = sb("x_sb", [P, TILES, D])
        x1_sb = sb("x1_sb", [P, TILES, D])
        c_sq = sb("c_sq", [P, TILES, DC])
        c_ssq = sb("c_ssq", [P, TILES])
        c_var = sb("c_var", [P, TILES])
        c_rstd = sb("c_rstd", [P, TILES])
        c_norm = sb("c_norm", [P, TILES, DC])
        chT = sb("chT", [P, SEQ])
        turned = sb("turned", [P, 4, SEQ])
        qT = sb("qT", [P, SEQ])
        kT = sb("kT", [P, SEQ])
        v_sb = sb("v_sb", [P, JT, P])
        neg_max = sb("neg_max", [P, TILES])
        exp_sum = sb("exp_sum", [P, TILES])
        exp_inv = sb("exp_inv", [P, TILES])
        probs = sb("probs", [P, 2, SEQ])
        probsT = sb("probsT", [P, 2, SEQ])
        oT = sb("oT", [P, P])
        y_sb = sb("y_sb", [P, 4, D])
        y_stats = sb("y_stats", [P, 2, 6])
        y_mv = sb("y_mv", [P, TILES, 2])
        y_var = sb("y_var", [P, 2])
        y_negmean = sb("y_negmean", [P, 2])
        y_rstd = sb("y_rstd", [P, TILES])
        y_shift = sb("y_shift", [P, TILES])
        x_gate_in = sb("x_gate_in", [P, TILES, E])
        x_gate = sb("x_gate", [P, TILES, E])
        o_gate = sb("o_gate", [P, TILES, E])
        l_raw = sb("l_raw", [P, TILES, E])
        logits = sb("logits", [P, TILES, E])
        l_max = sb("l_max", [P, TILES])
        l_cen = sb("l_cen", [P, TILES, E])
        l_exp = sb("l_exp", [P, TILES, E])
        l_sum = sb("l_sum", [P, TILES])
        l_inv = sb("l_inv", [P, TILES])
        r_probs = sb("r_probs", [P, TILES, E])
        top8 = sb("top8", [P, TILES, TOPK])
        l_left = sb("l_left", [P, TILES, E])
        chosen = sb("chosen", [P, TILES, E], BF16)
        earlier = sb("earlier", [P, E], BF16)
        c_choice = sb("c_choice", [P, E])
        fits = sb("fits", [P, TILES, E])
        slot_at = sb("slot_at", [P, TILES, E])
        slot = sb("slot", [P, TILES, E])
        slot8 = sb("slot8", [P, TILES, TOPK])
        slot_i = sb("slot_i", [P, TILES, TOPK], I32)
        block_i = sb("block_i", [P, TILES, TOPK], I32)
        place_i = sb("place_i", [P, TILES, TOPK], I32)
        block_h = sb("block_h", [P, TILES, TOPK], F16)
        place_h = sb("place_h", [P, TILES, TOPK], F16)
        hot_place = sb("hot_place", [P, 2, TOPK, P, 2], F16)
        hot_block = sb("hot_block", [P, 2, TOPK, P, 2], F16)
        pair_base = sb("pair_base", [P, 1])
        id_part = sb("id_part", [P, BLOCKS])
        ids = sb("ids", [P, BLOCKS])
        ids_t = sb("ids_t", [P, BLOCKS])
        rows_u = sb("rows_u", [P, BLOCKS], U32)
        W_GU, W_DN = KD * 2 * FF, KF * D
        w_gu = sb("w_gu", [P, 2, W_GU])
        w_dn = sb("w_dn", [P, 2, W_DN])
        rows_get = sb("rows_get", [P, 2 * HALVES], U32)
        rows_put = sb("rows_put", [P, 2 * HALVES], U32)
        xg = sb("xg", [P, 2 * HALVES, ROW])
        xgT = xT_sb[:, :, :].rearrange("p k n -> p (k n)")[:, 0:2 * KD * CAP].rearrange(
            "p (r k c) -> p r k c", r=2, k=KD)
        gate_act = x_sb[:, 0, :]
        h_sb = x_sb[:, 1:3, :]
        ye = x_sb[:, 3:3 + 2 * HALVES, :]
        w_new = sb("w_new", [P, 2 * HALVES])
        w_slot = sb("w_slot", [P, 2 * HALVES])
        zeros = l_left[:, :, :].rearrange("p t e -> p (t e)")
        f_stats = sb("f_stats", [P, 4, 6])
        f_mv = sb("f_mv", [P, 4, 2])
        f_var = sb("f_var", [P, 4])
        f_rstd = sb("f_rstd", [P, 4])
        bank = [ctx.enter_context(nc.psum_tensor(f"bank{i}", [P, 512], F32)) for i in range(8)]
        FINAL = 4
        ROUNDS3 = TOKENS // (FINAL * P)

        for name in (
            "bias_gate_ps", "bias_loaded", "c_norm_done", "c_rstd_done", "c_sq_done", "c_ssq_done",
            "c_var_done", "chT_done", "chT_ps", "choice_sum", "chosen_done", "compressed", "const_done",
            "const_loaded", "dummy_stored", "earlier_done", "exp_done", "f_mv_done", "f_rstd_done",
            "f_stats_done", "f_var_done", "final_done", "folded", "gate_centred", "gate_done",
            "gate_loaded", "gate_sum_ps", "h_done", "hot_done", "hot_ones", "hot_used", "id_part_done",
            "ids_done", "inv_done", "l_cen_done", "l_exp_done", "l_inv_done", "l_left_done", "l_max_done",
            "l_raw_done", "l_ready", "l_sum_done", "logits_done", "logits_ps", "logits_scaled", "max_done",
            "mv_done", "oT_done", "o_ps", "out_ps", "pos_ps", "probsT_done", "probsT_ps",
            "probs_done", "probs_stored", "proj_ps", "proj_zero", "qk_ready", "res_done", "route_loaded",
            "rows_ready", "rows_step", "rstd_done", "scores_done", "scrap_written", "shift_done",
            "slot8_done", "slot_done", "slot_i_done", "slot_sum", "split_done", "split_f_done", "started",
            "stats_done", "top8_done", "turned_done", "up_ps", "v_done", "v_ps", "w_fold2_loaded",
            "w_fold_loaded", "w_in_done", "w_in_ps", "w_in_shift", "w_in_sum", "w_new_done", "w_outT_done",
            "w_outT_ps", "w_out_done", "w_out_gate_ps", "w_out_ps", "w_slot_done", "w_sum_done", "x1_done",
            "xT_loaded", "x_gate_done", "x_gate_read", "xb_done", "xgT_done0", "xgT_done1",
            "xgT_ps", "y_done", "y_read0", "y_read1", "y_var_done", "zeros_ready", "gu_loaded0",
            "gu_loaded1", "dn_loaded0", "dn_loaded1", "sum_loaded0", "sum_loaded1", "out_stored0",
            "out_stored1", "gathered0", "gathered1", "added0", "added1",
        ):
            sems[name] = ctx.enter_context(nc.semaphore(name))
        for m in range(TILES):
            for name in ("x_loaded%d" % m, "x1_stored%d" % m):
                sems[name] = ctx.enter_context(nc.semaphore(name))
        block = ctx.enter_context(nc.Block())

        def slot_of(m):
            return (m % 2) * JT + m // 2

        def wide(b):
            return bank[b][:, :].rearrange("p (j w) -> p j w", w=DC + E)

        def of_seq(tensor, b):
            if len(tensor.shape) == 2:
                return tensor[:, :].rearrange("p (j two) -> p j two", two=2)[:, :, b]
            return tensor[:, :, :].rearrange("p (j two) c -> p j two c", two=2)[:, :, b, :]

        def rounds(eng, body):
            for p in (-1, 0, 1, 2):
                body(p)
            with eng.Fori(3, PAIRS - 1) as p:
                body(p)
            for p in (PAIRS - 1, PAIRS, PAIRS + 1):
                body(p)

        x_t = x.rearrange("(q s p) d -> q s p d", s=TILES, p=P)
        xT_t = xT.rearrange("q p n -> q p n")
        row_t = table[0:TOKENS, :].rearrange("(q s p) d -> q s p d", s=TILES, p=P)
        rowp_t = table[0:TOKENS, D:ROW].rearrange("(q s p) d -> q p s d", s=TILES, p=P)
        sum_t = total[0:TOKENS, :].rearrange("(q s p) d -> q s p d", s=TILES, p=P)
        sum3 = total[0:TOKENS, :].rearrange("(r s p) d -> r p s d", s=FINAL, p=P)
        out3 = out.rearrange("(r s p) d -> r p s d", s=FINAL, p=P)

        @block.sync
        def _(sp):
            def load_x(q, m):
                sp.dma_start(x_sb[:, m, :], x_t[bass.ds(q, 1), slot_of(m), :, :].rearrange("a p d -> p (a d)")
                             ).then_inc(S("x_loaded%d" % m), 16)

            def load_xT(q):
                sp.dma_start(xT_sb[:, :, :].rearrange("p k n -> p (k n)"),
                             xT_t[bass.ds(q, 1), :, :].rearrange("a p n -> p (a n)")
                             ).then_inc(S("xT_loaded"), 16)

            def load_gu(g, r):
                sp.dma_start(w_gu[:, r, :], w_experts[bass.ds(g * 2 + r, 1), :, 0:W_GU].rearrange("a p n -> p (a n)")
                             ).then_inc(S("gu_loaded%d" % r), 16)

            def load_dn(g, r):
                sp.dma_start(w_dn[:, r, :], w_experts[bass.ds(g * 2 + r, 1), :, W_GU:W_GU + W_DN].rearrange("a p n -> p (a n)")
                             ).then_inc(S("dn_loaded%d" % r), 16)

            sp.dma_start(w_kv_sb[:, :], w_kv).then_inc(S("w_fold_loaded"), 16)
            sp.dma_start(w_comp_sb[:, :], w_compT).then_inc(S("w_fold_loaded"), 16)
            load_xT(0)
            sp.dma_start(gate_sb[:, :, :], gateT.rearrange("(k p) e -> p k e", p=P)).then_inc(S("gate_loaded"), 16)
            sp.dma_start(bias_cols[:, :], bias_col).then_inc(S("gate_loaded"), 16)
            sp.dma_start(w_sum[:, :], w_resT).then_inc(S("w_fold2_loaded"), 16)
            sp.dma_start(w_c2l_sb[:, :], w_c2l).then_inc(S("w_fold2_loaded"), 16)
            sp.dma_start(ident[:, :], const[0, :, :]).then_inc(S("const_loaded"), 16)
            sp.dma_start(const_f[:, :, :], const[0:5, :, :].rearrange("c p n -> p c n")).then_inc(S("const_loaded"), 16)
            sp.dma_start(rope_sb[:, :, :], rope.rearrange("c p n -> p c n")).then_inc(S("const_loaded"), 16)
            sp.wait_ge(S("proj_zero"), 1)
            for b in range(2):
                part = slice(DC * b, DC * b + DC)
                sp.dma_start(proj[part, :, part], w_proj.rearrange("c p n -> p c n")).then_inc(S("const_loaded"), 16)
                sp.dma_start(gamma_sb[part, :], gamma).then_inc(S("const_loaded"), 16)
                sp.dma_start(beta_sb[part, :], beta).then_inc(S("const_loaded"), 16)
            sp.dma_start(bias_sb[:, :], bias[0:1, :].to_broadcast([P, D])).then_inc(S("bias_loaded"), 16)
            for m in range(TILES):
                load_x(0, m)
            sp.dma_start(empty_row[:, :], const[5, :, :]).then_inc(S("route_loaded"), 16)
            sp.dma_start(slot_base[:, :, :].rearrange("p t e -> p (t e)"),
                         const[6:10, :, :].rearrange("c p n -> p c n")).then_inc(S("route_loaded"), 16)
            sp.dma_start(local_id[:, :], const[10, :, 0:TILES]).then_inc(S("route_loaded"), 16)
            sp.wait_ge(S("zeros_ready"), 1)
            for h in range(DUMMY // P):
                rows = slice(TOKENS + h * P, TOKENS + (h + 1) * P)
                sp.dma_start(table[rows, 0:D], zeros[:, :]).then_inc(S("dummy_stored"), 16)
                sp.dma_start(table[rows, D:ROW], zeros[:, 0:E]).then_inc(S("dummy_stored"), 16)
                sp.dma_start(total[rows, :], zeros[:, :]).then_inc(S("dummy_stored"), 16)

            def body(p):
                for m in range(TILES):
                    if m == 3 and live(p + 2) and (not isinstance(p, int) or p + 2 >= 1):
                        if not isinstance(p, int) or p + 2 < PAIRS:
                            wait(sp, "compressed", 2, p + 1, 2)
                            load_xT(p + 2)
                    q, t = tile_at(p, m, LAG_X1)
                    if live(q):
                        wait(sp, "x1_done", TILES, q, t + 1)
                        sp.dma_start(row_t[bass.ds(q, 1), slot_of(t), :, 0:D].rearrange("a p d -> p (a d)"),
                                     x1_sb[:, t, :]).then_inc(S("x1_stored%d" % t), 16)
                        sp.dma_start(sum_t[bass.ds(q, 1), slot_of(t), :, :].rearrange("a p d -> p (a d)"),
                                     x1_sb[:, t, :]).then_inc(S("x1_stored%d" % t), 16)
                    q, t = tile_at(p, m, LAG_OUT + 1)
                    if live(q) and (not isinstance(q, int) or q + 1 < PAIRS):
                        wait(sp, "res_done", TILES, q, t + 1)
                        load_x(q + 1, t)
                    if m == 7 and live(p - 1):
                        wait(sp, "probs_done", 1, p - 1, 1)
                        sp.dma_start(rowp_t[bass.ds(p - 1, 1), :, :, :].rearrange("a p s e -> p (a s) e"),
                                     r_probs[:, :, :]).then_inc(S("probs_stored"), 16)

            for p in (-1, 0, 1):
                body(p)
            with sp.Fori(2, PAIRS - 2) as p:
                body(p)
            body(PAIRS - 2)
            for r in range(2):
                load_gu(0, r)
                load_dn(0, r)
            for p in (PAIRS - 1, PAIRS, PAIRS + 1):
                body(p)

            for r in range(2):
                wait(sp, "up_ps", 4, 0, 2 * r + 2)
                load_gu(1, r)
            with sp.Fori(1, E // 2 - 1) as g:
                for r in range(2):
                    wait(sp, "y_done", 4, g - 1, 2 * r + 2)
                    load_dn(g, r)
                    wait(sp, "up_ps", 4, g, 2 * r + 2)
                    load_gu(g + 1, r)
            for r in range(2):
                wait(sp, "y_done", 4, E // 2 - 2, 2 * r + 2)
                load_dn(E // 2 - 1, r)

            for r in range(2):
                wait(sp, "added%d" % r, 32, E // 2, 0)

            def load_sum(n, r):
                sp.dma_start(x_sb[:, FINAL * r:FINAL * (r + 1), :],
                             sum3[bass.ds(n, 1), :, :, :].rearrange("a p s d -> p (a s) d")
                             ).then_inc(S("sum_loaded%d" % r), 16)

            def store_out(g, r):
                wait(sp, "final_done", 2, g, r + 1)
                sp.dma_start(out3[bass.ds(g * 2 + r, 1), :, :, :].rearrange("a p s d -> p (a s) d"),
                             x1_sb[:, FINAL * r:FINAL * (r + 1), :]).then_inc(S("out_stored%d" % r), 16)

            for r in range(2):
                load_sum(r, r)
            with sp.Fori(0, ROUNDS3 // 2 - 1) as g:
                for r in range(2):
                    store_out(g, r)
                    load_sum(g * 2 + (r + 2), r)
            for r in range(2):
                store_out(ROUNDS3 // 2 - 1, r)
            for r in range(2):
                sp.wait_ge(S("out_stored%d" % r), 16 * (ROUNDS3 // 2))

        @block.tensor
        def _(pe):
            pe.wait_ge(S("w_fold_loaded"), 32)
            for k in range(KD):
                last = nc.tensor.matmul(bank[0][:, k * DC:(k + 1) * DC], w_kv_sb[:, k * P:(k + 1) * P],
                                        w_comp_sb[:, :], start=True, stop=True)
            last.then_inc(S("w_in_ps"), 1)
            pe.wait_ge(S("w_sum_done"), 1)
            nc.tensor.matmul(bank[1][:, :], w_c2l_sb[:, :], w_sum[:, :], start=True, stop=True
                             ).then_inc(S("w_out_ps"), 1)
            for k in range(KD):
                last = nc.tensor.matmul(bank[2][:, P * k:P * (k + 1)], w_sum[:, P * k:P * (k + 1)], w_c2l_sb[:, :],
                                        start=True, stop=True)
            last.then_inc(S("w_outT_ps"), 1)
            pe.wait_ge(S("const_loaded"), 16 * 9)
            pe.wait_ge(S("gate_loaded"), 32)
            for k in range(KD):
                last = nc.tensor.matmul(bank[3][:, 0:E], const_f[:, 3, :], gate_sb[:, k, :],
                                        start=(k == 0), stop=(k == KD - 1))
            last.then_inc(S("gate_sum_ps"), 1)
            pe.wait_ge(S("gate_centred"), 1)
            pe.wait_ge(S("w_outT_done"), 1)
            for k in range(KD):
                last = nc.tensor.matmul(bank[4][:, 0:E], w_outT[:, k, :], gate_sb[:, k, :],
                                        start=(k == 0), stop=(k == KD - 1))
            last.then_inc(S("w_out_gate_ps"), 1)
            for k in range(KD):
                last = nc.tensor.matmul(bank[5][:, 0:E], bias_rep[:, k, :], gate_sb[:, k, :],
                                        start=(k == 0), stop=(k == KD - 1))
            last.then_inc(S("bias_gate_ps"), 1)
            pe.wait_ge(S("w_in_done"), 1)
            pe.wait_ge(S("w_out_done"), 1)
            pe.wait_ge(S("folded"), 1)
            pe.wait_ge(S("const_done"), 5)

            def body(p):
                for m in range(TILES):
                    q, t = tile_at(p, m, LAG_PROBS)
                    if live(q):
                        wait(pe, "exp_done", TILES, q, t + 1)
                        wait(pe, "probsT_done", TILES, q, t)
                        for i in range(t // 2 + 1):
                            last = nc.tensor.transpose(bank[4][:, P * i:P * (i + 1)],
                                                       probs[:, t % 2, P * i:P * (i + 1)], ident[:, :])
                        last.then_inc(S("probsT_ps"), 1)
                    j, b = m // 2, m % 2
                    if live(p):
                        if m == 0:
                            wait(pe, "qk_ready", 2, p, 2)
                        wait(pe, "exp_done", TILES, p, m - 1)
                        s_ps = bank[2 + m % 2]
                        n = P * (j + 1)
                        part = slice(DC * b, DC * b + DC)
                        nc.tensor.matmul(s_ps[:, 0:n], qT[part, P * j:P * (j + 1)], kT[part, 0:n],
                                         start=True, stop=False)
                        nc.tensor.matmul(s_ps[:, P * j:n], ident_h[:, :], causal_h[:, :],
                                         start=False, stop=True).then_inc(S("scores_done"), 1)
                    q, t = tile_at(p, m, LAG_OUT)
                    if live(q):
                        part = slice(DC * (t % 2), DC * (t % 2) + DC)
                        wait(pe, "oT_done", TILES, q, t + 1)
                        wait(pe, "res_done", TILES, q, t)
                        nc.tensor.matmul(bank[6][:, :], oT[part, :], w_out[part, :],
                                         start=True, stop=True).then_inc(S("out_ps"), 1)
                        wait(pe, "logits_done", TILES, q, t)
                        nc.tensor.matmul(bank[5][:, 2 * P:2 * P + E], oT[part, :], w_out_gate[part, :],
                                         start=True, stop=True).then_inc(S("logits_ps"), 1)
                    q3 = p - 2
                    if m == 0 and live(q3):
                        wait(pe, "chosen_done", 1, q3, 1)
                        wait(pe, "earlier_done", 1, q3, 1)
                        wait(pe, "ids_done", 1, q3, 0)
                        pos = bank[7][:, :].rearrange("p (t e) -> p t e", e=E)
                        nc.tensor.matmul(pos, before_h[:, :], chosen[:, :, :], start=True, stop=False)
                        for s in range(TILES - 1):
                            n = TILES - 1 - s
                            nc.tensor.matmul(pos[:, s + 1:TILES, :], ones_h[:, :],
                                             chosen[:, s:s + 1, :].to_broadcast([P, n, E]),
                                             start=False, stop=False)
                        nc.tensor.matmul(pos, ones_h[:, :], earlier[:, None, :].to_broadcast([P, TILES, E]),
                                         start=False, stop=True).then_inc(S("pos_ps"), 1)
                    if 3 <= m <= 6 and live(q3):
                        c = m - 3
                        wait(pe, "hot_done", 4, q3, c + 1)
                        for i in range(2 * TOPK):
                            last = nc.tensor.matmul(bank[7][:, 0:BLOCKS], hot_place[:, c % 2, i // 2, :, i % 2],
                                                    hot_block[:, c % 2, i // 2, :, i % 2],
                                                    start=(c == 0 and i == 0), stop=(c == 3 and i == 2 * TOPK - 1))
                        last.then_inc(S("hot_used"), 1)
                    q1 = p + 1
                    if live(q1):
                        if m <= 2:
                            if m == 0:
                                wait(pe, "xT_loaded", 16, q1, 16)
                                wait(pe, "turned_done", 4, q1, 0)
                            for s in range(3 * m, min(3 * m + 3, TILES)):
                                if s == JT:
                                    wait(pe, "v_done", 1, q1, 0)
                                at = (s % JT) * (DC + E)
                                for k in range(KD):
                                    last = nc.tensor.matmul(bank[s // JT][:, at:at + DC + E],
                                                            xT_sb[:, k, P * s:P * (s + 1)], w_x[:, k, :],
                                                            start=(k == 0), stop=(k == KD - 1))
                                if s % JT == JT - 1:
                                    last.then_inc(S("compressed"), 1)
                        if m == 4:
                            wait(pe, "c_norm_done", 1, q1, 1)
                            wait(pe, "x_gate_read", 2, q1, 2)
                            for i in range(JT):
                                last = nc.tensor.transpose(bank[0][:, P * i:P * (i + 1)],
                                                           c_norm[:, 2 * i:2 * i + 2, :].rearrange("p t c -> p (t c)"),
                                                           ident[:, :])
                            last.then_inc(S("chT_ps"), 1)
                        if m == 5:
                            wait(pe, "chT_done", 1, q1, 1)
                            nc.tensor.matmul(bank[1][:, :], proj[:, 0, :], chT[:, :], start=True, stop=True
                                             ).then_inc(S("proj_ps"), 1)
                            nc.tensor.matmul(bank[0][:, :], proj[:, 1, :], chT[:, :], start=True, stop=True
                                             ).then_inc(S("proj_ps"), 1)
                        if m == 6:
                            wait(pe, "turned_done", 4, q1, 1)
                            nc.tensor.matmul(bank[1][:, :], proj[:, 2, :], chT[:, :], start=True, stop=True
                                             ).then_inc(S("proj_ps"), 1)
                            wait(pe, "turned_done", 4, q1, 2)
                            nc.tensor.matmul(bank[0][:, :], proj[:, 3, :], chT[:, :], start=True, stop=True
                                             ).then_inc(S("proj_ps"), 1)
                        if m == 7:
                            wait(pe, "turned_done", 4, q1, 3)
                            for i in range(JT):
                                last = nc.tensor.matmul(bank[1][:, P * i:P * (i + 1)], chT[:, P * i:P * (i + 1)],
                                                        proj[:, 4, :], start=True, stop=True)
                            last.then_inc(S("v_ps"), 1)
                    q, t = tile_at(p, m, LAG_PROBS)
                    if live(q):
                        if t == 0:
                            wait(pe, "v_done", 1, q, 1)
                        wait(pe, "probsT_done", TILES, q, t + 1)
                        wait(pe, "oT_done", TILES, q, t)
                        q5, t5 = tile_at(p, m, LAG_OUT)
                        if live(q5):
                            wait(pe, "logits_done", TILES, q5, t5 + 1)
                        for i in range(t // 2 + 1):
                            last = nc.tensor.matmul(bank[5][:, P * (t % 2):P * (t % 2 + 1)], v_sb[:, i, :],
                                                    probsT[:, t % 2, P * i:P * (i + 1)],
                                                    start=(i == 0), stop=(i == t // 2))
                        last.then_inc(S("o_ps"), 1)

            rounds(pe, body)

            def tokens_in(g, r):
                wait(pe, "gathered%d" % r, 32, g, 32)
                for i in range(2):
                    wait(pe, "xgT_done%d" % i, 2, g, r)
                    for kk in range(2):
                        for h in range(HALVES):
                            k = 2 * i + kk
                            at = CAP * kk + P * h
                            last = nc.tensor.transpose(bank[i][:, at:at + P],
                                                       xg[:, HALVES * r + h, P * k:P * (k + 1)], ident[:, :])
                    last.then_inc(S("xgT_ps"), 1)

            def up(g, r):
                wait(pe, "gu_loaded%d" % r, 16, g, 16)
                wait(pe, "xgT_done0", 2, g, r + 1)
                wait(pe, "xgT_done1", 2, g, r + 1)
                wait(pe, "h_done", 2, g, r)
                for u in range(2):
                    for f in range(KF):
                        for k in range(KD):
                            at = 2 * FF * k + FF * u + P * f
                            last = nc.tensor.matmul(bank[2 + u][:, CAP * f:CAP * (f + 1)],
                                                    w_gu[:, r, at:at + P], xgT[:, r, k, :],
                                                    start=(k == 0), stop=(k == KD - 1))
                    last.then_inc(S("up_ps"), 1)

            def down(g, r):
                wait(pe, "dn_loaded%d" % r, 16, g, 16)
                wait(pe, "h_done", 2, g, r + 1)
                for h in range(HALVES):
                    wait(pe, "y_read%d" % h, 2, g, r)
                    for f in range(KF):
                        last = nc.tensor.matmul(bank[4 + h][:, :], h_sb[:, r, CAP * f + P * h:CAP * f + P * (h + 1)],
                                                w_dn[:, r, D * f:D * (f + 1)], start=(f == 0), stop=(f == KF - 1))
                    last.then_inc(S("y_done"), 1)

            for r in range(2):
                tokens_in(0, r)
                up(0, r)
            def both(g):
                for r in range(2):
                    tokens_in(g, r)
                    down(g - 1, r)
                    up(g, r)

            both(1)
            with pe.Fori(2, E // 2) as g:
                both(g)
            for r in range(2):
                down(E // 2 - 1, r)

        @block.vector
        def _(dve):
            nc.vector.memset(proj[:, :, :], 0.0).then_inc(S("proj_zero"), 1)
            nc.vector.memset(zeros[:, :], 0.0).then_inc(S("zeros_ready"), 1)
            nc.vector.memset(earlier[:, :], 0.0).then_inc(S("earlier_done"), 1)
            nc.vector.memset(ids[:, :], 0.0)
            nc.vector.memset(pair_base[:, :], 0.0)
            nc.vector.memset(eps_add[:, :], EPS)
            nc.vector.memset(minus_one[:, :], -1.0)
            nc.vector.memset(eps_pow[:, :], -0.5).then_inc(S("started"), 1)
            dve.wait_ge(S("w_in_ps"), 1)
            w_in_ps = bank[0][:, 0:KD * DC].rearrange("p (k c) -> p k c", c=DC)
            nc.vector.reduce_sum(w_in_mean[:, :], w_in_ps, AX.X).then_inc(S("w_in_sum"), 1)
            dve.wait_ge(S("w_in_sum"), 1)
            for k in range(KD):
                last = nc.vector.tensor_scalar(w_in[:, k, :], w_in_mean[:, k:k + 1].to_broadcast([P, DC]), -1.0 / DC,
                                               None, ALU.mult)
            last.then_inc(S("w_in_shift"), 1)
            dve.wait_ge(S("w_in_shift"), 1)
            nc.vector.tensor_add(w_in[:, :, :], w_in[:, :, :], w_in_ps).then_inc(S("w_in_done"), 1)
            dve.wait_ge(S("w_fold2_loaded"), 32)
            nc.vector.tensor_add(w_sum[:, :], w_sum[:, :], w_kv_sb[:, :]).then_inc(S("w_sum_done"), 1)
            dve.wait_ge(S("w_out_ps"), 1)
            nc.vector.tensor_copy(w_out[:, :], bank[1][:, :]).then_inc(S("w_out_done"), 1)
            dve.wait_ge(S("w_outT_ps"), 1)
            nc.vector.tensor_copy(w_outT[:, :, :].rearrange("p k c -> p (k c)"), bank[2][:, :]).then_inc(S("w_outT_done"), 1)
            dve.wait_ge(S("gate_loaded"), 32)
            nc.vector.tensor_copy(bias_rep[:, :, :], bias_cols[:, :, None].to_broadcast([P, KD, P]))
            dve.wait_ge(S("gate_sum_ps"), 1)
            for k in range(KD):
                last = nc.vector.scalar_tensor_tensor(gate_sb[:, k, :], bank[3][:, 0:E], -1.0 / D, gate_sb[:, k, :],
                                                      ALU.mult, ALU.add)
            last.then_inc(S("gate_centred"), 1)
            dve.wait_ge(S("w_out_gate_ps"), 1)
            nc.vector.tensor_copy(w_out_gate[:, :], bank[4][:, 0:E])
            dve.wait_ge(S("bias_gate_ps"), 1)
            nc.vector.tensor_copy(bias_gate[:, :], bank[5][:, 0:E]).then_inc(S("folded"), 1)
            dve.wait_ge(S("const_loaded"), 16 * 9)
            for i, half in enumerate((ident_h, causal_h, before_h, ones_h)):
                nc.vector.tensor_copy(half[:, :], const_f[:, i, :]).then_inc(S("const_done"), 1)
            nc.vector.tensor_copy(ramp_h[:, :, :], const_f[:, 4, :, None].to_broadcast([P, P, 2])
                                  ).then_inc(S("const_done"), 1)

            def body(p):
                for m in range(TILES):
                    if live(p):
                        wait(dve, "scores_done", TILES, p, m + 1)
                        wait(dve, "exp_done", TILES, p, m - 7)
                        nc.vector.tensor_reduce(neg_max[:, m:m + 1], bank[2 + m % 2][:, 0:P * (m // 2 + 1)],
                                                AX.X, ALU.max, negate=True).then_inc(S("max_done"), 1)
                    q, t = tile_at(p, m, LAG_PROBS)
                    if live(q):
                        wait(dve, "exp_done", TILES, q, t + 1)
                        nc.vector.reciprocal(exp_inv[:, t:t + 1], exp_sum[:, t:t + 1]).then_inc(S("inv_done"), 1)
                    q, t = tile_at(p, m, LAG_OUT)
                    if live(q):
                        wait(dve, "out_ps", TILES, q, t + 1)
                        wait(dve, "xb_done", TILES, q, t + 1)
                        wait(dve, "x1_done", TILES, q, t - 3)
                        wait(dve, "inv_done", TILES, q, t + 1)
                        nc.vector.scalar_tensor_tensor(y_sb[:, t % 4, :], bank[6][:, :], exp_inv[:, t:t + 1],
                                                       x_sb[:, t, :], ALU.mult, ALU.add).then_inc(S("res_done"), 1)
                        wait(dve, "res_done", TILES, q, t + 1)
                        nc.vector.bn_stats(y_stats[:, t % 2, :], y_sb[:, t % 4, :]).then_inc(S("stats_done"), 1)
                        wait_apart(dve, ("stats_done", TILES, q, t + 1))
                        nc.vector.bn_aggr(y_mv[:, t, :], y_stats[:, t % 2, :]).then_inc(S("mv_done"), 1)
                    q1 = p + 1
                    if live(q1):
                        if m == 3:
                            wait(dve, "c_sq_done", 2, q1, 2)
                            nc.vector.reduce_sum(c_ssq[:, :], c_sq[:, :, :], AX.X).then_inc(S("c_ssq_done"), 1)
                            wait(dve, "c_ssq_done", 1, q1, 1)
                            wait(dve, "c_rstd_done", 1, q1, 0)
                            nc.vector.tensor_scalar(c_var[:, :], c_ssq[:, :], 1.0 / DC, EPS, ALU.mult, ALU.add
                                                    ).then_inc(S("c_var_done"), 1)
                        if m in (5, 6):
                            for i in (2 * (m - 5), 2 * (m - 5) + 1):
                                wait(dve, "proj_ps", 4, q1, i + 1)
                                wait(dve, "qk_ready", 2, q1, 0)
                                nc.vector.tensor_mul(turned[:, i, :], bank[1 - i % 2][:, :], rope_sb[:, i, :]
                                                     ).then_inc(S("turned_done"), 1)
                    q3 = p - 2
                    if live(q3):
                        if m == 0:
                            wait(dve, "pos_ps", 1, q3, 1)
                            wait(dve, "slot_done", 1, q3, 0)
                            pos = bank[7][:, :].rearrange("p (t e) -> p t e", e=E)
                            flat = "p t e -> p (t e)"
                            nc.vector.scalar_tensor_tensor(fits[:, :, :].rearrange(flat), bank[7][:, :], float(CAP),
                                                           chosen[:, :, :].rearrange(flat), ALU.is_lt, ALU.mult)
                            nc.vector.tensor_add(slot_at[:, :, :], pos, slot_base[:, :, :]).then_inc(S("slot_sum"), 1)
                            nc.vector.reduce_sum(c_choice[:, :], chosen[:, :, :].rearrange("p t e -> p e t"), AX.X
                                                 ).then_inc(S("choice_sum"), 1)
                            wait(dve, "choice_sum", 1, q3, 1)
                            nc.vector.tensor_add(earlier[:, :], earlier[:, :], c_choice[:, :]).then_inc(S("earlier_done"), 1)
                        if m == 1:
                            wait_apart(dve, ("slot_done", 1, q3, 1))
                            for s in range(TILES):
                                last = nc.vector.max(slot8[:, s, :], slot[:, s, :])
                            last.then_inc(S("slot8_done"), 1)
                            wait(dve, "slot8_done", 1, q3, 1)
                            nc.vector.tensor_scalar(slot_i[:, :, :], slot8[:, :, :], -1.0, None, ALU.add
                                                    ).then_inc(S("slot_i_done"), 1)
                            wait(dve, "slot_i_done", 1, q3, 1)
                            nc.vector.tensor_scalar(block_i[:, :, :], slot_i[:, :, :], 7, None, ALU.arith_shift_right)
                            nc.vector.tensor_scalar(place_i[:, :, :], slot_i[:, :, :], P - 1, None, ALU.bitwise_and
                                                    ).then_inc(S("split_done"), 1)
                            wait(dve, "split_done", 1, q3, 1)
                            nc.vector.tensor_copy(block_h[:, :, :], block_i[:, :, :])
                            nc.vector.tensor_copy(place_h[:, :, :], place_i[:, :, :]).then_inc(S("split_f_done"), 1)
                        if 2 <= m <= 5:
                            c = m - 2
                            if c == 0:
                                wait(dve, "split_f_done", 1, q3, 1)
                            if c >= 2:
                                wait(dve, "hot_used", 4, q3, c - 1)
                            ramp = ramp_h[:, None, :, :].to_broadcast([P, TOPK, P, 2])
                            for hot, number in ((hot_place, place_h), (hot_block, block_h)):
                                by_two = number[:, 2 * c:2 * c + 2, :].rearrange("p s (h w) -> p (s h) w", w=2)
                                last = nc.vector.tensor_tensor(hot[:, c % 2, :, :, :], ramp,
                                                               by_two[:, :, None, :].to_broadcast([P, TOPK, P, 2]),
                                                               ALU.is_equal)
                            last.then_inc(S("hot_ones"), 1)
                        if m == 7:
                            wait(dve, "hot_used", 4, q3, 4)
                            nc.vector.scalar_tensor_tensor(id_part[:, :], bank[7][:, 0:BLOCKS], 0.0,
                                                           pair_base[:, 0:1].to_broadcast([P, BLOCKS]),
                                                           ALU.is_gt, ALU.mult)
                            nc.vector.tensor_add(ids_t[:, :], ids[:, :], bank[7][:, 0:BLOCKS]).then_inc(S("id_part_done"), 1)
                            wait(dve, "id_part_done", 1, q3, 1)
                            nc.vector.tensor_scalar_add(pair_base[:, :], pair_base[:, :], float(TILES * P))
                            nc.vector.tensor_add(ids[:, :], ids_t[:, :], id_part[:, :]).then_inc(S("ids_done"), 1)
                    if m == 3 and live(q1):
                        wait(dve, "c_rstd_done", 1, q1, 1)
                        wait(dve, "x_gate_read", 2, q1, 2)
                        wait(dve, "chT_ps", 1, q1, 0)
                        for b in range(2):
                            last = nc.vector.tensor_mul(of_seq(c_norm, b), wide(b)[:, :, 0:DC],
                                                        of_seq(c_rstd, b)[:, :, None].to_broadcast([P, JT, DC]))
                        last.then_inc(S("c_norm_done"), 1)
                    q3 = p - 1
                    if live(q3):
                        if m == 4:
                            wait(dve, "logits_scaled", 1, q3, 1)
                            nc.vector.reduce_max(l_max[:, :], logits[:, :, :], AX.X).then_inc(S("l_max_done"), 1)
                            wait(dve, "l_max_done", 1, q3, 1)
                            wait(dve, "l_exp_done", 1, q3, 0)
                            nc.vector.tensor_sub(l_cen[:, :, :], logits[:, :, :],
                                                 l_max[:, :, None].to_broadcast([P, TILES, E])).then_inc(S("l_cen_done"), 1)
                            wait(dve, "l_cen_done", 1, q3, 1)
                            nc.vector.tensor_scalar_max(l_cen[:, :, :], l_cen[:, :, :], LOG_TINY).then_inc(S("l_ready"), 1)
                        if m == 6:
                            wait(dve, "l_exp_done", 1, q3, 1)
                            nc.vector.reduce_sum(l_sum[:, :], l_exp[:, :, :], AX.X).then_inc(S("l_sum_done"), 1)
                            wait(dve, "l_sum_done", 1, q3, 1)
                            wait(dve, "probs_done", 1, q3, 0)
                            nc.vector.reciprocal(l_inv[:, :], l_sum[:, :]).then_inc(S("l_inv_done"), 1)
                            for s in range(TILES):
                                last = nc.vector.max(top8[:, s, :], l_cen[:, s, :])
                            last.then_inc(S("top8_done"), 1)
                        if m == 7:
                            if isinstance(q3, int) and q3 == 0:
                                dve.wait_ge(S("dummy_stored"), 16 * 3 * (DUMMY // P))
                            wait_apart(dve, ("top8_done", 1, q3, 1))
                            for s in range(TILES):
                                last = nc.vector.match_replace(l_left[:, s, :], top8[:, s, :], l_cen[:, s, :], TAKEN)
                            last.then_inc(S("l_left_done"), 1)
                            wait(dve, "l_left_done", 1, q3, 1)
                            wait(dve, "pos_ps", 1, q3, 0)
                            nc.vector.tensor_scalar(chosen[:, :, :], l_left[:, :, :], 0.5 * TAKEN, None, ALU.is_lt
                                                    ).then_inc(S("chosen_done"), 1)
                            wait(dve, "chosen_done", 1, q3, 1)

            dve.wait_ge(S("route_loaded"), 48)
            rounds(dve, body)

            dve.wait_ge(S("ids_done"), PAIRS)
            nc.vector.tensor_scalar(id_part[:, :], ids[:, :], 0.0, None, ALU.is_equal).then_inc(S("rows_step"), 1)
            dve.wait_ge(S("rows_step"), 1)
            nc.vector.tensor_mul(id_part[:, :], id_part[:, :], empty_row[:, :]).then_inc(S("rows_step"), 1)
            dve.wait_ge(S("rows_step"), 2)
            nc.vector.tensor_add(ids_t[:, :], ids[:, :], id_part[:, :]).then_inc(S("rows_step"), 1)
            dve.wait_ge(S("rows_step"), 3)
            nc.vector.tensor_scalar(rows_u[:, :], ids_t[:, :], -1.0, None, ALU.add).then_inc(S("rows_step"), 1)
            dve.wait_ge(S("rows_step"), 4)

            def list_of(g, r):
                return rows_u[:, bass.ds(g * (2 * HALVES) + HALVES * r, HALVES)]

            def list_get(g, r):
                wait(dve, "gathered%d" % r, 32, g, 0)
                nc.vector.tensor_copy(rows_get[:, HALVES * r:HALVES * (r + 1)], list_of(g, r)
                                      ).then_inc(S("rows_ready"), 1)

            def evac(g, r):
                wait(dve, "xgT_ps", 4, g, 2 * r + 2)
                wait(dve, "up_ps", 4, g, 2 * r - 2)
                nc.vector.tensor_copy(xgT[:, r, 2:4, :].rearrange("p k c -> p (k c)"), bank[1][:, :]
                                      ).then_inc(S("xgT_done1"), 1)

            def weights_in(g, r):
                wait(dve, "gathered%d" % r, 32, g, 32)
                wait(dve, "w_slot_done", 2, g, r - 1)
                nc.vector.tensor_copy(w_new[:, HALVES * r:HALVES * (r + 1)],
                                      xg[:, HALVES * r:HALVES * (r + 1), bass.ds(g * 2 + (D + r), 1)
                                         ].rearrange("p h a -> p (h a)")).then_inc(S("w_new_done"), 1)

            def weigh(g, r):
                wait(dve, "y_read0", 2, g, r - 1)
                wait(dve, "y_read1", 2, g, r - 1)
                wait(dve, "w_new_done", 2, g, r + 1)
                nc.vector.tensor_copy(w_slot[:, HALVES * r:HALVES * (r + 1)], w_new[:, HALVES * r:HALVES * (r + 1)]
                                      ).then_inc(S("w_slot_done"), 1)

            def product(g, r):
                wait(dve, "gate_done", 2, g, r + 1)
                wait(dve, "up_ps", 4, g, 2 * r + 2)
                wait(dve, "y_done", 4, g, 2 * r - 2)
                nc.vector.tensor_mul(h_sb[:, r, :], gate_act, bank[3][:, :]).then_inc(S("h_done"), 1)

            def scale(g, r):
                wait(dve, "added%d" % r, 32, g, 0)
                nc.vector.tensor_copy(rows_put[:, HALVES * r:HALVES * (r + 1)], list_of(g, r))
                wait(dve, "y_done", 4, g, 2 * r + 2)
                wait(dve, "w_slot_done", 2, g, r + 1)
                nc.vector.tensor_scalar(ye[:, HALVES * r + 1, :], bank[5][:, :],
                                        w_slot[:, HALVES * r + 1:HALVES * r + 2], None, ALU.mult
                                        ).then_inc(S("y_read1"), 1)

            for r in range(2):
                list_get(0, r)
            for r in range(2):
                weights_in(0, r)
                list_get(1, r)
                evac(0, r)
                weigh(0, r)
                product(0, r)

            def both(g, last=False):
                for r in range(2):
                    weights_in(g, r)
                    if not last:
                        list_get(g + 1, r)
                    evac(g, r)
                    scale(g - 1, r)
                    weigh(g, r)
                    product(g, r)

            both(1)
            with dve.Fori(2, E // 2 - 1) as g:
                both(g)
            both(E // 2 - 1, last=True)
            for r in range(2):
                scale(E // 2 - 1, r)

            def final(g):
                for r in range(2):
                    buf = x_sb[:, FINAL * r:FINAL * (r + 1), :]
                    wait(dve, "sum_loaded%d" % r, 16, g, 16)
                    wait(dve, "out_stored%d" % r, 16, g, 0)
                    for s in range(FINAL):
                        last = nc.vector.bn_stats(f_stats[:, s, :], buf[:, s, :])
                    last.then_inc(S("f_stats_done"), 1)
                    wait_apart(dve, ("f_stats_done", 2, g, r + 1))
                    for s in range(FINAL):
                        last = nc.vector.bn_aggr(f_mv[:, s, :], f_stats[:, s, :])
                    last.then_inc(S("f_mv_done"), 1)
                    wait(dve, "f_rstd_done", 2, g, r + 1)
                    for s in range(FINAL):
                        last = nc.vector.tensor_scalar(x1_sb[:, FINAL * r + s, :], buf[:, s, :], f_mv[:, s, 0:1],
                                                f_rstd[:, s:s + 1], ALU.subtract, ALU.mult)
                    last.then_inc(S("final_done"), 1)

            final(0)
            with dve.Fori(1, ROUNDS3 // 2) as g:
                final(g)

        @block.scalar
        def _(act):
            def body(p):
                for m in range(TILES):
                    q, t = tile_at(p, m, LAG_PROBS)
                    if live(q):
                        wait(act, "probsT_ps", TILES, q, t + 1)
                        wait(act, "o_ps", TILES, q, t - 1)
                        n = P * (t // 2 + 1)
                        nc.scalar.copy(probsT[:, t % 2, 0:n], bank[4][:, 0:n]).then_inc(S("probsT_done"), 1)
                    if live(p):
                        wait(act, "max_done", TILES, p, m + 1)
                        wait(act, "probsT_ps", TILES, p, m - 1)
                        wait(act, "inv_done", TILES, p, m - 7)
                        n = P * (m // 2 + 1)
                        nc.scalar.activation(probs[:, m % 2, 0:n], bank[2 + m % 2][:, 0:n], ACT.Exp,
                                             bias=neg_max[:, m:m + 1], accum_out=exp_sum[:, m:m + 1]
                                             ).then_inc(S("exp_done"), 1)
                    q, t = tile_at(p, m, LAG_OUT)
                    if live(q):
                        wait(act, "logits_ps", TILES, q, t + 1)
                        wait(act, "inv_done", TILES, q, t + 1)
                        wait(act, "l_raw_done", 1, q, 0)
                        nc.scalar.activation(o_gate[:, slot_of(t), :], bank[5][:, 2 * P:2 * P + E], ACT.Copy,
                                             scale=exp_inv[:, t:t + 1]).then_inc(S("logits_done"), 1)
                    q, t = tile_at(p, m, LAG_X1)
                    if live(q):
                        wait(act, "shift_done", TILES, q, t + 1)
                        wait(act, "x1_stored%d" % t, 32, q, 0)
                        nc.scalar.activation(x1_sb[:, t, :], y_sb[:, t % 4, :], ACT.Identity,
                                             bias=y_shift[:, slot_of(t):slot_of(t) + 1],
                                             scale=y_rstd[:, slot_of(t):slot_of(t) + 1]).then_inc(S("x1_done"), 1)
                    if 2 <= m <= 5 and live(p - 2):
                        c = m - 2
                        wait(act, "hot_ones", 4, p - 2, c + 1)
                        for s in (2 * c, 2 * c + 1):
                            at = (s % 2) * (TOPK // 2)
                            part = hot_block[:, c % 2, at:at + TOPK // 2, :, :].rearrange("p h n w -> p (h n w)")
                            last = nc.scalar.activation(part, part, ACT.Copy, scale=local_id[:, s:s + 1])
                        last.then_inc(S("hot_done"), 1)
                    q, t = tile_at(p, m, LAG_PROBS)
                    if live(q):
                        wait(act, "o_ps", TILES, q, t + 1)
                        wait(act, "logits_ps", TILES, q, t - 1)
                        part = slice(DC * (t % 2), DC * (t % 2) + DC)
                        nc.scalar.copy(oT[part, :], bank[5][part, P * (t % 2):P * (t % 2 + 1)]
                                       ).then_inc(S("oT_done"), 1)
                    if m == 0 and live(p):
                        wait(act, "v_ps", 1, p, 1)
                        wait(act, "o_ps", TILES, p, 0)
                        nc.scalar.copy(v_sb[:, :, :].rearrange("p j c -> p (j c)"), bank[1][:, :]
                                       ).then_inc(S("v_done"), 1)
                    if m in (1, 2) and live(p + 1):
                        wait(act, "compressed", 2, p + 1, m)
                        wait(act, "c_ssq_done", 1, p + 1, 0)
                        nc.scalar.activation(of_seq(c_sq, m - 1), wide(m - 1)[:, :, 0:DC], ACT.Square
                                             ).then_inc(S("c_sq_done"), 1)
                    if m == 2 and live(p + 1):
                        wait(act, "compressed", 2, p + 1, 2)
                        wait(act, "x_gate_done", 1, p + 1, 0)
                        for b in range(2):
                            nc.scalar.copy(x_gate_in[:, JT * b:JT * (b + 1), :], wide(b)[:, :, DC:DC + E]
                                           ).then_inc(S("x_gate_read"), 1)
                    if m == 4 and live(p + 1):
                        wait(act, "chT_ps", 1, p + 1, 1)
                        wait(act, "v_ps", 1, p + 1, 0)
                        nc.scalar.activation(chT[:, :], bank[0][:, :], ACT.Identity, bias=beta_sb[:, :],
                                             scale=gamma_sb[:, :]).then_inc(S("chT_done"), 1)
                    if m == 4 and live(p - 1):
                        wait(act, "l_ready", 1, p - 1, 1)
                        wait(act, "probs_done", 1, p - 1, 0)
                        nc.scalar.activation(l_exp[:, :, :], l_cen[:, :, :], ACT.Exp).then_inc(S("l_exp_done"), 1)

            act.wait_ge(S("const_loaded"), 16 * 9)
            rounds(act, body)

            def evac(g, r):
                wait(act, "xgT_ps", 4, g, 2 * r + 1)
                wait(act, "up_ps", 4, g, 2 * r - 2)
                nc.scalar.copy(xgT[:, r, 0:2, :].rearrange("p k c -> p (k c)"), bank[0][:, :]
                               ).then_inc(S("xgT_done0"), 1)

            def gate(g, r):
                wait(act, "up_ps", 4, g, 2 * r + 1)
                wait(act, "h_done", 2, g, r)
                nc.scalar.activation(gate_act, bank[2][:, :], ACT.Silu).then_inc(S("gate_done"), 1)

            def scale(g, r):
                wait(act, "y_done", 4, g, 2 * r + 1)
                wait(act, "w_slot_done", 2, g, r + 1)
                wait(act, "added%d" % r, 32, g, 0)
                nc.scalar.activation(ye[:, HALVES * r, :], bank[4][:, :], ACT.Copy,
                                     scale=w_slot[:, HALVES * r:HALVES * r + 1]).then_inc(S("y_read0"), 1)

            for r in range(2):
                evac(0, r)
                gate(0, r)
            def both(g):
                for r in range(2):
                    evac(g, r)
                    scale(g - 1, r)
                    gate(g, r)

            both(1)
            with act.Fori(2, E // 2) as g:
                both(g)
            for r in range(2):
                scale(E // 2 - 1, r)

        @block.gpsimd
        def _(pool):
            pool.wait_ge(S("bias_loaded"), 16)
            pool.wait_ge(S("started"), 1)
            pool.wait_ge(S("folded"), 1)
            nc.gpsimd.memset(scrap_p[:, :], 0.0).then_inc(S("scrap_written"), 1)

            def body(p):
                for m in range(TILES):
                    if live(p):
                        wait(pool, "x_loaded%d" % m, 16, p, 16)
                        nc.gpsimd.tensor_tensor(x_sb[:, m, :], x_sb[:, m, :], bias_sb[:, :], ALU.add
                                                ).then_inc(S("xb_done"), 1)
                    if m == 0 and live(p - 2):
                        wait(pool, "slot_sum", 1, p - 2, 1)
                        wait(pool, "slot8_done", 1, p - 2, 0)
                        nc.gpsimd.tensor_tensor(slot[:, :, :], slot_at[:, :, :], fits[:, :, :], ALU.mult
                                                ).then_inc(S("slot_done"), 1)
                    if m == 2:
                        if live(p - 1):
                            wait(pool, "logits_done", TILES, p - 1, TILES)
                            wait(pool, "logits_scaled", 1, p - 1, 0)
                            nc.gpsimd.tensor_tensor(l_raw[:, :, :], o_gate[:, :, :], x_gate[:, :, :], ALU.add
                                                    ).then_inc(S("l_raw_done"), 1)
                        if live(p):
                            wait(pool, "x_gate_read", 2, p, 2)
                            wait(pool, "l_raw_done", 1, p, 0)
                            nc.gpsimd.tensor_tensor(x_gate[:, :, :], x_gate_in[:, :, :],
                                                    bias_gate[:, None, :].to_broadcast([P, TILES, E]), ALU.add
                                                    ).then_inc(S("x_gate_done"), 1)
                        if live(p - 1):
                            wait(pool, "l_raw_done", 1, p - 1, 1)
                            wait(pool, "l_cen_done", 1, p - 1, 0)
                            nc.gpsimd.tensor_tensor(logits[:, :, :], l_raw[:, :, :],
                                                    y_rstd[:, :, None].to_broadcast([P, TILES, E]), ALU.mult
                                                    ).then_inc(S("logits_scaled"), 1)
                    if m == 7 and live(p + 1):
                        wait(pool, "scores_done", TILES, p, TILES)
                        wait(pool, "turned_done", 4, p + 1, 4)
                        nc.gpsimd.tensor_tensor(qT[:, :], turned[:, 0, :], turned[:, 1, :], ALU.add
                                                ).then_inc(S("qk_ready"), 1)
                        nc.gpsimd.tensor_tensor(kT[:, :], turned[:, 2, :], turned[:, 3, :], ALU.add
                                                ).then_inc(S("qk_ready"), 1)
                    q, t = tile_at(p, m, LAG_OUT)
                    if live(q):
                        at = slot_of(t)
                        wait(pool, "mv_done", TILES, q, t + 1)
                        wait(pool, "shift_done", TILES, q, t - 1)
                        nc.gpsimd.tensor_tensor(y_var[:, t % 2:t % 2 + 1], y_mv[:, t, 1:2], eps_add[:, 0:1], ALU.add)
                        nc.gpsimd.tensor_tensor(y_negmean[:, t % 2:t % 2 + 1], y_mv[:, t, 0:1], minus_one[:, :], ALU.mult
                                                ).then_inc(S("y_var_done"), 1)
                        wait(pool, "y_var_done", TILES, q, t + 1)
                        wait(pool, "x1_done", TILES, q, t - 7)
                        wait(pool, "logits_scaled", 1, q, 0)
                        nc.gpsimd.tensor_tensor(y_rstd[:, at:at + 1], y_var[:, t % 2:t % 2 + 1], eps_pow[:, 0:1], ALU.pow
                                                ).then_inc(S("rstd_done"), 1)
                        wait(pool, "rstd_done", TILES, q, t + 1)
                        nc.gpsimd.tensor_tensor(y_shift[:, at:at + 1], y_negmean[:, t % 2:t % 2 + 1],
                                                y_rstd[:, at:at + 1], ALU.mult).then_inc(S("shift_done"), 1)
                    if m == 3 and live(p + 1):
                        wait(pool, "c_var_done", 1, p + 1, 1)
                        wait(pool, "c_norm_done", 1, p + 1, 0)
                        nc.gpsimd.tensor_tensor(c_rstd[:, :], c_var[:, :], eps_pow[:, :], ALU.pow
                                                ).then_inc(S("c_rstd_done"), 1)
                    if m == 6 and live(p - 1):
                        wait(pool, "l_inv_done", 1, p - 1, 1)
                        wait(pool, "probs_stored", 16, p - 1, 0)
                        nc.gpsimd.tensor_tensor(r_probs[:, :, :], l_exp[:, :, :],
                                                l_inv[:, :, None].to_broadcast([P, TILES, E]), ALU.mult
                                                ).then_inc(S("probs_done"), 1)

            rounds(pool, body)

            def gather(g, r):
                if not isinstance(g, int):
                    wait(pool, "scrap_written", 4, g - 3, 1)
                wait_apart(pool, ("rows_ready", 2, g, r + 1), ("xgT_ps", 4, g, 2 * r - 2),
                           ("w_new_done", 2, g, r - 1))
                for h in range(HALVES):
                    nc.gpsimd.indirect_dma_start(
                        xg[:, HALVES * r + h, :], None, table[:, :],
                        bass.IndirectOffsetOnAxis(rows_get[:, HALVES * r + h:HALVES * r + h + 1], 0),
                        bounds_check=TOKENS + DUMMY - 1).then_inc(S("gathered%d" % r), 16)

            def scatter(g, r):
                wait_apart(pool, ("added%d" % (1 - r), 32, g, 32 * r), ("y_read0", 2, g, r + 1),
                           ("y_read1", 2, g, r + 1))
                for h in range(HALVES):
                    nc.gpsimd.indirect_dma_start(
                        total[:, :],
                        bass.IndirectOffsetOnAxis(rows_put[:, HALVES * r + h:HALVES * r + h + 1], 0),
                        ye[:, HALVES * r + h, :], None,
                        bounds_check=TOKENS + DUMMY - 1, compute_op=ALU.add).then_inc(S("added%d" % r), 16)

            pool.wait_ge(S("dummy_stored"), 16 * 3 * (DUMMY // P))
            pool.wait_ge(S("probs_stored"), 16 * PAIRS)
            for m in range(TILES):
                pool.wait_ge(S("x1_stored%d" % m), 32 * PAIRS)
            for g in range(2):
                for r in range(2):
                    gather(g, r)

            def both(g):
                for r in range(2):
                    gather(g + 1, r)
                    scatter(g - 1, r)

            both(1)
            with pool.Fori(2, E // 2 - 1) as g:
                both(g)
            for g in (E // 2 - 2, E // 2 - 1):
                for r in range(2):
                    scatter(g, r)

            with pool.Fori(0, ROUNDS3 // 2) as g:
                for r in range(2):
                    wait(pool, "f_mv_done", 2, g, r + 1)
                    nc.gpsimd.tensor_tensor(f_var[:, :], f_mv[:, :, 1], eps_add[:, 0:FINAL], ALU.add).then_inc(S("f_var_done"), 1)
                    pool.wait_ge(S("f_var_done"), g * 2 + (r + 1))
                    nc.gpsimd.tensor_tensor(f_rstd[:, :], f_var[:, :], eps_pow[:, 0:FINAL], ALU.pow
                                            ).then_inc(S("f_rstd_done"), 1)


def constants():
    import numpy as np
    f = np.float32
    inv = (f(1.0) / f(10000.0) ** (np.arange(0, DC, 2, dtype=f) / f(DC))).astype(f)
    angle = np.arange(SEQ, dtype=f)[:, None] * inv[None, :]
    cos, sin = np.cos(angle).astype(f).T, np.sin(angle).astype(f).T
    cos, sin = np.concatenate([cos, cos]), np.concatenate([-sin, sin])
    scale = f(DC ** -0.5)
    rope = np.stack([np.concatenate([a, a]) for a in (cos * scale, sin * scale, cos, sin)]).astype(f)
    i = np.arange(P)
    const = np.zeros((11, P, P), f)
    const[0] = np.eye(P)
    const[1] = np.where(i[None, :] <= i[:, None], 0.0, TAKEN)
    const[2] = i[:, None] < i[None, :]
    const[3] = 1.0
    const[4] = i[None, :]
    const[5] = TOKENS + 1 + P * (i[None, :] % HALVES) + i[:, None]
    const[6:10] = np.tile(np.arange(E) * CAP + 1, TILES).reshape(4, 1, P)
    const[10, :, 0:TILES] = P * np.arange(TILES)[None, :] + i[:, None] + 1
    return rope, const


def kernel(**inputs):
    import numpy as np
    import concourse.bacc as bacc
    from concourse.bass_utils import run_bass_kernel_spmd

    a = {k.replace("L0_attn_", "").replace("L0_ffn_", ""): np.asarray(v) for k, v in inputs.items()}
    rope, const = constants()
    x = a["x"].reshape(TOKENS, D)
    half = np.r_[DC // 2:DC, 0:DC // 2]
    q, k, v = a["W_q_comp"], a["W_kv_comp"][:DC], a["W_kv_comp"][DC:]
    gu = np.concatenate([a["w_gate"].reshape(E, KD, P, FF), a["w_up"].reshape(E, KD, P, FF)], axis=3)
    gu = gu.transpose(0, 2, 1, 3).reshape(E, P, KD * 2 * FF)
    dn = a["w_down"].reshape(E, KF, P, D).transpose(0, 2, 1, 3).reshape(E, P, KF * D)
    arrays = {
        "xT": x.reshape(PAIRS, TILES * P, KD, P).transpose(0, 3, 2, 1).reshape(PAIRS, P, KD * TILES * P),
        "x": x,
        "w_kv": a["W_to_kv"],
        "w_compT": a["W_compress"].T,
        "gamma": a["ln_gamma"][:, None],
        "beta": a["ln_beta"][:, None],
        "w_proj": np.stack([q.T, q[half].T, k.T, k[half].T, v.T]),
        "w_c2l": np.concatenate([a["W_comp2lat"]] * 2, axis=1),
        "w_resT": a["W_out_res"].T,
        "bias": a["b_out_res"][None, :],
        "bias_col": a["b_out_res"].reshape(KD, P).T,
        "gateT": a["gate_w"].T,
        "w_experts": np.concatenate([gu, dn], axis=2),
        "rope": rope,
        "const": const,
    }
    arrays = {n: np.ascontiguousarray(v) for n, v in arrays.items()}
    nc = bacc.Bacc("TRN2", target_bir_lowering=False, num_devices=1)
    args = [nc.dram_tensor(n, v.shape, mybir.dt.from_np(v.dtype), kind="ExternalInput").ap() for n, v in arrays.items()]
    args.append(nc.dram_tensor("out", (TOKENS, D), F32, kind="ExternalOutput").ap())
    attention_router_moe(nc, *args)
    r = run_bass_kernel_spmd(nc, [arrays], core_ids=[0])
    return r.results[0]["out"].reshape(SEQS, SEQ, D)
```

```python
from contextlib import ExitStack

import concourse.bass as bass
from concourse import mybir

F32 = mybir.dt.float32
F32R = mybir.dt.float32r
BF16 = mybir.dt.bfloat16
F16 = mybir.dt.float16
I32 = mybir.dt.int32
U32 = mybir.dt.uint32
ALU = mybir.AluOpType
ACT = mybir.ActivationFunctionType
AX = mybir.AxisListType

P = 128
SEQS, SEQ, D = 16, 512, 512
TOKENS = SEQS * SEQ
LAT, DC = 128, 64
E, TOPK, CAP, FF = 64, 8, 256, 256
KD = D // P
KF = FF // P
JT = SEQ // P
PAIRS = SEQS // 2
TILES = 2 * JT
HALVES = CAP // P
BLOCKS = E * HALVES
ROW = D + E
DUMMY = CAP
FINAL = 2
RING = TILES * 2 // FINAL
AHEAD = 6
ROUNDS3 = TOKENS // (FINAL * P)
EPS = 1e-5
LOG_TINY = -104.0
TAKEN = -1e30

LAG_PROBS = 1
LAG_OUT = 2
LAG_RES = 3
LAG_VAR = 4
LAG_X1 = 5


def attention_router_moe(nc, xT, x, w_kv, w_compT, gamma, beta, w_proj, w_c2l, w_resT, bias, bias_col, gateT,
                         w_experts, rope, const, out):
    table = nc.dram_tensor("token_table", [TOKENS + DUMMY, ROW], F32, kind="Internal").ap()
    total = nc.dram_tensor("running_sum", [TOKENS + DUMMY, D], F32, kind="Internal").ap()
    ctx = ExitStack()
    alone = ExitStack()
    sems = {}
    places = []

    def sb(name, shape, dt=F32):
        return ctx.enter_context(nc.sbuf_tensor(name, shape, dt))

    def sb1(name, shape, dt=F32):
        return alone.enter_context(nc.sbuf_tensor(name, shape, dt))

    def S(name):
        return sems[name]

    def wait(eng, name, per, q, k):
        value = q * per + k
        if isinstance(value, int) and value <= 0:
            return
        eng.wait_ge(S(name), value)

    def wait_apart(eng, *waits):
        for name, per, q, k in waits:
            wait(eng, name, per, q, k)
        if not all(isinstance(q, int) for _, _, q, _ in waits):
            n = len(places)
            places.append(waits[0][0])
            if eng.engine == nc.vector.engine:
                nc.vector.memset(scrap_v[:, n:n + 1], 0.0)
            else:
                nc.gpsimd.tensor_tensor(scrap_p[:, n:n + 1], eps_pow[:, 0:1], eps_pow[:, 0:1], ALU.add
                                        ).then_inc(S("scrap_written"), 1)

    def tile_at(p, m, lag):
        d = m - lag
        return p + d // TILES, d % TILES

    def live(q):
        return not isinstance(q, int) or 0 <= q < PAIRS

    with ctx:
        rope_sb = sb("rope_sb", [P, 4, SEQ])
        ident = sb("ident", [P, P])
        ident_h = sb("ident_h", [P, P], BF16)
        causal_h = sb("causal_h", [P, P], BF16)
        before_h = sb("before_h", [P, P], BF16)
        ones_h = sb("ones_h", [P, P], BF16)
        ramp_h = sb("ramp_h", [P, P, 2], F16)
        const_f = sb("const_f", [P, 5, P])
        local_id = sb("local_id", [P, TILES])
        slot_base = sb("slot_base", [P, TILES, E])
        empty_row = sb("empty_row", [P, P])
        eps_pow = sb("eps_pow", [P, TILES])
        eps_add = sb("eps_add", [P, TILES])
        scrap_v = sb("scrap_v", [P, 64])
        scrap_p = sb("scrap_p", [P, 64])
        bias_sb = sb("bias_sb", [P, D])
        gamma_sb = sb("gamma_sb", [P, 1])
        beta_sb = sb("beta_sb", [P, 1])
        proj = sb("proj", [P, 5, P])
        w_comp_sb = sb("w_comp_sb", [LAT, DC])
        w_c2l_sb = sb("w_c2l_sb", [LAT, 2 * DC])
        w_x = sb("w_x", [P, KD, DC + E])
        w_in, gate_sb = w_x[:, :, 0:DC], w_x[:, :, DC:DC + E]
        w_out_hi = sb("w_out_hi", [P, D], F32R)
        w_out_lo = sb("w_out_lo", [P, D], F32R)
        w_out_gate_hi = sb("w_out_gate_hi", [P, E], F32R)
        w_out_gate_lo = sb("w_out_gate_lo", [P, E], F32R)
        w_in_mean = sb("w_in_mean", [P, KD])
        bias_cols = sb("bias_cols", [P, KD])
        bias_gate = sb("bias_gate", [P, E])
        minus_one = sb("minus_one", [P, FINAL])
        inv_d = sb("inv_d", [P, 1])
        neg_inv_d = sb("neg_inv_d", [P, 1])
        x_sb = sb("x_sb", [P, TILES, D])
        x1_sb = sb("x1_sb", [P, TILES, D])
        w_kv_sb, w_sum = x1_sb[:, 0, :], x1_sb[:, 1, :]
        w_outT = x1_sb[:, 2, :].rearrange("p (k c) -> p k c", c=P)
        bias_rep = x1_sb[:, 3, :].rearrange("p (k c) -> p k c", c=P)
        id_part = sb("id_part", [P, BLOCKS])
        ids = sb("ids", [P, BLOCKS])
        ids_t = sb("ids_t", [P, BLOCKS])
        rows_u = sb("rows_u", [P, BLOCKS], U32)
        W_GU, W_DN = KD * 2 * FF, KF * D
        w_gu = sb("w_gu", [P, 2, W_GU])
        w_dn = sb("w_dn", [P, 2, W_DN])
        rows_get = sb("rows_get", [P, 2 * HALVES], U32)
        rows_put = sb("rows_put", [P, 2 * HALVES], U32)
        xg = sb("xg", [P, 2 * HALVES, ROW])
        gate_act = x_sb[:, 0, :]
        h_sb = x_sb[:, 1, :]
        ye = x_sb[:, 3:3 + 2 * HALVES, :]
        w_new = sb("w_new", [P, 2 * HALVES])
        w_slot = sb("w_slot", [P, 2 * HALVES])
        f_stats = sb("f_stats", [P, FINAL, 6])
        f_mv = sb("f_mv", [P, 2, FINAL, 2])
        f_var = sb("f_var", [P, FINAL])
        f_negmean = sb("f_negmean", [P, FINAL])
        f_rstd = sb("f_rstd", [P, 2, FINAL])
        f_shift = sb("f_shift", [P, 2, FINAL])
        xT_sb = sb1("xT_sb", [P, KD, TILES * P])
        c_sq = sb1("c_sq", [P, TILES, DC])
        c_ssq = sb1("c_ssq", [P, TILES])
        c_var = sb1("c_var", [P, TILES])
        c_rstd = sb1("c_rstd", [P, TILES])
        c_norm = sb1("c_norm", [P, TILES, DC])
        chT = sb1("chT", [P, SEQ])
        turned = sb1("turned", [P, 4, SEQ])
        qT = sb1("qT", [P, SEQ])
        kT = sb1("kT", [P, SEQ])
        v_sb = sb1("v_sb", [P, 2, JT, 2, DC])
        neg_max = sb1("neg_max", [P, TILES])
        exp_sum = sb1("exp_sum", [P, TILES])
        exp_inv = sb1("exp_inv", [P, TILES])
        probs = sb1("probs", [P, 2, SEQ])
        probsT = sb1("probsT", [P, 2, SEQ])
        oT = sb1("oT", [P, 2, P], F32R)
        o_full = sb1("o_full", [P, 2, P])
        y_sb = sb1("y_sb", [P, 4, D])
        y_sum = sb1("y_sum", [P, TILES])
        y_ssq = sb1("y_ssq", [P, TILES])
        y_meansq = sb1("y_meansq", [P, 2])
        y_var = sb1("y_var", [P, 2])
        y_negmean = sb1("y_negmean", [P, 2])
        y_rstd = sb1("y_rstd", [P, TILES])
        y_shift = sb1("y_shift", [P, TILES])
        x_gate_in = sb1("x_gate_in", [P, TILES, E])
        x_gate = sb1("x_gate", [P, TILES, E])
        o_gate = sb1("o_gate", [P, TILES, E])
        l_raw = sb1("l_raw", [P, TILES, E])
        logits = sb1("logits", [P, TILES, E])
        l_max = sb1("l_max", [P, TILES])
        l_cen = sb1("l_cen", [P, TILES, E])
        l_exp = sb1("l_exp", [P, TILES, E])
        l_sum = sb1("l_sum", [P, TILES])
        l_inv = sb1("l_inv", [P, TILES])
        r_probs = sb1("r_probs", [P, TILES, E])
        top8 = sb1("top8", [P, TILES, TOPK])
        l_left = sb1("l_left", [P, TILES, E])
        chosen = sb1("chosen", [P, TILES, E], BF16)
        earlier = sb1("earlier", [P, E], BF16)
        c_choice = sb1("c_choice", [P, E])
        fits = sb1("fits", [P, TILES, E])
        slot_at = sb1("slot_at", [P, TILES, E])
        slot = sb1("slot", [P, TILES, E])
        slot8 = sb1("slot8", [P, TILES, TOPK])
        slot_i = sb1("slot_i", [P, TILES, TOPK], I32)
        block_i = sb1("block_i", [P, TILES, TOPK], I32)
        place_i = sb1("place_i", [P, TILES, TOPK], I32)
        block_h = sb1("block_h", [P, TILES, TOPK], F16)
        place_h = sb1("place_h", [P, TILES, TOPK], F16)
        hot_place = sb1("hot_place", [P, 3, TOPK, P, 2], F16)
        hot_block = sb1("hot_block", [P, 3, TOPK, P, 2], F16)
        pair_base = sb1("pair_base", [P, 1])
        zeros = l_left[:, :, :].rearrange("p t e -> p (t e)")
        alone.close()
        gu_hi = sb("gu_hi", [P, 2, W_GU], F32R)
        gu_lo = sb("gu_lo", [P, 2, W_GU], F32R)
        dn_hi = sb("dn_hi", [P, 2, W_DN], F32R)
        dn_lo = sb("dn_lo", [P, 2, W_DN], F32R)
        xgT_hi = sb("xgT_hi", [P, 2, KD, CAP], F32R)
        xgT_lo = sb("xgT_lo", [P, 2, KD, CAP], F32R)
        h_hi = sb("h_hi", [P, 2, KF * CAP], F32R)
        h_lo = sb("h_lo", [P, 2, KF * CAP], F32R)
        bank = [ctx.enter_context(nc.psum_tensor(f"bank{i}", [P, 512], F32)) for i in range(8)]

        for name in (
            "added0", "added1", "bias_gate_ps", "bias_loaded", "c_norm_done", "c_rstd_done",
            "c_sq_done", "c_ssq_done", "c_var_done", "chT_done", "chT_ps", "choice_sum",
            "chosen_done", "compressed", "const_done", "const_loaded", "dn_hi_done", "dn_lo_done",
            "dn_loaded0", "dn_loaded1", "dummy_stored", "earlier_done", "exp_done", "f_mv_done",
            "f_rstd_done", "f_shift_done", "f_stats_done", "f_var_done", "final_done", "fold_step",
            "folded", "gate_centred", "gate_done", "gate_loaded", "gate_sum_ps", "gathered0",
            "gathered1", "gu_hi_done", "gu_lo_done", "gu_loaded0", "gu_loaded1", "h_done",
            "h_hi_done", "h_lo_done", "hot_blocks", "hot_done", "hot_places", "hot_used",
            "id_part_done", "ids_done", "inv_done", "l_cen_done", "l_exp_done", "l_inv_done",
            "l_left_done", "l_max_done", "l_raw_done", "l_ready", "l_sum_done", "logits_done",
            "logits_ps", "logits_scaled", "max_done", "mean_done", "meansq_done", "oT_done", "o_ps",
            "o_read", "ones_loaded", "out_ps", "pos_ps", "probsT_done", "probsT_ps", "probs_done",
            "probs_stored", "proj_ps", "proj_zero", "qk_ready", "res_done", "route_loaded",
            "rows_ready", "rows_step", "rstd_done", "scores_done", "scrap_written", "shift_done",
            "slot8_done", "slot_done", "slot_i_done", "slot_sum", "split_done", "split_f_done",
            "ssq_done", "started", "top8_done", "turned_done", "up_ps", "v_done", "v_ps",
            "w_fold2_loaded", "w_fold_loaded", "w_in_done", "w_in_ps", "w_new_done", "w_outT_done",
            "w_outT_ps", "w_out_done", "w_out_gate_ps", "w_out_ps", "w_slot_done", "w_sum_done",
            "x1_done", "xT_loaded", "x_gate_done", "x_gate_read", "xb_done", "xgT_ps", "xg_hi_done",
            "xg_lo_done", "y_done", "y_read0", "y_read1", "y_var_done", "zeros_ready",
        ):
            sems[name] = ctx.enter_context(nc.semaphore(name))
        for m in range(TILES):
            for name in ("x_loaded%d" % m, "x1_stored%d" % m):
                sems[name] = ctx.enter_context(nc.semaphore(name))
        for i in range(RING):
            for name in ("sum_loaded%d" % i, "out_stored%d" % i):
                sems[name] = ctx.enter_context(nc.semaphore(name))
        block = ctx.enter_context(nc.Block())

        def slot_of(m):
            return (m % 2) * JT + m // 2

        def wide(b):
            return bank[b][:, :].rearrange("p (j w) -> p j w", w=DC + E)

        def of_seq(tensor, b):
            if len(tensor.shape) == 2:
                return tensor[:, :].rearrange("p (j two) -> p j two", two=2)[:, :, b]
            return tensor[:, :, :].rearrange("p (j two) c -> p j two c", two=2)[:, :, b, :]

        def rounds(eng, body):
            for p in (-1, 0, 1, 2):
                body(p)
            with eng.Fori(3, PAIRS - 2) as p:
                body(p)
            for p in (PAIRS - 2, PAIRS - 1, PAIRS, PAIRS + 1):
                body(p)

        CONST_LOADS = 8
        LAST = E // 2 - 1

        def after(g, r, n=1):
            return g + (r + n) // 2, (r + n) % 2

        def exists(g):
            return not isinstance(g, int) or 0 <= g <= LAST

        def experts(eng, body):
            body(0)
            body(1)
            with eng.Fori(2, LAST - 1) as g:
                body(g)
            body(LAST - 1)
            body(LAST)

        def final_buf(i):
            at = FINAL * i
            return (x_sb, x1_sb)[at // TILES][:, at % TILES:at % TILES + FINAL, :]

        def final_rounds(eng, body):
            body(0)
            with eng.Fori(1, ROUNDS3 // RING - 1) as g:
                body(g)
            body(ROUNDS3 // RING - 1)

        x_t = x.rearrange("(q s p) d -> q s p d", s=TILES, p=P)
        xT_t = xT.rearrange("q p n -> q p n")
        row_t = table[0:TOKENS, :].rearrange("(q s p) d -> q s p d", s=TILES, p=P)
        rowp_t = table[0:TOKENS, D:ROW].rearrange("(q s p) d -> q p s d", s=TILES, p=P)
        sum_t = total[0:TOKENS, :].rearrange("(q s p) d -> q s p d", s=TILES, p=P)
        sum3 = total[0:TOKENS, :].rearrange("(r s p) d -> r p s d", s=FINAL, p=P)
        out3 = out.rearrange("(r s p) d -> r p s d", s=FINAL, p=P)

        @block.sync
        def _(sp):
            def load_x(q, m):
                sp.dma_start(x_sb[:, m, :], x_t[bass.ds(q, 1), slot_of(m), :, :].rearrange("a p d -> p (a d)")
                             ).then_inc(S("x_loaded%d" % m), 16)

            def load_xT(q):
                sp.dma_start(xT_sb[:, :, :].rearrange("p k n -> p (k n)"),
                             xT_t[bass.ds(q, 1), :, :].rearrange("a p n -> p (a n)")
                             ).then_inc(S("xT_loaded"), 16)

            def load_gu(g, r):
                sp.dma_start(w_gu[:, r, :], w_experts[bass.ds(g * 2 + r, 1), :, 0:W_GU].rearrange("a p n -> p (a n)")
                             ).then_inc(S("gu_loaded%d" % r), 16)

            def load_dn(g, r):
                sp.dma_start(w_dn[:, r, :], w_experts[bass.ds(g * 2 + r, 1), :, W_GU:W_GU + W_DN
                                                      ].rearrange("a p n -> p (a n)")
                                                                              ).then_inc(S("dn_loaded%d" % r), 16)

            sp.dma_start(w_kv_sb[:, :], w_kv).then_inc(S("w_fold_loaded"), 16)
            sp.dma_start(w_comp_sb[:, :], w_compT).then_inc(S("w_fold_loaded"), 16)
            sp.dma_start(gate_sb[:, :, :], gateT.rearrange("(k p) e -> p k e", p=P)).then_inc(S("gate_loaded"), 16)
            sp.dma_start(bias_cols[:, :], bias_col).then_inc(S("gate_loaded"), 16)
            sp.dma_start(const_f[:, :, :], const[0:5, :, :].rearrange("c p n -> p c n")).then_inc(S("ones_loaded"), 16)
            sp.dma_start(w_sum[:, :], w_resT).then_inc(S("w_fold2_loaded"), 16)
            sp.dma_start(w_c2l_sb[:, :], w_c2l).then_inc(S("w_fold2_loaded"), 16)
            load_xT(0)
            sp.dma_start(ident[:, :], const[0, :, :]).then_inc(S("const_loaded"), 16)
            sp.wait_ge(S("proj_zero"), 1)
            for b in range(2):
                part = slice(DC * b, DC * b + DC)
                sp.dma_start(proj[part, :, part], w_proj.rearrange("c p n -> p c n")).then_inc(S("const_loaded"), 16)
                sp.dma_start(gamma_sb[part, :], gamma).then_inc(S("const_loaded"), 16)
                sp.dma_start(beta_sb[part, :], beta).then_inc(S("const_loaded"), 16)
            sp.dma_start(rope_sb[:, :, :], rope.rearrange("c p n -> p c n")).then_inc(S("const_loaded"), 16)
            sp.dma_start(bias_sb[:, :], bias[0:1, :].to_broadcast([P, D])).then_inc(S("bias_loaded"), 16)
            for m in range(TILES):
                load_x(0, m)
            sp.dma_start(empty_row[:, :], const[5, :, :]).then_inc(S("route_loaded"), 16)
            sp.dma_start(slot_base[:, :, :].rearrange("p t e -> p (t e)"),
                         const[6:10, :, :].rearrange("c p n -> p c n")).then_inc(S("route_loaded"), 16)
            sp.dma_start(local_id[:, :], const[10, :, 0:TILES]).then_inc(S("route_loaded"), 16)
            sp.wait_ge(S("zeros_ready"), 1)
            for h in range(DUMMY // P):
                rows = slice(TOKENS + h * P, TOKENS + (h + 1) * P)
                sp.dma_start(table[rows, 0:D], zeros[:, :]).then_inc(S("dummy_stored"), 16)
                sp.dma_start(table[rows, D:ROW], zeros[:, 0:E]).then_inc(S("dummy_stored"), 16)
                sp.dma_start(total[rows, :], zeros[:, :]).then_inc(S("dummy_stored"), 16)

            def body(p):
                for m in range(TILES):
                    if m == 3 and live(p + 2) and (not isinstance(p, int) or p + 2 >= 1):
                        if not isinstance(p, int) or p + 2 < PAIRS:
                            wait(sp, "compressed", 2, p + 1, 2)
                            load_xT(p + 2)
                    q, t = tile_at(p, m, LAG_X1)
                    if live(q):
                        wait(sp, "x1_done", TILES, q, t + 1)
                        sp.dma_start(row_t[bass.ds(q, 1), slot_of(t), :, 0:D].rearrange("a p d -> p (a d)"),
                                     x1_sb[:, t, :]).then_inc(S("x1_stored%d" % t), 16)
                        sp.dma_start(sum_t[bass.ds(q, 1), slot_of(t), :, :].rearrange("a p d -> p (a d)"),
                                     x1_sb[:, t, :]).then_inc(S("x1_stored%d" % t), 16)
                    q, t = tile_at(p, m, LAG_RES + 1)
                    if live(q) and (not isinstance(q, int) or q + 1 < PAIRS):
                        wait(sp, "res_done", TILES, q, t + 1)
                        load_x(q + 1, t)
                    if m == 7 and live(p - 1):
                        wait(sp, "probs_done", 1, p - 1, 1)
                        sp.dma_start(rowp_t[bass.ds(p - 1, 1), :, :, :].rearrange("a p s e -> p (a s) e"),
                                     r_probs[:, :, :]).then_inc(S("probs_stored"), 16)

            for p in (-1, 0, 1):
                body(p)
            with sp.Fori(2, PAIRS - 2) as p:
                body(p)
            body(PAIRS - 2)
            for r in range(2):
                load_gu(0, r)
                load_dn(0, r)
            for p in (PAIRS - 1, PAIRS, PAIRS + 1):
                body(p)

            def next_gu(g, r):
                if exists(g):
                    wait(sp, "gu_hi_done", 2, g, r - 1)
                    wait(sp, "gu_lo_done", 2, g, r - 1)
                    load_gu(g, r)

            def pair(g):
                for r in range(2):
                    next_gu(*after(g, r, 3))
                    if exists(g + 1):
                        wait(sp, "dn_hi_done", 2, g, r + 1)
                        wait(sp, "dn_lo_done", 2, g, r + 1)
                        load_dn(g + 1, r)

            next_gu(1, 0)
            experts(sp, pair)

            for r in range(2):
                wait(sp, "added%d" % r, 32, E // 2, 0)

            def load_sum(g, i):
                wait(sp, "out_stored%d" % i, 16, g, 0)
                sp.dma_start(final_buf(i), sum3[bass.ds(g * RING + i, 1), :, :, :].rearrange("a p s d -> p (a s) d")
                             ).then_inc(S("sum_loaded%d" % i), 16)

            def store_out(g, i):
                wait(sp, "final_done", RING, g, i + 1)
                sp.dma_start(out3[bass.ds(g * RING + i, 1), :, :, :].rearrange("a p s d -> p (a s) d"),
                             final_buf(i)).then_inc(S("out_stored%d" % i), 16)

            def final(g):
                for i in range(RING):
                    store_out(g, i)
                    if not (isinstance(g, int) and g * RING + i + AHEAD >= ROUNDS3):
                        load_sum(g + (i + AHEAD) // RING, (i + AHEAD) % RING)

            for i in range(AHEAD):
                load_sum(0, i)
            final_rounds(sp, final)
            for i in range(RING):
                sp.wait_ge(S("out_stored%d" % i), 16 * (ROUNDS3 // RING))

        @block.tensor
        def _(pe):
            pe.wait_ge(S("w_fold_loaded"), 32)
            for k in range(KD):
                last = nc.tensor.matmul(bank[0][:, k * DC:(k + 1) * DC], w_kv_sb[:, k * P:(k + 1) * P],
                                        w_comp_sb[:, :], start=True, stop=True)
            last.then_inc(S("w_in_ps"), 1)
            pe.wait_ge(S("ones_loaded"), 16)
            pe.wait_ge(S("gate_loaded"), 32)
            for k in range(KD):
                last = nc.tensor.matmul(bank[3][:, 0:E], const_f[:, 3, :], gate_sb[:, k, :],
                                        start=(k == 0), stop=(k == KD - 1))
            last.then_inc(S("gate_sum_ps"), 1)
            pe.wait_ge(S("w_sum_done"), 1)
            nc.tensor.matmul(bank[1][:, :], w_c2l_sb[:, :], w_sum[:, :], start=True, stop=True
                             ).then_inc(S("w_out_ps"), 1)
            for k in range(KD):
                last = nc.tensor.matmul(bank[2][:, P * k:P * (k + 1)], w_sum[:, P * k:P * (k + 1)], w_c2l_sb[:, :],
                                        start=True, stop=True)
            last.then_inc(S("w_outT_ps"), 1)
            pe.wait_ge(S("gate_centred"), 1)
            pe.wait_ge(S("w_outT_done"), 1)
            for k in range(KD):
                last = nc.tensor.matmul(bank[4][:, 0:E], w_outT[:, k, :], gate_sb[:, k, :],
                                        start=(k == 0), stop=(k == KD - 1))
            last.then_inc(S("w_out_gate_ps"), 1)
            for k in range(KD):
                last = nc.tensor.matmul(bank[5][:, 0:E], bias_rep[:, k, :], gate_sb[:, k, :],
                                        start=(k == 0), stop=(k == KD - 1))
            last.then_inc(S("bias_gate_ps"), 1)
            pe.wait_ge(S("w_in_done"), 1)
            pe.wait_ge(S("w_out_done"), 1)
            pe.wait_ge(S("folded"), 1)
            pe.wait_ge(S("const_loaded"), 16 * CONST_LOADS)
            pe.wait_ge(S("const_done"), 5)

            def body(p):
                for m in range(TILES):
                    q, t = tile_at(p, m, LAG_PROBS)
                    if live(q):
                        wait(pe, "exp_done", TILES, q, t + 1)
                        wait(pe, "probsT_done", TILES, q, t)
                        for i in range(t // 2 + 1):
                            last = nc.tensor.transpose(bank[4][:, P * i:P * (i + 1)],
                                                       probs[:, t % 2, P * i:P * (i + 1)], ident[:, :])
                        last.then_inc(S("probsT_ps"), 1)
                    j, b = m // 2, m % 2
                    if live(p):
                        if m == 0:
                            wait(pe, "qk_ready", 2, p, 2)
                        wait(pe, "exp_done", TILES, p, m - 1)
                        s_ps = bank[2 + m % 2]
                        n = P * (j + 1)
                        part = slice(DC * b, DC * b + DC)
                        nc.tensor.matmul(s_ps[:, 0:n], qT[part, P * j:P * (j + 1)], kT[part, 0:n],
                                         start=True, stop=False)
                        nc.tensor.matmul(s_ps[:, P * j:n], ident_h[:, :], causal_h[:, :],
                                         start=False, stop=True).then_inc(S("scores_done"), 1)
                    q3 = p - 2
                    if m == 0 and live(q3):
                        wait(pe, "chosen_done", 1, q3, 1)
                        wait(pe, "earlier_done", 1, q3, 1)
                        wait(pe, "ids_done", 1, q3, 0)
                        pos = bank[7][:, :].rearrange("p (t e) -> p t e", e=E)
                        nc.tensor.matmul(pos, before_h[:, :], chosen[:, :, :], start=True, stop=False)
                        for s in range(TILES - 1):
                            n = TILES - 1 - s
                            nc.tensor.matmul(pos[:, s + 1:TILES, :], ones_h[:, :],
                                             chosen[:, s:s + 1, :].to_broadcast([P, n, E]),
                                             start=False, stop=False)
                        nc.tensor.matmul(pos, ones_h[:, :], earlier[:, None, :].to_broadcast([P, TILES, E]),
                                         start=False, stop=True).then_inc(S("pos_ps"), 1)
                    if m >= 4 and live(q3):
                        c = m - 4
                        wait(pe, "hot_places", 4, q3, c + 1)
                        wait(pe, "hot_done", 4, q3, c + 1)
                        for i in range(2 * TOPK):
                            last = nc.tensor.matmul(bank[7][:, 0:BLOCKS], hot_place[:, c % 3, i // 2, :, i % 2],
                                                    hot_block[:, c % 3, i // 2, :, i % 2],
                                                    start=(c == 0 and i == 0), stop=(c == 3 and i == 2 * TOPK - 1))
                        last.then_inc(S("hot_used"), 1)
                    q1 = p + 1
                    if live(q1):
                        if m == 4:
                            wait(pe, "c_norm_done", 1, q1, 1)
                            wait(pe, "x_gate_read", 2, q1, 2)
                            for i in range(JT):
                                last = nc.tensor.transpose(bank[0][:, P * i:P * (i + 1)],
                                                           c_norm[:, 2 * i:2 * i + 2, :].rearrange("p t c -> p (t c)"),
                                                           ident[:, :])
                            last.then_inc(S("chT_ps"), 1)
                        if m == 5:
                            wait(pe, "chT_done", 1, q1, 1)
                            nc.tensor.matmul(bank[1][:, :], proj[:, 0, :], chT[:, :], start=True, stop=True
                                             ).then_inc(S("proj_ps"), 1)
                            nc.tensor.matmul(bank[0][:, :], proj[:, 1, :], chT[:, :], start=True, stop=True
                                             ).then_inc(S("proj_ps"), 1)
                        if m == 6:
                            wait(pe, "turned_done", 4, q1, 1)
                            nc.tensor.matmul(bank[1][:, :], proj[:, 2, :], chT[:, :], start=True, stop=True
                                             ).then_inc(S("proj_ps"), 1)
                            wait(pe, "turned_done", 4, q1, 2)
                            nc.tensor.matmul(bank[0][:, :], proj[:, 3, :], chT[:, :], start=True, stop=True
                                             ).then_inc(S("proj_ps"), 1)
                        if m == 7:
                            wait(pe, "turned_done", 4, q1, 3)
                            for i in range(JT):
                                last = nc.tensor.matmul(bank[1][:, P * i:P * (i + 1)], chT[:, P * i:P * (i + 1)],
                                                        proj[:, 4, :], start=True, stop=True)
                            last.then_inc(S("v_ps"), 1)
                    qx, tiles = (p + 2, (0, 1)) if m == 7 else (q1, (2 * m + 2, 2 * m + 3))
                    if m == 0 and isinstance(p, int) and p == -1:
                        tiles = (0, 1, 2, 3)
                    if (m <= 2 or m == 7) and live(qx):
                        for s in tiles:
                            if s == 0:
                                wait(pe, "xT_loaded", 16, qx, 16)
                                wait(pe, "turned_done", 4, qx, 0)
                            if s == JT:
                                wait(pe, "v_done", 1, qx, 0)
                            at = (s % JT) * (DC + E)
                            for k in range(KD):
                                last = nc.tensor.matmul(bank[s // JT][:, at:at + DC + E],
                                                        xT_sb[:, k, P * s:P * (s + 1)], w_x[:, k, :],
                                                        start=(k == 0), stop=(k == KD - 1))
                            if s % JT == JT - 1:
                                last.then_inc(S("compressed"), 1)
                    q, t = tile_at(p, m, LAG_OUT)
                    if live(q):
                        wait(pe, "oT_done", TILES, q, t + 1)
                        wait(pe, "res_done", TILES, q, t)
                        nc.tensor.matmul(bank[6][:, :], oT[:, t % 2, :], w_out_hi[:, :], start=True, stop=False)
                        nc.tensor.matmul(bank[6][:, :], oT[0:DC, t % 2, :], w_out_lo[0:DC, :],
                                         start=False, stop=True).then_inc(S("out_ps"), 1)
                    q5, t5 = tile_at(p, m, LAG_RES)
                    if live(q5):
                        wait(pe, "logits_done", TILES, q5, t5 + 1)
                    if live(q):
                        nc.tensor.matmul(bank[5][:, 2 * P:2 * P + E], oT[:, t % 2, :], w_out_gate_hi[:, :],
                                         start=True, stop=False)
                        nc.tensor.matmul(bank[5][:, 2 * P:2 * P + E], oT[0:DC, t % 2, :], w_out_gate_lo[0:DC, :],
                                         start=False, stop=True).then_inc(S("logits_ps"), 1)
                    q, t = tile_at(p, m, LAG_PROBS)
                    if live(q):
                        if t == 0:
                            wait(pe, "v_done", 1, q, 1)
                        wait(pe, "probsT_done", TILES, q, t + 1)
                        wait(pe, "o_read", TILES, q, t)
                        for i in range(t // 2 + 1):
                            last = nc.tensor.matmul(bank[5][:, P * (t % 2):P * (t % 2 + 1)],
                                                    v_sb[:, t % 2, i, :, :].rearrange("p w c -> p (w c)"),
                                                    probsT[:, t % 2, P * i:P * (i + 1)],
                                                    start=(i == 0), stop=(i == t // 2))
                        last.then_inc(S("o_ps"), 1)

            rounds(pe, body)

            def tokens_in(g, r):
                wait(pe, "gathered%d" % r, 32, g, 32)
                for i in range(2):
                    wait(pe, "xg_lo_done", 4, g, 2 * r + i - 1)
                    for kk in range(2):
                        for h in range(HALVES):
                            k = 2 * i + kk
                            at = CAP * kk + P * h
                            last = nc.tensor.transpose(bank[i][:, at:at + P],
                                                       xg[:, HALVES * r + h, P * k:P * (k + 1)], ident[:, :])
                    last.then_inc(S("xgT_ps"), 1)

            def up(g, r):
                wait(pe, "gu_hi_done", 2, g, r + 1)
                wait(pe, "gu_lo_done", 2, g, r + 1)
                wait(pe, "xg_lo_done", 4, g, 2 * r + 2)
                wait(pe, "h_done", 2, g, r - 1)
                for u in range(2):
                    for f in range(KF):
                        for k in range(KD):
                            at = 2 * FF * k + FF * u + P * f
                            for i, (w, t) in enumerate(((gu_hi, xgT_lo), (gu_lo, xgT_hi), (gu_hi, xgT_hi))):
                                last = nc.tensor.matmul(bank[2 + 4 * r + u][:, CAP * f:CAP * (f + 1)],
                                                        w[:, r, at:at + P], t[:, r, k, :],
                                                        start=(k == 0 and i == 0), stop=(k == KD - 1 and i == 2))
                    last.then_inc(S("up_ps"), 1)

            def down(g, r):
                wait(pe, "dn_hi_done", 2, g, r + 1)
                wait(pe, "dn_lo_done", 2, g, r + 1)
                wait(pe, "h_lo_done", 2, g, r + 1)
                for h in range(HALVES):
                    wait(pe, "y_read%d" % h, 2, g, r)
                    for f in range(KF):
                        at = CAP * f + P * h
                        for i, (t, w) in enumerate(((h_lo, dn_hi), (h_hi, dn_lo), (h_hi, dn_hi))):
                            last = nc.tensor.matmul(bank[4 + h][:, :], t[:, r, at:at + P],
                                                    w[:, r, D * f:D * (f + 1)],
                                                    start=(f == 0 and i == 0), stop=(f == KF - 1 and i == 2))
                    last.then_inc(S("y_done"), 1)

            tokens_in(0, 0)

            def pair(g):
                for r in range(2):
                    if exists(after(g, r)[0]):
                        tokens_in(*after(g, r))
                    if exists(g - 1):
                        down(g - 1, r)
                    up(g, r)

            experts(pe, pair)
            for r in range(2):
                down(LAST, r)

        @block.vector
        def _(dve):
            nc.vector.memset(proj[:, :, :], 0.0).then_inc(S("proj_zero"), 1)
            nc.vector.memset(zeros[:, :], 0.0).then_inc(S("zeros_ready"), 1)
            nc.vector.memset(earlier[:, :], 0.0).then_inc(S("earlier_done"), 1)
            nc.vector.memset(ids[:, :], 0.0)
            nc.vector.memset(pair_base[:, :], 0.0)
            nc.vector.memset(eps_add[:, :], EPS)
            nc.vector.memset(minus_one[:, :], -1.0)
            nc.vector.memset(inv_d[:, :], 1.0 / D)
            nc.vector.memset(neg_inv_d[:, :], -1.0 / D)
            nc.vector.memset(eps_pow[:, :], -0.5).then_inc(S("started"), 1)
            dve.wait_ge(S("w_in_ps"), 1)
            w_in_ps = bank[0][:, 0:KD * DC].rearrange("p (k c) -> p k c", c=DC)
            nc.vector.reduce_sum(w_in_mean[:, :], w_in_ps, AX.X).then_inc(S("fold_step"), 1)
            dve.wait_ge(S("fold_step"), 1)
            for k in range(KD):
                last = nc.vector.tensor_scalar(w_in[:, k, :], w_in_mean[:, k:k + 1].to_broadcast([P, DC]), -1.0 / DC,
                                               None, ALU.mult)
            last.then_inc(S("fold_step"), 1)
            dve.wait_ge(S("fold_step"), 2)
            nc.vector.tensor_add(w_in[:, :, :], w_in[:, :, :], w_in_ps).then_inc(S("w_in_done"), 1)
            dve.wait_ge(S("gate_loaded"), 32)
            nc.vector.tensor_copy(bias_rep[:, :, :], bias_cols[:, :, None].to_broadcast([P, KD, P]))
            dve.wait_ge(S("gate_sum_ps"), 1)
            for k in range(KD):
                last = nc.vector.scalar_tensor_tensor(gate_sb[:, k, :], bank[3][:, 0:E], -1.0 / D, gate_sb[:, k, :],
                                                      ALU.mult, ALU.add)
            last.then_inc(S("gate_centred"), 1)
            dve.wait_ge(S("w_fold2_loaded"), 32)
            nc.vector.tensor_add(w_sum[:, :], w_sum[:, :], w_kv_sb[:, :]).then_inc(S("w_sum_done"), 1)
            dve.wait_ge(S("w_out_ps"), 1)
            nc.vector.tensor_copy(w_out_hi[:, :], bank[1][:, :]).then_inc(S("fold_step"), 1)
            dve.wait_ge(S("fold_step"), 3)
            nc.vector.tensor_sub(w_out_lo[:, :], bank[1][:, :], w_out_hi[:, :].bitcast(F32)
                                    ).then_inc(S("w_out_done"), 1)
            dve.wait_ge(S("w_outT_ps"), 1)
            nc.vector.tensor_copy(w_outT[:, :, :].rearrange("p k c -> p (k c)"), bank[2][:, :]
                                    ).then_inc(S("w_outT_done"), 1)
            dve.wait_ge(S("w_out_gate_ps"), 1)
            nc.vector.tensor_copy(w_out_gate_hi[:, :], bank[4][:, 0:E]).then_inc(S("fold_step"), 1)
            dve.wait_ge(S("fold_step"), 4)
            nc.vector.tensor_sub(w_out_gate_lo[:, :], bank[4][:, 0:E], w_out_gate_hi[:, :].bitcast(F32))
            dve.wait_ge(S("bias_gate_ps"), 1)
            nc.vector.tensor_copy(bias_gate[:, :], bank[5][:, 0:E]).then_inc(S("folded"), 1)
            dve.wait_ge(S("ones_loaded"), 16)
            for i, half in enumerate((ident_h, causal_h, before_h, ones_h)):
                nc.vector.tensor_copy(half[:, :], const_f[:, i, :]).then_inc(S("const_done"), 1)
            nc.vector.tensor_copy(ramp_h[:, :, :], const_f[:, 4, :, None].to_broadcast([P, P, 2])
                                  ).then_inc(S("const_done"), 1)

            def body(p):
                for m in range(TILES):
                    if live(p):
                        wait(dve, "scores_done", TILES, p, m + 1)
                        wait(dve, "exp_done", TILES, p, m - 7)
                        nc.vector.tensor_reduce(neg_max[:, m:m + 1], bank[2 + m % 2][:, 0:P * (m // 2 + 1)],
                                                AX.X, ALU.max, negate=True).then_inc(S("max_done"), 1)
                    q, t = tile_at(p, m, LAG_PROBS)
                    if live(q):
                        wait(dve, "exp_done", TILES, q, t + 1)
                        nc.vector.reciprocal(exp_inv[:, t:t + 1], exp_sum[:, t:t + 1]).then_inc(S("inv_done"), 1)
                    q, t = tile_at(p, m, LAG_OUT)
                    if live(q):
                        wait(dve, "o_read", TILES, q, t + 1)
                        low = oT[DC:P, t % 2, :]
                        nc.vector.tensor_sub(low, o_full[DC:P, t % 2, :], low.bitcast(F32)
                                             ).then_inc(S("oT_done"), 1)
                    q, t = tile_at(p, m, LAG_RES)
                    if live(q):
                        wait(dve, "out_ps", TILES, q, t + 1)
                        wait(dve, "xb_done", TILES, q, t + 1)
                        wait(dve, "x1_done", TILES, q, t - 3)
                        wait(dve, "inv_done", TILES, q, t + 1)
                        wait(dve, "mean_done", TILES, q, t - 7)
                        nc.vector.scalar_tensor_tensor(y_sb[:, t % 4, :], bank[6][:, :], exp_inv[:, t:t + 1],
                                                       x_sb[:, t, :], ALU.mult, ALU.add,
                                                       accum_out=y_sum[:, t:t + 1]).then_inc(S("res_done"), 1)
                    q1 = p + 1
                    if live(q1):
                        if m == 3:
                            wait(dve, "c_sq_done", 2, q1, 2)
                            nc.vector.reduce_sum(c_ssq[:, :], c_sq[:, :, :], AX.X).then_inc(S("c_ssq_done"), 1)
                            wait(dve, "c_ssq_done", 1, q1, 1)
                            wait(dve, "c_rstd_done", 1, q1, 0)
                            nc.vector.tensor_scalar(c_var[:, :], c_ssq[:, :], 1.0 / DC, EPS, ALU.mult, ALU.add
                                                    ).then_inc(S("c_var_done"), 1)
                        if m in (5, 6):
                            for i in (2 * (m - 5), 2 * (m - 5) + 1):
                                wait(dve, "proj_ps", 4, q1, i + 1)
                                wait(dve, "qk_ready", 2, q1, 0)
                                nc.vector.tensor_mul(turned[:, i, :], bank[1 - i % 2][:, :], rope_sb[:, i, :]
                                                     ).then_inc(S("turned_done"), 1)
                    q3 = p - 2
                    if live(q3):
                        if m == 0:
                            wait(dve, "pos_ps", 1, q3, 1)
                            wait(dve, "slot_done", 1, q3, 0)
                            pos = bank[7][:, :].rearrange("p (t e) -> p t e", e=E)
                            flat = "p t e -> p (t e)"
                            nc.vector.scalar_tensor_tensor(fits[:, :, :].rearrange(flat), bank[7][:, :], float(CAP),
                                                           chosen[:, :, :].rearrange(flat), ALU.is_lt, ALU.mult)
                            nc.vector.tensor_add(slot_at[:, :, :], pos, slot_base[:, :, :]).then_inc(S("slot_sum"), 1)
                            nc.vector.reduce_sum(c_choice[:, :], chosen[:, :, :].rearrange("p t e -> p e t"), AX.X
                                                 ).then_inc(S("choice_sum"), 1)
                            wait(dve, "choice_sum", 1, q3, 1)
                            nc.vector.tensor_add(earlier[:, :], earlier[:, :], c_choice[:, :]
                                                    ).then_inc(S("earlier_done"), 1)
                        if m == 1:
                            wait_apart(dve, ("slot_done", 1, q3, 1))
                            for s in range(TILES):
                                last = nc.vector.max(slot8[:, s, :], slot[:, s, :])
                            last.then_inc(S("slot8_done"), 1)
                            wait(dve, "slot8_done", 1, q3, 1)
                            nc.vector.tensor_scalar(slot_i[:, :, :], slot8[:, :, :], -1.0, None, ALU.add
                                                    ).then_inc(S("slot_i_done"), 1)
                            wait(dve, "slot_i_done", 1, q3, 1)
                            nc.vector.tensor_scalar(block_i[:, :, :], slot_i[:, :, :], 7, None, ALU.arith_shift_right)
                            nc.vector.tensor_scalar(place_i[:, :, :], slot_i[:, :, :], P - 1, None, ALU.bitwise_and
                                                    ).then_inc(S("split_done"), 1)
                            wait(dve, "split_done", 1, q3, 1)
                            nc.vector.tensor_copy(block_h[:, :, :], block_i[:, :, :])
                            nc.vector.tensor_copy(place_h[:, :, :], place_i[:, :, :]).then_inc(S("split_f_done"), 1)
                        ramp = ramp_h[:, None, :, :].to_broadcast([P, TOPK, P, 2])
                        for hot, number, c, made in ((hot_place, place_h, m - 2, "hot_places"),
                                                     (hot_block, block_h, m - 1, "hot_blocks")):
                            if 0 <= c <= 3:
                                if c == 3:
                                    wait(dve, "hot_used", 4, q3, 1)
                                by_two = number[:, 2 * c:2 * c + 2, :].rearrange("p s (h w) -> p (s h) w", w=2)
                                wait(dve, "split_f_done", 1, q3, 1)
                                nc.vector.tensor_tensor(hot[:, c % 3, :, :, :], ramp,
                                                        by_two[:, :, None, :].to_broadcast([P, TOPK, P, 2]),
                                                        ALU.is_equal).then_inc(S(made), 1)
                    if m == 3 and live(q1):
                        wait(dve, "c_rstd_done", 1, q1, 1)
                        wait(dve, "x_gate_read", 2, q1, 2)
                        wait(dve, "chT_ps", 1, q1, 0)
                        for b in range(2):
                            last = nc.vector.tensor_mul(of_seq(c_norm, b), wide(b)[:, :, 0:DC],
                                                        of_seq(c_rstd, b)[:, :, None].to_broadcast([P, JT, DC]))
                        last.then_inc(S("c_norm_done"), 1)
                    q3 = p - 1
                    if live(q3):
                        if m == 4:
                            wait(dve, "logits_scaled", 1, q3, 1)
                            wait(dve, "l_cen_done", 1, q3, 0)
                            nc.vector.reduce_max(l_max[:, :], logits[:, :, :], AX.X).then_inc(S("l_max_done"), 1)
                        if m == 5:
                            wait(dve, "l_cen_done", 1, q3, 1)
                            nc.vector.tensor_scalar_max(l_cen[:, :, :], l_cen[:, :, :], LOG_TINY
                                                    ).then_inc(S("l_ready"), 1)
                        if m == 6:
                            wait(dve, "l_exp_done", 1, q3, 1)
                            nc.vector.reduce_sum(l_sum[:, :], l_exp[:, :, :], AX.X).then_inc(S("l_sum_done"), 1)
                            wait(dve, "l_sum_done", 1, q3, 1)
                            wait(dve, "probs_done", 1, q3, 0)
                            nc.vector.reciprocal(l_inv[:, :], l_sum[:, :]).then_inc(S("l_inv_done"), 1)
                            for s in range(TILES):
                                last = nc.vector.max(top8[:, s, :], l_cen[:, s, :])
                            last.then_inc(S("top8_done"), 1)
                        if m == 7:
                            if isinstance(q3, int) and q3 == 0:
                                dve.wait_ge(S("dummy_stored"), 16 * 3 * (DUMMY // P))
                            wait_apart(dve, ("top8_done", 1, q3, 1))
                            for s in range(TILES):
                                last = nc.vector.match_replace(l_left[:, s, :], top8[:, s, :], l_cen[:, s, :], TAKEN)
                            last.then_inc(S("l_left_done"), 1)
                            wait(dve, "l_left_done", 1, q3, 1)
                            wait(dve, "pos_ps", 1, q3, 0)
                            nc.vector.tensor_scalar(chosen[:, :, :], l_left[:, :, :], 0.5 * TAKEN, None, ALU.is_lt
                                                    ).then_inc(S("chosen_done"), 1)
                            wait(dve, "chosen_done", 1, q3, 1)
                    if m == 7 and live(p - 2):
                        wait(dve, "hot_used", 4, p - 2, 4)
                        nc.vector.scalar_tensor_tensor(id_part[:, :], bank[7][:, 0:BLOCKS], 0.0,
                                                       pair_base[:, 0:1].to_broadcast([P, BLOCKS]),
                                                       ALU.is_gt, ALU.mult)
                        nc.vector.tensor_add(ids_t[:, :], ids[:, :], bank[7][:, 0:BLOCKS]
                                                ).then_inc(S("id_part_done"), 1)
                        wait(dve, "id_part_done", 1, p - 2, 1)
                        nc.vector.tensor_scalar_add(pair_base[:, :], pair_base[:, :], float(TILES * P))
                        nc.vector.tensor_add(ids[:, :], ids_t[:, :], id_part[:, :]).then_inc(S("ids_done"), 1)

            dve.wait_ge(S("const_loaded"), 16 * CONST_LOADS)
            dve.wait_ge(S("route_loaded"), 48)
            rounds(dve, body)

            dve.wait_ge(S("ids_done"), PAIRS)
            nc.vector.tensor_scalar(id_part[:, :], ids[:, :], 0.0, None, ALU.is_equal).then_inc(S("rows_step"), 1)
            dve.wait_ge(S("rows_step"), 1)
            nc.vector.tensor_mul(id_part[:, :], id_part[:, :], empty_row[:, :]).then_inc(S("rows_step"), 1)
            dve.wait_ge(S("rows_step"), 2)
            nc.vector.tensor_add(ids_t[:, :], ids[:, :], id_part[:, :]).then_inc(S("rows_step"), 1)
            dve.wait_ge(S("rows_step"), 3)
            nc.vector.tensor_scalar(rows_u[:, :], ids_t[:, :], -1.0, None, ALU.add).then_inc(S("rows_step"), 1)
            dve.wait_ge(S("rows_step"), 4)

            def list_of(g, r):
                return rows_u[:, bass.ds(g * (2 * HALVES) + HALVES * r, HALVES)]

            def list_get(g, r):
                wait(dve, "gathered%d" % r, 32, g, 0)
                nc.vector.tensor_copy(rows_get[:, HALVES * r:HALVES * (r + 1)], list_of(g, r)
                                      ).then_inc(S("rows_ready"), 1)

            def tokens_lo(g, r):
                for i in range(2):
                    wait(dve, "xgT_ps", 4, g, 2 * r + i + 1)
                    wait(dve, "xg_hi_done", 4, g, 2 * r + i + 1)
                    wait(dve, "up_ps", 4, g, 2 * r - 2)
                    nc.vector.tensor_sub(xgT_lo[:, r, 2 * i:2 * i + 2, :].rearrange("p k c -> p (k c)"),
                                         bank[i][:, :],
                                         xgT_hi[:, r, 2 * i:2 * i + 2, :].rearrange("p k c -> p (k c)").bitcast(F32)
                                         ).then_inc(S("xg_lo_done"), 1)

            def gu_split(g, r):
                wait(dve, "gu_loaded%d" % r, 16, g, 16)
                wait(dve, "gu_hi_done", 2, g, r + 1)
                wait(dve, "up_ps", 4, g, 2 * r - 2)
                nc.vector.tensor_sub(gu_lo[:, r, :], w_gu[:, r, :], gu_hi[:, r, :].bitcast(F32)
                                     ).then_inc(S("gu_lo_done"), 1)

            def dn_split(g, r):
                wait(dve, "dn_loaded%d" % r, 16, g, 16)
                wait(dve, "dn_hi_done", 2, g, r + 1)
                wait(dve, "y_done", 4, g, 2 * r - 2)
                nc.vector.tensor_sub(dn_lo[:, r, :], w_dn[:, r, :], dn_hi[:, r, :].bitcast(F32)
                                     ).then_inc(S("dn_lo_done"), 1)

            def h_split(g, r):
                wait(dve, "h_hi_done", 2, g, r + 1)
                wait(dve, "y_done", 4, g, 2 * r - 2)
                nc.vector.tensor_sub(h_lo[:, r, :], h_sb, h_hi[:, r, :].bitcast(F32)).then_inc(S("h_lo_done"), 1)

            def weights_in(g, r):
                wait(dve, "gathered%d" % r, 32, g, 32)
                wait(dve, "w_slot_done", 2, g, r - 1)
                nc.vector.tensor_copy(w_new[:, HALVES * r:HALVES * (r + 1)],
                                      xg[:, HALVES * r:HALVES * (r + 1), bass.ds(g * 2 + (D + r), 1)
                                         ].rearrange("p h a -> p (h a)")).then_inc(S("w_new_done"), 1)

            def weigh(g, r):
                wait(dve, "y_read0", 2, g, r - 1)
                wait(dve, "y_read1", 2, g, r - 1)
                wait(dve, "w_new_done", 2, g, r + 1)
                nc.vector.tensor_copy(w_slot[:, HALVES * r:HALVES * (r + 1)], w_new[:, HALVES * r:HALVES * (r + 1)]
                                      ).then_inc(S("w_slot_done"), 1)

            def product(g, r):
                wait(dve, "gate_done", 2, g, r + 1)
                wait(dve, "up_ps", 4, g, 2 * r + 2)
                wait(dve, "h_lo_done", 2, g, r)
                nc.vector.tensor_mul(h_sb, gate_act, bank[3 + 4 * r][:, :]).then_inc(S("h_done"), 1)

            def scale(g, r):
                wait(dve, "added%d" % r, 32, g, 0)
                nc.vector.tensor_copy(rows_put[:, HALVES * r:HALVES * (r + 1)], list_of(g, r))
                wait(dve, "y_done", 4, g, 2 * r + 2)
                wait(dve, "w_slot_done", 2, g, r + 1)
                nc.vector.tensor_scalar(ye[:, HALVES * r + 1, :], bank[5][:, :],
                                        w_slot[:, HALVES * r + 1:HALVES * r + 2], None, ALU.mult
                                        ).then_inc(S("y_read1"), 1)

            for r in range(2):
                list_get(0, r)
            dve.wait_ge(S("probs_stored"), 16 * PAIRS)
            gu_split(0, 0)
            weights_in(0, 0)
            list_get(1, 0)
            tokens_lo(0, 0)

            def pair(g):
                for r in range(2):
                    if exists(after(g, r)[0]):
                        weights_in(*after(g, r))
                    if exists(after(g, r, 3)[0]):
                        list_get(*after(g, r, 3))
                    if exists(after(g, r)[0]):
                        tokens_lo(*after(g, r))
                    if exists(after(g, r, -1)[0]):
                        h_split(*after(g, r, -1))
                    if exists(g - 1):
                        scale(g - 1, r)
                    weigh(g, r)
                    if exists(after(g, r)[0]):
                        gu_split(*after(g, r))
                    dn_split(g, r)
                    product(g, r)

            experts(dve, pair)
            h_split(LAST, 1)
            for r in range(2):
                scale(LAST, r)

            def final(g):
                for i in range(RING):
                    wait(dve, "sum_loaded%d" % i, 16, g, 16)
                    wait(dve, "f_mv_done", RING, g, i)
                    for s in range(FINAL):
                        last = nc.vector.bn_stats(f_stats[:, s, :], final_buf(i)[:, s, :])
                    last.then_inc(S("f_stats_done"), 1)
                    wait_apart(dve, ("f_stats_done", RING, g, i + 1), ("f_shift_done", RING, g, i - 1))
                    for s in range(FINAL):
                        last = nc.vector.bn_aggr(f_mv[:, i % 2, s, :], f_stats[:, s, :])
                    last.then_inc(S("f_mv_done"), 1)

            final_rounds(dve, final)

        @block.scalar
        def _(act):
            def body(p):
                for m in range(TILES):
                    q, t = tile_at(p, m, LAG_OUT)
                    if live(q):
                        wait(act, "o_ps", TILES, q, t + 1)
                        wait(act, "logits_ps", TILES, q, t - 1)
                        wait(act, "oT_done", TILES, q, t - 1)
                        o_in = bank[5][:, P * (t % 2):P * (t % 2 + 1)]
                        nc.scalar.copy(oT[:, t % 2, :], o_in)
                        nc.scalar.copy(o_full[DC:P, t % 2, :], o_in[DC:P, :]).then_inc(S("o_read"), 1)
                    q, t = tile_at(p, m, LAG_RES)
                    if live(q):
                        wait(act, "logits_ps", TILES, q, t + 1)
                        wait(act, "inv_done", TILES, q, t + 1)
                        wait(act, "l_raw_done", 1, q, 0)
                        nc.scalar.activation(o_gate[:, slot_of(t), :], bank[5][:, 2 * P:2 * P + E], ACT.Copy,
                                             scale=exp_inv[:, t:t + 1]).then_inc(S("logits_done"), 1)
                    if m == 1 and live(p):
                        wait(act, "v_ps", 1, p, 1)
                        wait(act, "o_ps", TILES, p, 0)
                        v_in = bank[1][:, :].rearrange("p (j b c) -> p j b c", b=2, c=DC)
                        for b in range(2):
                            last = nc.scalar.copy(v_sb[:, b, :, :, :],
                                                  v_in[:, :, b, None, :].to_broadcast([P, JT, 2, DC]))
                        last.then_inc(S("v_done"), 1)
                    q, t = tile_at(p, m, LAG_PROBS)
                    if live(q):
                        wait(act, "probsT_ps", TILES, q, t + 1)
                        wait(act, "o_ps", TILES, q, t - 1)
                        n = P * (t // 2 + 1)
                        nc.scalar.copy(probsT[:, t % 2, 0:n], bank[4][:, 0:n]).then_inc(S("probsT_done"), 1)
                    if live(p):
                        wait(act, "max_done", TILES, p, m + 1)
                        wait(act, "probsT_ps", TILES, p, m - 1)
                        wait(act, "inv_done", TILES, p, m - 7)
                        n = P * (m // 2 + 1)
                        nc.scalar.activation(probs[:, m % 2, 0:n], bank[2 + m % 2][:, 0:n], ACT.Exp,
                                             bias=neg_max[:, m:m + 1], accum_out=exp_sum[:, m:m + 1]
                                             ).then_inc(S("exp_done"), 1)
                    if 3 <= m <= 6 and live(p - 2):
                        c = m - 3
                        wait(act, "hot_blocks", 4, p - 2, c + 1)
                        for s in (2 * c, 2 * c + 1):
                            at = (s % 2) * (TOPK // 2)
                            part = hot_block[:, c % 3, at:at + TOPK // 2, :, :].rearrange("p h n w -> p (h n w)")
                            last = nc.scalar.activation(part, part, ACT.Copy, scale=local_id[:, s:s + 1])
                        last.then_inc(S("hot_done"), 1)
                    q, t = tile_at(p, m, LAG_VAR)
                    if live(q):
                        wait(act, "mean_done", TILES, q, t + 1)
                        wait(act, "meansq_done", TILES, q, t - 7)
                        wait(act, "x1_stored%d" % t, 32, q, 0)
                        nc.scalar.activation(x1_sb[:, t, :], y_sb[:, t % 4, :], ACT.Square,
                                             bias=y_negmean[:, t % 2:t % 2 + 1],
                                             accum_out=y_ssq[:, t:t + 1]).then_inc(S("ssq_done"), 1)
                    q, t = tile_at(p, m, LAG_X1)
                    if live(q):
                        wait(act, "shift_done", TILES, q, t + 1)
                        nc.scalar.activation(x1_sb[:, t, :], y_sb[:, t % 4, :], ACT.Identity,
                                             bias=y_shift[:, slot_of(t):slot_of(t) + 1],
                                             scale=y_rstd[:, slot_of(t):slot_of(t) + 1]).then_inc(S("x1_done"), 1)
                    if m in (1, 2) and live(p + 1):
                        wait(act, "compressed", 2, p + 1, m)
                        wait(act, "c_ssq_done", 1, p + 1, 0)
                        nc.scalar.activation(of_seq(c_sq, m - 1), wide(m - 1)[:, :, 0:DC], ACT.Square
                                             ).then_inc(S("c_sq_done"), 1)
                    if m == 2 and live(p + 1):
                        wait(act, "compressed", 2, p + 1, 2)
                        wait(act, "x_gate_done", 1, p + 1, 0)
                        for b in range(2):
                            nc.scalar.copy(x_gate_in[:, JT * b:JT * (b + 1), :], wide(b)[:, :, DC:DC + E]
                                           ).then_inc(S("x_gate_read"), 1)
                    if m == 4 and live(p + 1):
                        wait(act, "chT_ps", 1, p + 1, 1)
                        wait(act, "v_ps", 1, p + 1, 0)
                        nc.scalar.activation(chT[:, :], bank[0][:, :], ACT.Identity, bias=beta_sb[:, :],
                                             scale=gamma_sb[:, :]).then_inc(S("chT_done"), 1)
                    if m == 5 and live(p - 1):
                        wait(act, "l_ready", 1, p - 1, 1)
                        wait(act, "probs_done", 1, p - 1, 0)
                        nc.scalar.activation(l_exp[:, :, :], l_cen[:, :, :], ACT.Exp).then_inc(S("l_exp_done"), 1)

            act.wait_ge(S("const_loaded"), 16 * CONST_LOADS)
            rounds(act, body)

            def tokens_hi(g, r):
                for i in range(2):
                    wait(act, "xgT_ps", 4, g, 2 * r + i + 1)
                    wait(act, "up_ps", 4, g, 2 * r - 2)
                    nc.scalar.copy(xgT_hi[:, r, 2 * i:2 * i + 2, :].rearrange("p k c -> p (k c)"), bank[i][:, :]
                                   ).then_inc(S("xg_hi_done"), 1)

            def gu_split(g, r):
                wait(act, "gu_loaded%d" % r, 16, g, 16)
                wait(act, "up_ps", 4, g, 2 * r - 2)
                nc.scalar.copy(gu_hi[:, r, :], w_gu[:, r, :]).then_inc(S("gu_hi_done"), 1)

            def dn_split(g, r):
                wait(act, "dn_loaded%d" % r, 16, g, 16)
                wait(act, "y_done", 4, g, 2 * r - 2)
                nc.scalar.copy(dn_hi[:, r, :], w_dn[:, r, :]).then_inc(S("dn_hi_done"), 1)

            def h_split(g, r):
                wait(act, "h_done", 2, g, r + 1)
                wait(act, "y_done", 4, g, 2 * r - 2)
                nc.scalar.copy(h_hi[:, r, :], h_sb).then_inc(S("h_hi_done"), 1)

            def gate(g, r):
                wait(act, "up_ps", 4, g, 2 * r + 1)
                wait(act, "h_done", 2, g, r)
                nc.scalar.activation(gate_act, bank[2 + 4 * r][:, :], ACT.Silu).then_inc(S("gate_done"), 1)

            def scale(g, r):
                wait(act, "y_done", 4, g, 2 * r + 1)
                wait(act, "w_slot_done", 2, g, r + 1)
                wait(act, "added%d" % r, 32, g, 0)
                nc.scalar.activation(ye[:, HALVES * r, :], bank[4][:, :], ACT.Copy,
                                     scale=w_slot[:, HALVES * r:HALVES * r + 1]).then_inc(S("y_read0"), 1)

            act.wait_ge(S("ids_done"), PAIRS)
            act.wait_ge(S("probs_stored"), 16 * PAIRS)
            gu_split(0, 0)
            tokens_hi(0, 0)

            def pair(g):
                for r in range(2):
                    if exists(after(g, r)[0]):
                        tokens_hi(*after(g, r))
                    if exists(after(g, r, -1)[0]):
                        h_split(*after(g, r, -1))
                    if exists(g - 1):
                        scale(g - 1, r)
                    if exists(after(g, r)[0]):
                        gu_split(*after(g, r))
                    dn_split(g, r)
                    gate(g, r)

            experts(act, pair)
            h_split(LAST, 1)
            for r in range(2):
                scale(LAST, r)

            def final(g):
                for i in range(RING):
                    wait(act, "f_shift_done", RING, g, i + 1)
                    for s in range(FINAL):
                        last = nc.scalar.activation(final_buf(i)[:, s, :], final_buf(i)[:, s, :], ACT.Identity,
                                                    bias=f_shift[:, i % 2, s:s + 1], scale=f_rstd[:, i % 2, s:s + 1])
                    last.then_inc(S("final_done"), 1)

            final_rounds(act, final)

        @block.gpsimd
        def _(pool):
            pool.wait_ge(S("bias_loaded"), 16)
            pool.wait_ge(S("started"), 1)
            pool.wait_ge(S("folded"), 1)
            nc.gpsimd.memset(scrap_p[:, :], 0.0).then_inc(S("scrap_written"), 1)

            def body(p):
                for m in range(TILES):
                    if m == 0 and live(p - 2):
                        wait(pool, "slot_sum", 1, p - 2, 1)
                        wait(pool, "slot8_done", 1, p - 2, 0)
                        nc.gpsimd.tensor_tensor(slot[:, :, :], slot_at[:, :, :], fits[:, :, :], ALU.mult
                                                ).then_inc(S("slot_done"), 1)
                    if m == 7 and live(p + 1):
                        wait(pool, "scores_done", TILES, p, TILES)
                        wait(pool, "turned_done", 4, p + 1, 4)
                        nc.gpsimd.tensor_tensor(qT[:, :], turned[:, 0, :], turned[:, 1, :], ALU.add
                                                ).then_inc(S("qk_ready"), 1)
                        nc.gpsimd.tensor_tensor(kT[:, :], turned[:, 2, :], turned[:, 3, :], ALU.add
                                                ).then_inc(S("qk_ready"), 1)
                    if m == 2:
                        if live(p - 1):
                            wait(pool, "logits_done", TILES, p - 1, TILES)
                            wait(pool, "logits_scaled", 1, p - 1, 0)
                            nc.gpsimd.tensor_tensor(l_raw[:, :, :], o_gate[:, :, :], x_gate[:, :, :], ALU.add
                                                    ).then_inc(S("l_raw_done"), 1)
                        if live(p):
                            wait(pool, "x_gate_read", 2, p, 2)
                            wait(pool, "l_raw_done", 1, p, 0)
                            nc.gpsimd.tensor_tensor(x_gate[:, :, :], x_gate_in[:, :, :],
                                                    bias_gate[:, None, :].to_broadcast([P, TILES, E]), ALU.add
                                                    ).then_inc(S("x_gate_done"), 1)
                    q, t = tile_at(p, m, LAG_RES)
                    if live(q):
                        wait(pool, "res_done", TILES, q, t + 1)
                        wait(pool, "ssq_done", TILES, q, t - 1)
                        wait(pool, "shift_done", TILES, q, t - 1)
                        nc.gpsimd.tensor_tensor(y_negmean[:, t % 2:t % 2 + 1], y_sum[:, t:t + 1], neg_inv_d[:, :],
                                                ALU.mult).then_inc(S("mean_done"), 1)
                    if m == 3 and live(p + 1):
                        wait(pool, "c_var_done", 1, p + 1, 1)
                        wait(pool, "c_norm_done", 1, p + 1, 0)
                        nc.gpsimd.tensor_tensor(c_rstd[:, :], c_var[:, :], eps_pow[:, :], ALU.pow
                                                ).then_inc(S("c_rstd_done"), 1)
                    q, t = tile_at(p, m, LAG_VAR)
                    if live(q):
                        at = slot_of(t)
                        wait(pool, "ssq_done", TILES, q, t + 1)
                        nc.gpsimd.tensor_tensor(y_meansq[:, t % 2:t % 2 + 1], y_ssq[:, t:t + 1], inv_d[:, :], ALU.mult
                                                ).then_inc(S("meansq_done"), 1)
                        wait(pool, "meansq_done", TILES, q, t + 1)
                        nc.gpsimd.tensor_tensor(y_var[:, t % 2:t % 2 + 1], y_meansq[:, t % 2:t % 2 + 1],
                                                eps_add[:, 0:1], ALU.add).then_inc(S("y_var_done"), 1)
                        wait(pool, "y_var_done", TILES, q, t + 1)
                        wait(pool, "x1_done", TILES, q, t - 7)
                        wait(pool, "logits_scaled", 1, q, 0)
                        nc.gpsimd.tensor_tensor(y_rstd[:, at:at + 1], y_var[:, t % 2:t % 2 + 1], eps_pow[:, 0:1], ALU.pow
                                                ).then_inc(S("rstd_done"), 1)
                        wait(pool, "rstd_done", TILES, q, t + 1)
                        wait(pool, "mean_done", TILES, q, t + 1)
                        nc.gpsimd.tensor_tensor(y_shift[:, at:at + 1], y_negmean[:, t % 2:t % 2 + 1],
                                                y_rstd[:, at:at + 1], ALU.mult).then_inc(S("shift_done"), 1)
                    if m == 3:
                        if live(p - 1):
                            wait(pool, "l_raw_done", 1, p - 1, 1)
                            wait(pool, "l_cen_done", 1, p - 1, 0)
                            nc.gpsimd.tensor_tensor(logits[:, :, :], l_raw[:, :, :],
                                                    y_rstd[:, :, None].to_broadcast([P, TILES, E]), ALU.mult
                                                    ).then_inc(S("logits_scaled"), 1)
                    if m == 4 and live(p - 1):
                        wait(pool, "l_max_done", 1, p - 1, 1)
                        wait(pool, "l_exp_done", 1, p - 1, 0)
                        nc.gpsimd.tensor_tensor(l_cen[:, :, :], logits[:, :, :],
                                                l_max[:, :, None].to_broadcast([P, TILES, E]), ALU.subtract
                                                ).then_inc(S("l_cen_done"), 1)
                    if m == 6 and live(p - 1):
                        wait(pool, "l_inv_done", 1, p - 1, 1)
                        wait(pool, "probs_stored", 16, p - 1, 0)
                        nc.gpsimd.tensor_tensor(r_probs[:, :, :], l_exp[:, :, :],
                                                l_inv[:, :, None].to_broadcast([P, TILES, E]), ALU.mult
                                                ).then_inc(S("probs_done"), 1)
                    if live(p):
                        wait(pool, "x_loaded%d" % m, 16, p, 16)
                        nc.gpsimd.tensor_tensor(x_sb[:, m, :], x_sb[:, m, :], bias_sb[:, :], ALU.add
                                                ).then_inc(S("xb_done"), 1)

            rounds(pool, body)

            def gather(g, r):
                wait_apart(pool, ("rows_ready", 2, g, r + 1), ("xgT_ps", 4, g, 2 * r - 2),
                           ("w_new_done", 2, g, r - 1))
                for h in range(HALVES):
                    nc.gpsimd.indirect_dma_start(
                        xg[:, HALVES * r + h, :], None, table[:, :],
                        bass.IndirectOffsetOnAxis(rows_get[:, HALVES * r + h:HALVES * r + h + 1], 0),
                        bounds_check=TOKENS + DUMMY - 1).then_inc(S("gathered%d" % r), 16)

            def scatter(g, r):
                wait_apart(pool, ("added%d" % (1 - r), 32, g, 32 * r), ("y_read0", 2, g, r + 1),
                           ("y_read1", 2, g, r + 1))
                for h in range(HALVES):
                    nc.gpsimd.indirect_dma_start(
                        total[:, :],
                        bass.IndirectOffsetOnAxis(rows_put[:, HALVES * r + h:HALVES * r + h + 1], 0),
                        ye[:, HALVES * r + h, :], None,
                        bounds_check=TOKENS + DUMMY - 1, compute_op=ALU.add).then_inc(S("added%d" % r), 16)

            pool.wait_ge(S("dummy_stored"), 16 * 3 * (DUMMY // P))
            pool.wait_ge(S("probs_stored"), 16 * PAIRS)
            for m in range(TILES):
                pool.wait_ge(S("x1_stored%d" % m), 32 * PAIRS)
            for n in range(3):
                gather(*after(0, 0, n))

            def pair(g):
                if not isinstance(g, int):
                    wait(pool, "scrap_written", 4, g - 2, 1)
                for r in range(2):
                    if exists(after(g, r, 3)[0]):
                        gather(*after(g, r, 3))
                    if exists(g - 1):
                        scatter(g - 1, r)

            experts(pool, pair)
            for r in range(2):
                scatter(LAST, r)

            def final(g):
                for i in range(RING):
                    b = i % 2
                    wait(pool, "f_mv_done", RING, g, i + 1)
                    wait(pool, "f_shift_done", RING, g, i)
                    nc.gpsimd.tensor_tensor(f_negmean[:, :], f_mv[:, b, :, 0], minus_one[:, :], ALU.mult)
                    nc.gpsimd.tensor_tensor(f_var[:, :], f_mv[:, b, :, 1], eps_add[:, 0:FINAL], ALU.add
                                            ).then_inc(S("f_var_done"), 1)
                    wait(pool, "f_var_done", RING, g, i + 1)
                    wait(pool, "final_done", RING, g, i - 1)
                    nc.gpsimd.tensor_tensor(f_rstd[:, b, :], f_var[:, :], eps_pow[:, 0:FINAL], ALU.pow
                                            ).then_inc(S("f_rstd_done"), 1)
                    wait(pool, "f_rstd_done", RING, g, i + 1)
                    nc.gpsimd.tensor_tensor(f_shift[:, b, :], f_negmean[:, :], f_rstd[:, b, :], ALU.mult
                                            ).then_inc(S("f_shift_done"), 1)

            final_rounds(pool, final)


def constants():
    import numpy as np
    f = np.float32
    inv = (f(1.0) / f(10000.0) ** (np.arange(0, DC, 2, dtype=f) / f(DC))).astype(f)
    angle = np.arange(SEQ, dtype=f)[:, None] * inv[None, :]
    cos, sin = np.cos(angle).astype(f).T, np.sin(angle).astype(f).T
    cos, sin = np.concatenate([cos, cos]), np.concatenate([-sin, sin])
    scale = f(DC ** -0.5)
    rope = np.stack([np.concatenate([a, a]) for a in (cos * scale, sin * scale, cos, sin)]).astype(f)
    i = np.arange(P)
    const = np.zeros((11, P, P), f)
    const[0] = np.eye(P)
    const[1] = np.where(i[None, :] <= i[:, None], 0.0, TAKEN)
    const[2] = i[:, None] < i[None, :]
    const[3] = 1.0
    const[4] = i[None, :]
    const[5] = TOKENS + 1 + P * (i[None, :] % HALVES) + i[:, None]
    const[6:10] = np.tile(np.arange(E) * CAP + 1, TILES).reshape(4, 1, P)
    const[10, :, 0:TILES] = P * np.arange(TILES)[None, :] + i[:, None] + 1
    return rope, const


def kernel(**inputs):
    import numpy as np
    import concourse.bacc as bacc
    from concourse.bass_utils import run_bass_kernel_spmd

    a = {k.replace("L0_attn_", "").replace("L0_ffn_", ""): np.asarray(v) for k, v in inputs.items()}
    rope, const = constants()
    x = a["x"].reshape(TOKENS, D)
    half = np.r_[DC // 2:DC, 0:DC // 2]
    q, k, v = a["W_q_comp"], a["W_kv_comp"][:DC], a["W_kv_comp"][DC:]
    gu = np.concatenate([a["w_gate"].reshape(E, KD, P, FF), a["w_up"].reshape(E, KD, P, FF)], axis=3)
    gu = gu.transpose(0, 2, 1, 3).reshape(E, P, KD * 2 * FF)
    dn = a["w_down"].reshape(E, KF, P, D).transpose(0, 2, 1, 3).reshape(E, P, KF * D)
    arrays = {
        "xT": x.reshape(PAIRS, TILES * P, KD, P).transpose(0, 3, 2, 1).reshape(PAIRS, P, KD * TILES * P),
        "x": x,
        "w_kv": a["W_to_kv"],
        "w_compT": a["W_compress"].T,
        "gamma": a["ln_gamma"][:, None],
        "beta": a["ln_beta"][:, None],
        "w_proj": np.stack([q.T, q[half].T, k.T, k[half].T, v.T]),
        "w_c2l": np.concatenate([a["W_comp2lat"]] * 2, axis=1),
        "w_resT": a["W_out_res"].T,
        "bias": a["b_out_res"][None, :],
        "bias_col": a["b_out_res"].reshape(KD, P).T,
        "gateT": a["gate_w"].T,
        "w_experts": np.concatenate([gu, dn], axis=2),
        "rope": rope,
        "const": const,
    }
    arrays = {n: np.ascontiguousarray(v) for n, v in arrays.items()}
    nc = bacc.Bacc("TRN2", target_bir_lowering=False, num_devices=1)
    args = [nc.dram_tensor(n, v.shape, mybir.dt.from_np(v.dtype), kind="ExternalInput").ap() for n, v in arrays.items()]
    args.append(nc.dram_tensor("out", (TOKENS, D), F32, kind="ExternalOutput").ap())
    attention_router_moe(nc, *args)
    r = run_bass_kernel_spmd(nc, [arrays], core_ids=[0])
    return r.results[0]["out"].reshape(SEQS, SEQ, D)
```
